# Optimizing a Trainium2 kernel written in Bass

```python
import numpy as np
import jax
import jax.numpy as jnp

def _softmax(x, axis=-1):
    return jax.nn.softmax(x, axis=axis)

def _gelu(x):
    return jax.nn.gelu(x, approximate=True)

def _silu(x):
    return jax.nn.silu(x)

def _sigmoid(x):
    return jax.nn.sigmoid(x)

def _layernorm(x, axis=-1, eps=1e-05):
    m = jnp.mean(x, axis=axis, keepdims=True)
    v = jnp.var(x, axis=axis, keepdims=True)
    return (x - m) / jnp.sqrt(v + eps)

def _scatter_add(tgt, idx, src, axis=0):
    return tgt.at[idx].add(src)

def _segment_sum(src, seg, n):
    return jax.ops.segment_sum(src, seg, n)
kernel_name = 'mk_xattn_ffn_d4_seqx_r4_903281'

def setup_inputs(seed: int=0):
    np.random.seed(seed)
    _w = jnp.asarray

    def _rec_inputs():
        import jax
        import jax.numpy as jnp
        _rk = jax.random.key(seed)
        x = -0.0002928 + 1 * jax.random.normal(jax.random.fold_in(_rk, 1), (4, 512, 256), jnp.float32)
        _lenS = 512 - jax.random.randint(jax.random.fold_in(_rk, 7), (4,), 0, max(1, 512 // 4) + 1, jnp.int32)
        _lenS2 = 512 - jax.random.randint(jax.random.fold_in(_rk, 8), (4,), 0, max(1, 512 // 4) + 1, jnp.int32)
        _ctx_1024P = jax.random.normal(jax.random.fold_in(_rk, 11), (4, 16, 256), jnp.float32)
        _ctx_1024c = jax.random.dirichlet(jax.random.fold_in(_rk, 511), 0.3 * jnp.ones((16,), jnp.float32), (4, 512))
        _ctx_1024t = jnp.einsum('bsk,bkd->bsd', _ctx_1024c, _ctx_1024P)
        _ctx_1024t = _ctx_1024t * jax.lax.rsqrt(jnp.mean(jnp.square(_ctx_1024t)) + 1e-12) * 0.953939
        ctx_1024 = -1.39393e-06 + 0.999914 * (_ctx_1024t + 0.3 * jax.random.normal(jax.random.fold_in(_rk, 611), (4, 512, 256), jnp.float32))
        return (x, ctx_1024)
    x, ctx_1024 = _rec_inputs()

    def _L0_xattn_setup():
        import jax, jax.numpy as jnp
        import numpy as np
        D_MODEL = 256
        N_HEADS = 16
        D_K = D_MODEL // N_HEADS
        WINDOW = 128
        GLOBAL = 16
        CAUSAL = True

        def _rope_tables(seq_len, dk, dtype):
            inv_freq = 1.0 / 10000.0 ** (jnp.arange(0, dk, 2, dtype=jnp.float32) / dk)
            t = jnp.arange(seq_len, dtype=jnp.float32)
            freqs = t[:, None] * inv_freq[None, :]
            emb = jnp.concatenate([freqs, freqs], axis=-1)
            return (jnp.cos(emb).astype(dtype), jnp.sin(emb).astype(dtype))

        def _apply_rope(x, cos, sin):
            x_rope = jnp.concatenate([-x[..., 1::2], x[..., ::2]], axis=-1)
            return x * cos + x_rope * sin

        def _local_window_mask(seq_len, window, global_tokens, causal, dtype):
            i = jnp.arange(seq_len)[:, None]
            j = jnp.arange(seq_len)[None, :]
            blocked = jnp.abs(i - j) > window
            if causal:
                blocked = blocked | (j > i)
            is_global = (i < global_tokens) | (j < global_tokens)
            return jnp.where(blocked & ~is_global, jnp.asarray(-jnp.inf, dtype), jnp.asarray(0.0, dtype))
        key = jax.random.key(seed)
        ks = jax.random.split(key, 11)
        B, S = (2, 512)
        s = 1.0 / np.sqrt(D_MODEL)
        return {'q': jax.random.normal(ks[0], (B, S, D_MODEL), jnp.float32), 'k': jax.random.normal(ks[1], (B, S, D_MODEL), jnp.float32), 'v': jax.random.normal(ks[2], (B, S, D_MODEL), jnp.float32), 'wq': jax.random.normal(ks[3], (D_MODEL, D_MODEL), jnp.float32) * s, 'bq': jax.random.normal(ks[4], (D_MODEL,), jnp.float32) * s, 'wk': jax.random.normal(ks[5], (D_MODEL, D_MODEL), jnp.float32) * s, 'bk': jax.random.normal(ks[6], (D_MODEL,), jnp.float32) * s, 'wv': jax.random.normal(ks[7], (D_MODEL, D_MODEL), jnp.float32) * s, 'bv': jax.random.normal(ks[8], (D_MODEL,), jnp.float32) * s, 'wo': jax.random.normal(ks[9], (D_MODEL, D_MODEL), jnp.float32) * s, 'bo': jax.random.normal(ks[10], (D_MODEL,), jnp.float32) * s}
    _L0_xattn_all = _L0_xattn_setup()
    _L0_xattn_in = {k: v for k, v in _L0_xattn_all.items() if k in ('wq', 'bq', 'wk', 'bk', 'wv', 'bv', 'wo', 'bo')}
    del _L0_xattn_all

    def _L0_ffn_setup():
        import jax, jax.numpy as jnp
        import numpy as np
        DIM = 256
        NUM_HEAVY = 256
        N_ITERS = 50
        EPS = 1.0
        FETCH_K_RATIO = 9.0 / 8.0

        def rms_norm(x, gamma):
            norm = jnp.maximum(jnp.linalg.norm(x, axis=-1, keepdims=True), 1e-12)
            return x / norm * x.shape[-1] ** 0.5 * gamma

        def feed_forward(x, gamma, w1, b1, w2, b2):
            h = jax.nn.gelu(rms_norm(x, gamma) @ w1 + b1, approximate=False)
            return h @ w2 + b2

        def coor_descent(s, k, n_iters, eps):
            logk = jnp.log(jnp.asarray(k, dtype=s.dtype))

            def step(ab, _):
                a, b = ab
                sb = (s + b) / eps
                a = eps * (logk - jax.scipy.special.logsumexp(sb, axis=-1, keepdims=True))
                b = -jax.nn.relu(s + a)
                return ((a, b), None)
            a0 = jnp.zeros_like(s[..., :1])
            b0 = -s
            (a, b), _ = jax.lax.scan(step, (a0, b0), None, length=n_iters)
            return jnp.exp((s + a + b) / eps)
        key = jax.random.key(seed)
        ks = jax.random.split(key, 8)
        b, n, d = (4, 2048, DIM)
        dl, dh = (int(d * 0.5), d * 4)
        u = lambda k, shape, fan_in: jax.random.uniform(k, shape, jnp.float32, -1.0, 1.0) / np.sqrt(fan_in)
        return {'x': jax.random.normal(ks[0], (b, n, d), jnp.float32), 'routing_token': jax.random.normal(ks[1], (d,), jnp.float32), 'light_gamma': jnp.ones((d,), jnp.float32), 'light_w1': u(ks[2], (d, dl), d), 'light_b1': jnp.zeros((dl,), jnp.float32), 'light_w2': u(ks[3], (dl, d), dl), 'light_b2': jnp.zeros((d,), jnp.float32), 'heavy_gamma': jnp.ones((d,), jnp.float32), 'heavy_w1': u(ks[4], (d, dh), d), 'heavy_b1': jnp.zeros((dh,), jnp.float32), 'heavy_w2': u(ks[5], (dh, d), dh), 'heavy_b2': jnp.zeros((d,), jnp.float32)}
    _L0_ffn_all = _L0_ffn_setup()
    _L0_ffn_in = {k: v for k, v in _L0_ffn_all.items() if k in ('routing_token', 'light_gamma', 'light_w1', 'light_b1', 'light_w2', 'light_b2', 'heavy_gamma', 'heavy_w1', 'heavy_b1', 'heavy_w2', 'heavy_b2')}
    del _L0_ffn_all

    def _L1_xattn_setup():
        import jax, jax.numpy as jnp
        import numpy as np
        WINDOW_SIZE = 20
        NEG_BIG = -100000000.0

        def band_mask(S):
            idx = jnp.arange(S)
            return jnp.where(jnp.abs(idx[:, None] - idx[None, :]) <= WINDOW_SIZE, 0.0, NEG_BIG).astype(jnp.float32)
        key = jax.random.key(seed)
        k1, k2, k3, k4 = jax.random.split(key, 4)
        B, S, Dq, Dk = (8, 512, 256, 256)
        queries = jax.random.normal(k1, (B, S, Dq), dtype=jnp.float32)
        keys = jax.random.normal(k2, (B, S, Dk), dtype=jnp.float32)
        lim = 1.0 / np.sqrt(Dk)
        W_reduce = jax.random.uniform(k3, (Dq, Dk), jnp.float32, -lim, lim)
        b_reduce = jax.random.uniform(k4, (Dq,), jnp.float32, -lim, lim)
        return {'queries': queries, 'keys': keys, 'W_reduce': W_reduce, 'b_reduce': b_reduce}
    _L1_xattn_all = _L1_xattn_setup()
    _L1_xattn_in = {k: v for k, v in _L1_xattn_all.items() if k in ('W_reduce', 'b_reduce')}
    del _L1_xattn_all

    def _L1_ffn_setup():
        import jax, jax.numpy as jnp
        import numpy as np
        from jax import lax
        H = 256
        E = 8
        E_MLP = E - 4
        TOP_K = 2
        I = 128
        KC = 4
        SHARED_SCALE = 1.0
        key = jax.random.key(seed)
        ks = jax.random.split(key, 8)
        B, S = (4, 1024)
        s_h = 1.0 / np.sqrt(H)
        s_i = 1.0 / np.sqrt(I)
        return {'hidden_states': jax.random.normal(ks[0], (B, S, H), dtype=jnp.float32), 'Wr': jax.random.normal(ks[1], (H, E), dtype=jnp.float32) * s_h, 'router_bias': jnp.zeros((E,), dtype=jnp.float32), 'Wg': jax.random.normal(ks[2], (E_MLP, H, I), dtype=jnp.float32) * s_h, 'Wu': jax.random.normal(ks[3], (E_MLP, H, I), dtype=jnp.float32) * s_h, 'Wd': jax.random.normal(ks[4], (E_MLP, I, H), dtype=jnp.float32) * s_i, 'conv_w': jax.random.normal(ks[5], (KC, 1, H), dtype=jnp.float32) * (1.0 / np.sqrt(KC)), 'conv_b': jnp.zeros((H,), dtype=jnp.float32)}
    _L1_ffn_all = _L1_ffn_setup()
    _L1_ffn_in = {k: v for k, v in _L1_ffn_all.items() if k in ('Wr', 'router_bias', 'Wg', 'Wu', 'Wd', 'conv_w', 'conv_b')}
    del _L1_ffn_all

    def _L2_xattn_setup():
        import jax, jax.numpy as jnp
        import numpy as np
        B, N, D = (4, 1024, 256)
        H = 16
        HD = D // H
        EPS = 1e-06
        BASE_SPARSITY = 0.3
        KEEP = max(int((1.0 - BASE_SPARSITY) * HD), 1)
        LEAKY_SLOPE = 0.01

        def _focus(x, focusing_factor):
            x = jnp.abs(jnp.where(x >= 0, x, LEAKY_SLOPE * x)) + EPS
            nrm = x.mean(axis=-1, keepdims=True)
            return jax.nn.softmax(jnp.log(x) * focusing_factor, axis=-1) * nrm

        def _to_heads(x):
            b, n, d = x.shape
            return x.reshape(b, n, H, HD).transpose(0, 2, 1, 3).reshape(b * H, n, HD)

        def _topk_sparsify(x):
            c = x.shape[-1]
            flat = x.reshape(-1, c)
            _, idx = jax.lax.top_k(jnp.abs(flat), KEEP)
            rows = jnp.arange(flat.shape[0])[:, None]
            mask = jnp.zeros(flat.shape, dtype=bool).at[rows, idx].set(True)
            return (flat * mask).reshape(x.shape)
        key = jax.random.key(seed)
        ks = jax.random.split(key, 8)
        mk = lambda k_, shp, s: jax.random.normal(k_, shp, dtype=jnp.float32) * s
        return {'q': mk(ks[0], (B, N, D), 1.0), 'k': mk(ks[1], (B, N, D), 1.0), 'v': mk(ks[2], (B, N, D), 1.0), 'Wq': mk(ks[3], (D, D), 0.02), 'Wk': mk(ks[4], (D, D), 0.02), 'Wv': mk(ks[5], (D, D), 0.02), 'Wp': mk(ks[6], (D, D), 0.02), 'focusing_factor': jnp.asarray(3.0, dtype=jnp.float32)}
    _L2_xattn_all = _L2_xattn_setup()
    _L2_xattn_in = {k: v for k, v in _L2_xattn_all.items() if k in ('Wq', 'Wk', 'Wv', 'Wp', 'focusing_factor')}
    del _L2_xattn_all

    def _L2_ffn_setup():
        import jax, jax.numpy as jnp
        import numpy as np
        TOP_K = 2
        key = jax.random.key(seed)
        ks = jax.random.split(key, 8)
        B, S, H, F, E = (1, 256, 256, 256, 8)
        Fs = 2 * F
        s = lambda k, shape, scale: jax.random.normal(k, shape, dtype=jnp.float32) * scale
        return {'x': s(ks[0], (B, S, H), 1.0), 'router_w': s(ks[1], (H, E), 0.02), 'gate_w': s(ks[2], (E, H, F), 0.02), 'up_w': s(ks[3], (E, H, F), 0.02), 'down_w': s(ks[4], (E, F, H), 0.02), 'shared_gate_w': s(ks[5], (H, Fs), 0.02), 'shared_up_w': s(ks[6], (H, Fs), 0.02), 'shared_down_w': s(ks[7], (Fs, H), 0.02)}
    _L2_ffn_all = _L2_ffn_setup()
    _L2_ffn_in = {k: v for k, v in _L2_ffn_all.items() if k in ('router_w', 'gate_w', 'up_w', 'down_w', 'shared_gate_w', 'shared_up_w', 'shared_down_w')}
    del _L2_ffn_all

    def _L3_xattn_setup():
        import jax, jax.numpy as jnp
        import numpy as np
        EPS = 0.001
        LEAKY_ALPHA = 0.2

        def layer_norm(x, gamma, beta):
            mu = jnp.mean(x, axis=-1, keepdims=True)
            var = jnp.mean(jnp.square(x - mu), axis=-1, keepdims=True)
            return (x - mu) * jax.lax.rsqrt(var + EPS) * gamma + beta

        def attention_head(x_k, x_v, x_q, Wk, Wq, Wv, use_mask):
            K = x_k @ Wk
            V = x_v @ Wv
            Q = x_q @ Wq
            Lq, Lk = (Q.shape[1], K.shape[1])
            score = jnp.einsum('bqd,bkd->bqk', Q, K) / jnp.sqrt(jnp.float32(Lk))
            if use_mask:
                mask = jnp.triu(jnp.full((Lq, Lk), -jnp.inf, dtype=score.dtype), k=1)
                score = score + mask
            return jax.nn.softmax(score, axis=-1) @ V
        key = jax.random.key(seed)
        ks = jax.random.split(key, 12)
        B, S, D = (8, 512, 256)
        inp = {'inputs': jax.random.normal(ks[0], (B, S, D), jnp.float32), 'context_sequence': jax.random.normal(ks[1], (B, S, D), jnp.float32), 'Wk1': jax.random.normal(ks[2], (D, D), jnp.float32) * 0.01, 'Wq1': jax.random.normal(ks[3], (D, D), jnp.float32) * 0.01, 'Wv1': jax.random.normal(ks[4], (D, D), jnp.float32) * 0.01, 'Wk2': jax.random.normal(ks[5], (D, D), jnp.float32) * 0.01, 'Wq2': jax.random.normal(ks[6], (D, D), jnp.float32) * 0.01, 'Wv2': jax.random.normal(ks[7], (D, D), jnp.float32) * 0.01, 'W1': jax.random.normal(ks[8], (D, D), jnp.float32) * (1.0 / np.sqrt(D)), 'b1': jnp.zeros((D,), jnp.float32), 'W2': jax.random.normal(ks[9], (D, D), jnp.float32) * (1.0 / np.sqrt(D)), 'b2': jnp.zeros((D,), jnp.float32), 'gamma': jnp.ones((D,), jnp.float32), 'beta': jnp.zeros((D,), jnp.float32)}
        return inp
    _L3_xattn_all = _L3_xattn_setup()
    _L3_xattn_in = {k: v for k, v in _L3_xattn_all.items() if k in ('Wk1', 'Wq1', 'Wv1', 'Wk2', 'Wq2', 'Wv2', 'W1', 'b1', 'W2', 'b2', 'gamma', 'beta')}
    del _L3_xattn_all

    def _L3_ffn_setup():
        import jax, jax.numpy as jnp
        import numpy as np
        DIM = 256
        HIDDEN = 768
        SCALE = 1.0 / 127.0

        def _dequant(w_int, dtype):
            return w_int.astype(dtype) * jnp.asarray(SCALE, dtype)
        key = jax.random.key(seed)
        k_x, k_g, k_u, k_d = jax.random.split(key, 4)
        x = jax.random.normal(k_x, (4, 512, DIM), dtype=jnp.float32)
        w_gate = jax.random.randint(k_g, (HIDDEN, DIM), -127, 128, dtype=jnp.int32)
        w_up = jax.random.randint(k_u, (HIDDEN, DIM), -127, 128, dtype=jnp.int32)
        w_down = jax.random.randint(k_d, (DIM, HIDDEN), -127, 128, dtype=jnp.int32)
        return {'x': x, 'w_gate': w_gate, 'w_up': w_up, 'w_down': w_down}
    _L3_ffn_all = _L3_ffn_setup()
    _L3_ffn_in = {k: v for k, v in _L3_ffn_all.items() if k in ('w_gate', 'w_up', 'w_down')}
    del _L3_ffn_all
    return {'x': x, 'ctx_1024': ctx_1024, 'L0_xattn_wq': _L0_xattn_in['wq'], 'L0_xattn_bq': _L0_xattn_in['bq'], 'L0_xattn_wk': _L0_xattn_in['wk'], 'L0_xattn_bk': _L0_xattn_in['bk'], 'L0_xattn_wv': _L0_xattn_in['wv'], 'L0_xattn_bv': _L0_xattn_in['bv'], 'L0_xattn_wo': _L0_xattn_in['wo'], 'L0_xattn_bo': _L0_xattn_in['bo'], 'L0_ffn_routing_token': _L0_ffn_in['routing_token'], 'L0_ffn_light_gamma': _L0_ffn_in['light_gamma'], 'L0_ffn_light_w1': _L0_ffn_in['light_w1'], 'L0_ffn_light_b1': _L0_ffn_in['light_b1'], 'L0_ffn_light_w2': _L0_ffn_in['light_w2'], 'L0_ffn_light_b2': _L0_ffn_in['light_b2'], 'L0_ffn_heavy_gamma': _L0_ffn_in['heavy_gamma'], 'L0_ffn_heavy_w1': _L0_ffn_in['heavy_w1'], 'L0_ffn_heavy_b1': _L0_ffn_in['heavy_b1'], 'L0_ffn_heavy_w2': _L0_ffn_in['heavy_w2'], 'L0_ffn_heavy_b2': _L0_ffn_in['heavy_b2'], 'L1_xattn_W_reduce': _L1_xattn_in['W_reduce'], 'L1_xattn_b_reduce': _L1_xattn_in['b_reduce'], 'L1_ffn_Wr': _L1_ffn_in['Wr'], 'L1_ffn_router_bias': _L1_ffn_in['router_bias'], 'L1_ffn_Wg': _L1_ffn_in['Wg'], 'L1_ffn_Wu': _L1_ffn_in['Wu'], 'L1_ffn_Wd': _L1_ffn_in['Wd'], 'L1_ffn_conv_w': _L1_ffn_in['conv_w'], 'L1_ffn_conv_b': _L1_ffn_in['conv_b'], 'L2_xattn_Wq': _L2_xattn_in['Wq'], 'L2_xattn_Wk': _L2_xattn_in['Wk'], 'L2_xattn_Wv': _L2_xattn_in['Wv'], 'L2_xattn_Wp': _L2_xattn_in['Wp'], 'L2_xattn_focusing_factor': _L2_xattn_in['focusing_factor'], 'L2_ffn_router_w': _L2_ffn_in['router_w'], 'L2_ffn_gate_w': _L2_ffn_in['gate_w'], 'L2_ffn_up_w': _L2_ffn_in['up_w'], 'L2_ffn_down_w': _L2_ffn_in['down_w'], 'L2_ffn_shared_gate_w': _L2_ffn_in['shared_gate_w'], 'L2_ffn_shared_up_w': _L2_ffn_in['shared_up_w'], 'L2_ffn_shared_down_w': _L2_ffn_in['shared_down_w'], 'L3_xattn_Wk1': _L3_xattn_in['Wk1'], 'L3_xattn_Wq1': _L3_xattn_in['Wq1'], 'L3_xattn_Wv1': _L3_xattn_in['Wv1'], 'L3_xattn_Wk2': _L3_xattn_in['Wk2'], 'L3_xattn_Wq2': _L3_xattn_in['Wq2'], 'L3_xattn_Wv2': _L3_xattn_in['Wv2'], 'L3_xattn_W1': _L3_xattn_in['W1'], 'L3_xattn_b1': _L3_xattn_in['b1'], 'L3_xattn_W2': _L3_xattn_in['W2'], 'L3_xattn_b2': _L3_xattn_in['b2'], 'L3_xattn_gamma': _L3_xattn_in['gamma'], 'L3_xattn_beta': _L3_xattn_in['beta'], 'L3_ffn_w_gate': _L3_ffn_in['w_gate'], 'L3_ffn_w_up': _L3_ffn_in['w_up'], 'L3_ffn_w_down': _L3_ffn_in['w_down']}

def reference(x, ctx_1024, L0_xattn_wq, L0_xattn_bq, L0_xattn_wk, L0_xattn_bk, L0_xattn_wv, L0_xattn_bv, L0_xattn_wo, L0_xattn_bo, L0_ffn_routing_token, L0_ffn_light_gamma, L0_ffn_light_w1, L0_ffn_light_b1, L0_ffn_light_w2, L0_ffn_light_b2, L0_ffn_heavy_gamma, L0_ffn_heavy_w1, L0_ffn_heavy_b1, L0_ffn_heavy_w2, L0_ffn_heavy_b2, L1_xattn_W_reduce, L1_xattn_b_reduce, L1_ffn_Wr, L1_ffn_router_bias, L1_ffn_Wg, L1_ffn_Wu, L1_ffn_Wd, L1_ffn_conv_w, L1_ffn_conv_b, L2_xattn_Wq, L2_xattn_Wk, L2_xattn_Wv, L2_xattn_Wp, L2_xattn_focusing_factor, L2_ffn_router_w, L2_ffn_gate_w, L2_ffn_up_w, L2_ffn_down_w, L2_ffn_shared_gate_w, L2_ffn_shared_up_w, L2_ffn_shared_down_w, L3_xattn_Wk1, L3_xattn_Wq1, L3_xattn_Wv1, L3_xattn_Wk2, L3_xattn_Wq2, L3_xattn_Wv2, L3_xattn_W1, L3_xattn_b1, L3_xattn_W2, L3_xattn_b2, L3_xattn_gamma, L3_xattn_beta, L3_ffn_w_gate, L3_ffn_w_up, L3_ffn_w_down):
    import jax
    import jax.numpy as jnp

    def _L0_xattn_ref(q, k, v, wq, bq, wk, bk, wv, bv, wo, bo):
        import jax, jax.numpy as jnp
        import numpy as np
        D_MODEL = 256
        N_HEADS = 16
        D_K = D_MODEL // N_HEADS
        WINDOW = 128
        GLOBAL = 16
        CAUSAL = True

        def _rope_tables(seq_len, dk, dtype):
            inv_freq = 1.0 / 10000.0 ** (jnp.arange(0, dk, 2, dtype=jnp.float32) / dk)
            t = jnp.arange(seq_len, dtype=jnp.float32)
            freqs = t[:, None] * inv_freq[None, :]
            emb = jnp.concatenate([freqs, freqs], axis=-1)
            return (jnp.cos(emb).astype(dtype), jnp.sin(emb).astype(dtype))

        def _apply_rope(x, cos, sin):
            x_rope = jnp.concatenate([-x[..., 1::2], x[..., ::2]], axis=-1)
            return x * cos + x_rope * sin

        def _local_window_mask(seq_len, window, global_tokens, causal, dtype):
            i = jnp.arange(seq_len)[:, None]
            j = jnp.arange(seq_len)[None, :]
            blocked = jnp.abs(i - j) > window
            if causal:
                blocked = blocked | (j > i)
            is_global = (i < global_tokens) | (j < global_tokens)
            return jnp.where(blocked & ~is_global, jnp.asarray(-jnp.inf, dtype), jnp.asarray(0.0, dtype))
        B, S, _ = q.shape
        Q = q @ wq.T + bq
        K = k @ wk.T + bk
        V = v @ wv.T + bv
        Q = Q.reshape(B, S, N_HEADS, D_K).transpose(0, 2, 1, 3)
        K = K.reshape(B, S, N_HEADS, D_K).transpose(0, 2, 1, 3)
        V = V.reshape(B, S, N_HEADS, D_K).transpose(0, 2, 1, 3)
        cos, sin = _rope_tables(S, D_K, Q.dtype)
        Q = _apply_rope(Q, cos, sin)
        K = _apply_rope(K, cos, sin)
        mask = _local_window_mask(S, WINDOW, GLOBAL, CAUSAL, Q.dtype)
        scores = jnp.einsum('bhid,bhjd->bhij', Q, K) / jnp.sqrt(jnp.asarray(D_K, Q.dtype))
        scores = scores + mask[None, None, :, :]
        probs = jax.nn.softmax(scores, axis=-1)
        out = jnp.einsum('bhij,bhjd->bhid', probs, V)
        out = out.transpose(0, 2, 1, 3).reshape(B, S, D_MODEL)
        return out @ wo.T + bo

    def _L0_ffn_ref(x, routing_token, light_gamma, light_w1, light_b1, light_w2, light_b2, heavy_gamma, heavy_w1, heavy_b1, heavy_w2, heavy_b2):
        import jax, jax.numpy as jnp
        import numpy as np
        DIM = 256
        NUM_HEAVY = 256
        N_ITERS = 50
        EPS = 1.0
        FETCH_K_RATIO = 9.0 / 8.0

        def rms_norm(x, gamma):
            norm = jnp.maximum(jnp.linalg.norm(x, axis=-1, keepdims=True), 1e-12)
            return x / norm * x.shape[-1] ** 0.5 * gamma

        def feed_forward(x, gamma, w1, b1, w2, b2):
            h = jax.nn.gelu(rms_norm(x, gamma) @ w1 + b1, approximate=False)
            return h @ w2 + b2

        def coor_descent(s, k, n_iters, eps):
            logk = jnp.log(jnp.asarray(k, dtype=s.dtype))

            def step(ab, _):
                a, b = ab
                sb = (s + b) / eps
                a = eps * (logk - jax.scipy.special.logsumexp(sb, axis=-1, keepdims=True))
                b = -jax.nn.relu(s + a)
                return ((a, b), None)
            a0 = jnp.zeros_like(s[..., :1])
            b0 = -s
            (a, b), _ = jax.lax.scan(step, (a0, b0), None, length=n_iters)
            return jnp.exp((s + a + b) / eps)
        b, n, d = x.shape
        light_out = feed_forward(x, light_gamma, light_w1, light_b1, light_w2, light_b2)
        s = jnp.einsum('bnd,d->bn', x, routing_token)
        effective_k = min(NUM_HEAVY * FETCH_K_RATIO, n)
        scores = coor_descent(s, effective_k, N_ITERS, EPS)
        sel_scores, sel_idx = jax.lax.top_k(scores, NUM_HEAVY)
        sel_scores = sel_scores + jax.lax.stop_gradient(1.0 - sel_scores)
        routed = jnp.take_along_axis(x, sel_idx[..., None], axis=1)
        routed_out = feed_forward(routed, heavy_gamma, heavy_w1, heavy_b1, heavy_w2, heavy_b2)
        routed_out = routed_out * sel_scores[..., None]
        batch_idx = jnp.arange(b)[:, None]
        heavy_out = jnp.zeros_like(x).at[batch_idx, sel_idx].set(routed_out)
        return light_out + heavy_out

    def _L1_xattn_ref(queries, keys, W_reduce, b_reduce):
        import jax, jax.numpy as jnp
        import numpy as np
        WINDOW_SIZE = 20
        NEG_BIG = -100000000.0

        def band_mask(S):
            idx = jnp.arange(S)
            return jnp.where(jnp.abs(idx[:, None] - idx[None, :]) <= WINDOW_SIZE, 0.0, NEG_BIG).astype(jnp.float32)
        values = keys
        keys_r = jnp.einsum('bkd,qd->bkq', keys, W_reduce) + b_reduce
        sims = jnp.einsum('bqd,bkd->bqk', queries, keys_r)
        sims = sims + band_mask(queries.shape[1])
        weights = jax.nn.softmax(sims, axis=-1)
        return jnp.einsum('bqk,bkd->bqd', weights, values)

    def _L1_ffn_ref(hidden_states, Wr, router_bias, Wg, Wu, Wd, conv_w, conv_b):
        import jax, jax.numpy as jnp
        import numpy as np
        from jax import lax
        H = 256
        E = 8
        E_MLP = E - 4
        TOP_K = 2
        I = 128
        KC = 4
        SHARED_SCALE = 1.0
        B, S, Hd = hidden_states.shape
        T = B * S
        x = hidden_states.reshape(T, Hd)
        scores = jax.nn.sigmoid(x @ Wr)
        _, idx = lax.top_k(scores + router_bias, TOP_K)
        w = jnp.take_along_axis(scores, idx, axis=-1)
        w = w / (jnp.sum(w, axis=-1, keepdims=True) + 1e-09)
        cw = jnp.zeros((T, E), dtype=x.dtype).at[jnp.arange(T)[:, None], idx].add(w)
        g = jnp.einsum('th,ehi->tei', x, Wg)
        u = jnp.einsum('th,ehi->tei', x, Wu)
        hid = jax.nn.silu(g) * u
        mlp_out = jnp.einsum('tei,eih->teh', hid, Wd)
        routed = jnp.einsum('te,teh->th', cw[:, :E_MLP], mlp_out)
        routed = routed + cw[:, E_MLP:E_MLP + 1] * x
        routed = routed + cw[:, E_MLP + 2:E_MLP + 3] * x
        routed = routed + cw[:, E_MLP + 3:E_MLP + 4] * jax.nn.relu(x)
        routed = routed.reshape(B, S, Hd)
        shared = lax.conv_general_dilated(hidden_states, conv_w, window_strides=(1,), padding=[(KC - 1, 0)], dimension_numbers=('NHC', 'HIO', 'NHC'), feature_group_count=Hd) + conv_b
        return routed + SHARED_SCALE * shared

    def _L2_xattn_ref(q, k, v, Wq, Wk, Wv, Wp, focusing_factor):
        import jax, jax.numpy as jnp
        import numpy as np
        B, N, D = (4, 1024, 256)
        H = 16
        HD = D // H
        EPS = 1e-06
        BASE_SPARSITY = 0.3
        KEEP = max(int((1.0 - BASE_SPARSITY) * HD), 1)
        LEAKY_SLOPE = 0.01

        def _focus(x, focusing_factor):
            x = jnp.abs(jnp.where(x >= 0, x, LEAKY_SLOPE * x)) + EPS
            nrm = x.mean(axis=-1, keepdims=True)
            return jax.nn.softmax(jnp.log(x) * focusing_factor, axis=-1) * nrm

        def _to_heads(x):
            b, n, d = x.shape
            return x.reshape(b, n, H, HD).transpose(0, 2, 1, 3).reshape(b * H, n, HD)

        def _topk_sparsify(x):
            c = x.shape[-1]
            flat = x.reshape(-1, c)
            _, idx = jax.lax.top_k(jnp.abs(flat), KEEP)
            rows = jnp.arange(flat.shape[0])[:, None]
            mask = jnp.zeros(flat.shape, dtype=bool).at[rows, idx].set(True)
            return (flat * mask).reshape(x.shape)
        b, n, d = q.shape
        q = q @ Wq.T
        k = k @ Wk.T
        v = v @ Wv.T
        q = _focus(q, focusing_factor)
        k = _focus(k, focusing_factor)
        qh, kh, vh = (_to_heads(q), _to_heads(k), _to_heads(v))
        qh = _topk_sparsify(qh)
        kh = _topk_sparsify(kh)
        length_k = float(n)
        sqrt_l = jnp.sqrt(jnp.asarray(length_k, dtype=q.dtype))
        k_mean = kh.mean(axis=1)
        z_inv = jnp.einsum('bnd,bd->bn', qh, k_mean) + EPS
        kv = jnp.einsum('bnc,bnd->bcd', kh / sqrt_l, vh / sqrt_l)
        y = jnp.einsum('bnc,bcd->bnd', qh, kv) / z_inv[..., None]
        y = y.reshape(b, H, n, HD).transpose(0, 2, 1, 3).reshape(b, n, d)
        return y @ Wp.T

    def _L2_ffn_ref(x, router_w, gate_w, up_w, down_w, shared_gate_w, shared_up_w, shared_down_w):
        import jax, jax.numpy as jnp
        import numpy as np
        TOP_K = 2
        B, S, H = x.shape
        N = B * S
        xf = x.reshape(N, H)
        scores = jax.nn.softmax(xf @ router_w, axis=-1)
        topk_scores, topk_idx = jax.lax.top_k(scores, TOP_K)
        E = scores.shape[-1]
        combine = jnp.zeros((N, E), dtype=x.dtype).at[jnp.arange(N)[:, None], topk_idx].add(topk_scores)
        g = jnp.einsum('nh,ehf->enf', xf, gate_w)
        u = jnp.einsum('nh,ehf->enf', xf, up_w)
        y = jnp.einsum('enf,efh->enh', jax.nn.silu(g) * u, down_w)
        routed = jnp.einsum('enh,ne->nh', y, combine)
        shared = jax.nn.silu(xf @ shared_gate_w) * (xf @ shared_up_w) @ shared_down_w
        return (shared + routed).reshape(B, S, H)

    def _L3_xattn_ref(inputs, context_sequence, Wk1, Wq1, Wv1, Wk2, Wq2, Wv2, W1, b1, W2, b2, gamma, beta):
        import jax, jax.numpy as jnp
        import numpy as np
        EPS = 0.001
        LEAKY_ALPHA = 0.2

        def layer_norm(x, gamma, beta):
            mu = jnp.mean(x, axis=-1, keepdims=True)
            var = jnp.mean(jnp.square(x - mu), axis=-1, keepdims=True)
            return (x - mu) * jax.lax.rsqrt(var + EPS) * gamma + beta

        def attention_head(x_k, x_v, x_q, Wk, Wq, Wv, use_mask):
            K = x_k @ Wk
            V = x_v @ Wv
            Q = x_q @ Wq
            Lq, Lk = (Q.shape[1], K.shape[1])
            score = jnp.einsum('bqd,bkd->bqk', Q, K) / jnp.sqrt(jnp.float32(Lk))
            if use_mask:
                mask = jnp.triu(jnp.full((Lq, Lk), -jnp.inf, dtype=score.dtype), k=1)
                score = score + mask
            return jax.nn.softmax(score, axis=-1) @ V
        att = attention_head(inputs, inputs, inputs, Wk1, Wq1, Wv1, use_mask=True)
        norm = layer_norm(att + inputs, gamma, beta)
        att2 = attention_head(context_sequence, context_sequence, att, Wk2, Wq2, Wv2, use_mask=False)
        norm2 = layer_norm(att2 + norm, gamma, beta)
        h = jax.nn.leaky_relu(norm2 @ W1 + b1, negative_slope=LEAKY_ALPHA)
        ff = h @ W2 + b2
        norm3 = layer_norm(ff + norm2, gamma, beta)
        return jax.nn.relu(norm3)

    def _L3_ffn_ref(x, w_gate, w_up, w_down):
        import jax, jax.numpy as jnp
        import numpy as np
        DIM = 256
        HIDDEN = 768
        SCALE = 1.0 / 127.0

        def _dequant(w_int, dtype):
            return w_int.astype(dtype) * jnp.asarray(SCALE, dtype)
        wg = _dequant(w_gate, x.dtype)
        wu = _dequant(w_up, x.dtype)
        wd = _dequant(w_down, x.dtype)
        gate = jnp.einsum('bsd,hd->bsh', x, wg)
        up = jnp.einsum('bsd,hd->bsh', x, wu)
        h = jax.nn.silu(gate) * up
        return jnp.einsum('bsh,dh->bsd', h, wd)
    x = x + _L0_xattn_ref(_layernorm(x, axis=-1), ctx_1024, ctx_1024, L0_xattn_wq, L0_xattn_bq, L0_xattn_wk, L0_xattn_bk, L0_xattn_wv, L0_xattn_bv, L0_xattn_wo, L0_xattn_bo)
    x = x + _L0_ffn_ref(_layernorm(x, axis=-1), L0_ffn_routing_token, L0_ffn_light_gamma, L0_ffn_light_w1, L0_ffn_light_b1, L0_ffn_light_w2, L0_ffn_light_b2, L0_ffn_heavy_gamma, L0_ffn_heavy_w1, L0_ffn_heavy_b1, L0_ffn_heavy_w2, L0_ffn_heavy_b2)
    x = x + _L1_xattn_ref(_layernorm(x, axis=-1), ctx_1024, L1_xattn_W_reduce, L1_xattn_b_reduce)
    x = x + _L1_ffn_ref(_layernorm(x, axis=-1), L1_ffn_Wr, L1_ffn_router_bias, L1_ffn_Wg, L1_ffn_Wu, L1_ffn_Wd, L1_ffn_conv_w, L1_ffn_conv_b)
    x = x + _L2_xattn_ref(_layernorm(x, axis=-1), ctx_1024, ctx_1024, L2_xattn_Wq, L2_xattn_Wk, L2_xattn_Wv, L2_xattn_Wp, L2_xattn_focusing_factor)
    x = x + _L2_ffn_ref(_layernorm(x, axis=-1), L2_ffn_router_w, L2_ffn_gate_w, L2_ffn_up_w, L2_ffn_down_w, L2_ffn_shared_gate_w, L2_ffn_shared_up_w, L2_ffn_shared_down_w)
    x = x + _L3_xattn_ref(_layernorm(x, axis=-1), ctx_1024, L3_xattn_Wk1, L3_xattn_Wq1, L3_xattn_Wv1, L3_xattn_Wk2, L3_xattn_Wq2, L3_xattn_Wv2, L3_xattn_W1, L3_xattn_b1, L3_xattn_W2, L3_xattn_b2, L3_xattn_gamma, L3_xattn_beta)
    x = x + _L3_ffn_ref(_layernorm(x, axis=-1), L3_ffn_w_gate, L3_ffn_w_up, L3_ffn_w_down)
    return x

_drawn_inputs = setup_inputs


def setup_inputs(seed=0):
    import zlib

    import numpy as np

    out = dict(_drawn_inputs(seed))
    spreads = {'L0_ffn_light_gamma': (1.0, 0.2),
     'L0_ffn_light_b1': (0.0, 0.1),
     'L0_ffn_light_b2': (0.0, 0.1),
     'L0_ffn_heavy_gamma': (1.0, 0.2),
     'L0_ffn_heavy_b1': (0.0, 0.1),
     'L0_ffn_heavy_b2': (0.0, 0.1),
     'L1_ffn_router_bias': (0.0, 0.1),
     'L1_ffn_conv_b': (0.0, 0.1),
     'L3_xattn_b1': (0.0, 1.308),
     'L3_xattn_b2': (0.0, 0.88),
     'L3_xattn_gamma': (1.0, 0.2),
     'L3_xattn_beta': (0.0, 0.309)}
    factors = {'L1_xattn_b_reduce': 200.0,
     'L2_xattn_Wq': 4.018,
     'L2_xattn_Wk': 4.145,
     'L2_ffn_router_w': 8.0,
     'L2_ffn_gate_w': 8.0,
     'L2_ffn_up_w': 8.0,
     'L2_ffn_down_w': 8.0,
     'L2_ffn_shared_gate_w': 3.549,
     'L2_ffn_shared_up_w': 3.486,
     'L2_ffn_shared_down_w': 3.484,
     'L3_xattn_Wk1': 64.0,
     'L3_xattn_Wq1': 64.0,
     'L3_xattn_Wk2': 64.0,
     'L3_xattn_Wq2': 64.0,
     'L3_xattn_Wv1': 8.0,
     'L3_xattn_Wv2': 5.786}
    for name, (base, spread) in spreads.items():
        noise = np.random.default_rng([zlib.crc32(name.encode()), seed]).standard_normal(out[name].shape)
        drawn = base * np.exp(spread * noise) if base else spread * noise
        out[name] = jnp.asarray(drawn.astype(out[name].dtype))
    for name, factor in factors.items():
        out[name] = (out[name] * factor).astype(out[name].dtype)
    return out
```

```python
from contextlib import ExitStack

import concourse.bass as bass
from concourse import mybir

F32 = mybir.dt.float32
BF16 = mybir.dt.bfloat16
I32 = mybir.dt.int32
ALU = mybir.AluOpType
ACT = mybir.ActivationFunctionType
AX_X = mybir.AxisListType.X

P = 128
NB, S, D = 4, 512, 256
NT = S // P
NH, DK = 16, 16
HG = 4
NG = NH // HG
BIG = 3.0e38
K_EFF = 256 * 9.0 / 8.0
TOP_HEAVY = 256
ROUNDS, ITERS = 4, 12
KEYW = 192
KEYPAD = 640
WIN = (512, 256, 288, 288)
WOFF = (0, 512, 768, 1056)
NSLOT = 2
CHUNK = 2048

WEIGHTS = [("wq", 1024), ("wk", 1024), ("wv", 512), ("wo", 512),
           ("lw1", 256), ("lw2", 256),
           ("wred", 512), ("l1r", 16), ("l1g", 1024), ("l1u", 1024), ("l1d", 1024),
           ("w2q", 512), ("w2k", 512), ("w2v", 512), ("w2p", 512), ("l2r", 16),
           ("k1", 512), ("q1", 512), ("v1", 512), ("k2", 512), ("q2", 512), ("v2", 512),
           ("f1", 512), ("f2", 512)]
WGROUPS = [("wq", "wo"), ("lw1", "lw2"), ("wred", "l1d"), ("w2q", "l2r"), ("k1", "f2")]
COLS = [("bq", 4), ("bk", 4), ("lgam", 2), ("hgam", 2), ("lb1", 1), ("hb1", 8), ("bred", 2),
        ("convw", 8), ("b1", 2), ("focus", 1)]
ROWS = [("bv", 256), ("bo", 256), ("lb2", 256), ("hb2", 256), ("convb", 256), ("b2", 256),
        ("gamma", 256), ("beta", 256), ("rt", 256), ("rbias", 8)]
CONST = [("rope", 512), ("fold", 128), ("ident", 128), ("gmask", 256), ("bmask", 136)]
CONSTB = [("identb", 128), ("mask0", 1344), ("band", 4 * KEYW), ("causal", 128), ("lt", 896), ("ge", 896)]


def offsets(table):
    at, out = 0, {}
    for name, n in table:
        out[name] = (at, n)
        at += n
    return out, at


def tiles_of_unit(u):
    qt = u // NG
    if qt == 0:
        return [(j,) for j in range(HG)]
    return ([None] if qt >= 2 else []) + [(0, 1), (2, 3)]


PT_TILES = [(u, heads) for u in range(NT * NG) for heads in tiles_of_unit(u)]


def psum_plan():
    out = []

    def use(key, bank):
        out.append((key, bank))

    def pair(name, banks):
        for i, bank in enumerate(banks):
            use((name, i), bank)

    for g in range(NG):
        use(("K", g), 2 + g % 2)
        use(("F", g), 4 + g % 2)
    pair("V", (6, 7))
    use("Vg", 2)
    pair("xT0", (0, 1))
    for g in range(NG):
        use(("Q", g), 3 + g % 3)
    for j in range(HG):
        use(("S", 0, j), j)
    for n, (u, heads) in enumerate(PT_TILES):
        if (n == 0 or PT_TILES[n - 1][0] != u) and u + 1 < NT * NG:
            for j in range(HG):
                use(("S", u + 1, j), j)
        use(("PT", n), 4 + n % 3)
        if n >= 2:
            plan_o(use, n - 2)
    plan_o(use, len(PT_TILES) - 2)
    plan_o(use, len(PT_TILES) - 1)
    pair("OT", (4, 5))
    pair("Y0", (0, 1))
    use("R", 2)
    pair("xT1", (0, 1))
    use(("h", "light"), 3)
    use("chain", 2)
    for m in range(8):
        use(("h", m), (0, 1, 3)[m % 3])
    pair("yl", (4, 5))
    pair("yh", (6, 7))
    pair("KT1", (2, 3))
    pair("xT2", (0, 1))
    for t in range(NT):
        use(("S1", t), 4 + t)
    for t in range(NT):
        use(("PT1", t), 2 + t % 2)
    pair("O1", (0, 1))
    pair("xT3", (0, 1))
    use("RT3", 7)
    for e in range(4):
        use(("G3", e), 2 + e % 2)
        use(("U3", e), 4 + e % 2)
        if e == 0:
            pair("CT3", (6, 0))
        else:
            for i in range(2):
                use(("Y3", e - 1, i), (1, 6, 0)[(2 * e + i) % 3])
    for i in range(2):
        use(("Y3", 3, i), (1, 6, 0)[(8 + i) % 3])
    pair("k4", (2, 3))
    pair("v4", (4, 5))
    pair("xT4", (0, 1))
    pair("q4", (6, 7))
    pair("KV4", (2, 3))
    pair("QT4", (4, 5))
    for t in range(NT):
        use(("y4", t), 6 + t % 2)
    pair("yT4", (0, 1))
    pair("O4", (2, 3))
    pair("xT5", (0, 1))
    use("RT5", 7)
    for e in range(10):
        for f in range(2):
            use(("G5", e, f), 2 + f)
            use(("U5", e, f), 4 + f)
        if e:
            for i in range(2):
                use(("Y5", e - 1, i), (6, 7, 0, 1)[(2 * e + i) % 4])
    for i in range(2):
        use(("Y5", 9, i), (6, 7, 0, 1)[(20 + i) % 4])
    for h in range(2):
        use(("K6", 1, h), 2 + h)
    for i in range(2):
        use(("V6", 1, i), 4 + i)
    pair("xT6", (0, 1))
    for h in range(2):
        use(("K6", 0, h), 2 + h)
        use(("Q6", 0, h), 4 + h)
    for i in range(2):
        use(("V6", 0, i), 6 + i)
    for a in range(2):
        for t in range(NT):
            use(("S6", a, t), 2 + t)
        for t in range(NT):
            use(("P6", a, t), 6 + t % 2)
        for i in range(2):
            use(("O6", a, i), i)
        if a == 0:
            pair("aT6", (2, 3))
            for h in range(2):
                use(("Q6", 1, h), 4 + h)
    pair("nT6", (6, 7))
    for m in range(2):
        use(("h6", m), 2 + m)
    pair("f6", (4, 5))
    pair("xT7", (0, 1))
    for m in range(6):
        use(("G7", m), 2 + m % 2)
        use(("U7", m), 4 + m % 2)
    pair("Y7", (6, 7))
    count, where = [0] * 8, {}
    for key, bank in out:
        assert key not in where, key
        where[key] = (bank, count[bank])
        count[bank] += 1
    return where


def plan_o(use, n):
    u = PT_TILES[n][0]
    if u % NG == 0 and (n == 0 or PT_TILES[n - 1][0] != u):
        use(("O", u // NG), 7)


PLAN = psum_plan()
LN_INDEX = {0: 0, 1: 1, 2: 2, 3: 3, 4: 4, 5: 5, 6: 6, "6a": 7, "6b": 8, "6c": 9, 7: 10}


def network(nc, x_in, ctxT_in, ctxs_in, ctx0_in, w_in, stream_in, wint_in, cols_in, rows_in, const_in, constb_in, out):
    stack = ExitStack()
    with stack:
        def sb(name, shape, dt=F32):
            return stack.enter_context(nc.sbuf_tensor(name, shape, dt))

        def sem(name):
            return stack.enter_context(nc.semaphore(name))

        woff, wn = offsets(WEIGHTS)
        coff, cn = offsets(COLS)
        roff, rn = offsets(ROWS)
        koff, kn = offsets(CONST)
        boff, bn = offsets(CONSTB)
        weights = sb("weights", [P, wn])
        wint = sb("wint", [P, 4608], I32)
        wl3 = wint[:, :].bitcast(F32)
        stream = sb("stream", [P, NSLOT, CHUNK])
        cols = sb("cols", [P, cn])
        rows = sb("rows", [P, rn])
        const = sb("const", [P, kn])
        constb = sb("constb", [P, bn], BF16)

        def W(name, k=2):
            at, n = woff[name]
            return weights[:, at:at + n].rearrange("p (k n) -> p k n", k=k)

        def col(name, i=0):
            return cols[:, coff[name][0] + i:coff[name][0] + i + 1]

        def row(name, n=1):
            at, w = roff[name]
            r = rows[:, at:at + w]
            return r if n == 1 else r.unsqueeze(1).broadcast_to([P, n, w])

        def K(name):
            at, n = koff[name]
            return const[:, at:at + n]

        def KB(name):
            at, n = boff[name]
            return constb[:, at:at + n]

        x = sb("x", [P, NT, D])
        xn = sb("xn", [P, NT, D])
        xnT = sb("xnT", [P, 2, S])
        ctxT = sb("ctxT", [P, 2, S])
        ctxs = sb("ctxs", [P, 5, D])
        small = sb("small", [P, 512])
        onesk = sb("onesk", [P, P])
        EVEN, ODD = 12288, 7168
        even = sb("even", [P, EVEN])
        odd = sb("odd", [P, ODD])
        at_small = [0]

        def sm(n, shape=None):
            a = small[:, at_small[0]:at_small[0] + n]
            at_small[0] += n
            assert at_small[0] <= 512
            return a if shape is None else a.rearrange("p (a b) -> p a b", a=shape)

        class Area:
            def __init__(self, t, size):
                self.t, self.size, self.at = t, size, 0

            def take(self, n):
                a = self.t[:, self.at:self.at + n]
                self.at += n
                assert self.at <= self.size, self.at
                return a

        def v3(ap, a):
            return ap.rearrange("p (a b) -> p a b", a=a)

        eps6 = sm(1)
        mhalf = sm(NT)
        stats = sm(NT * 6, NT)
        mv = sm(NT * 2, NT)
        var = sm(NT)
        rstd = sm(NT)
        nm = sm(8, 2)
        den = sm(NT * NH, NT)
        rden = sm(NH)
        rden4 = sm(NT)
        nm4 = sm(NT)
        den4 = sm(NT)
        ss = sm(NT)
        rmsr = sm(NT)
        scol = sm(NT)
        kcol = sm(NT)
        nmax = sm(1)
        lsum = sm(1)
        lnv = sm(1)
        lsh = sm(2)
        lfin = sm(1)
        ce = sm(NT)
        ev = sm(NT)
        jc = sm(NT)
        rs = sm(2)
        rk1 = sm(NT)
        rk2 = sm(NT)
        score = sm(NT)
        wgt = sm(NT)
        sc = sm(32, NT)
        tb = sm(64, NT)
        t8 = sm(32, NT)
        tr = sm(64, NT)
        cw = sm(40, NT)
        c46 = sm(NT)
        fsum = sm(NT)
        psumm = sm(NT)
        fmax = sm(NT)
        fco = sm(NT)

        ar = Area(even, EVEN)
        Kf = v3(ar.take(NG * S), NG)
        Qr = v3(ar.take(NG * S), NG)
        V0 = v3(ar.take(NT * D), NT)
        Vg = ar.take(D)
        probs = ar.take(2 * HG * S).rearrange("p (a b c) -> p a b c", a=2, b=HG)
        Kr = probs[:, 0]
        PTs = v3(ar.take(3 * S), 3)
        Ot = v3(ar.take(NT * D), NT)
        OT = probs[:, 0, 0:2]
        ctx0 = Ot[:, 0:2, 0:P]
        ar = Area(even, EVEN)
        kr1 = v3(ar.take(2 * KEYPAD), 2)
        P1 = v3(ar.take(NT * KEYW), NT)
        PT1 = v3(ar.take(NT * 256), NT)
        ar = Area(even, EVEN)
        V2 = ar.take(NT * 2 * 132).rearrange("p (t c n) -> p t c n", t=NT, c=2)
        fa = v3(ar.take(NT * D), NT)
        fb = v3(ar.take(NT * D), NT)
        yin = ar.take(NT * NH * 19).rearrange("p (t h n) -> p t h n", t=NT, h=NH)
        yout = ar.take(NT * NH * 19).rearrange("p (t h n) -> p t h n", t=NT, h=NH)
        ym = ar.take(2 * NT * D).rearrange("p (w t n) -> p w t n", w=2, t=NT)
        top8 = ar.take(NT * NH * 8).rearrange("p (t h n) -> p t h n", t=NT, h=NH)
        kvm = v3(ar.take(2 * 136), 2)
        qsT = v3(ar.take(2 * S), 2)
        y4 = v3(ar.take(NT * D), NT)
        yT4 = v3(ar.take(2 * S), 2)
        zr = v3(ar.take(16), 2)
        ar = Area(even, EVEN)
        K6 = [v3(ar.take(2 * S), 2) for _ in range(2)]
        V6 = [v3(ar.take(NT * D), NT) for _ in range(2)]
        Q6 = v3(ar.take(2 * S), 2)
        P6 = v3(ar.take(NT * S), NT)
        PT6 = v3(ar.take(2 * S), 2)
        att = v3(ar.take(NT * D), NT)
        n1 = v3(ar.take(NT * D), NT)
        n2 = v3(ar.take(NT * D), NT)
        attT = v3(ar.take(2 * S), 2)
        h6 = K6[0]
        ar = Area(odd, ODD)
        xlT = v3(ar.take(2 * S), 2)
        xhT = v3(ar.take(2 * S), 2)
        hL = ar.take(S)
        hH = v3(ar.take(8 * S), 8)
        srow = ar.take(S)
        krow = xlT[:, 0, :]
        jrow = xlT[:, 1, :]
        th = xhT[:, 0, 0:D]
        ar = Area(odd, ODD)
        sg3 = v3(ar.take(2 * S), 2)
        hid3 = v3(ar.take(2 * S), 2)
        conv = v3(ar.take(2 * S), 2)
        extra = v3(ar.take(NT * D), NT)
        pa3 = ar.take(D)
        pb3 = ar.take(D)
        ar = Area(odd, ODD)
        sg5 = v3(ar.take(2 * S), 2)
        hid5 = ar.take(4 * S).rearrange("p (e f n) -> p e f n", e=2, f=2)
        ar = Area(odd, ODD)
        sg7 = v3(ar.take(2 * S), 2)
        hid7 = v3(ar.take(6 * S), 6)
        v6 = v3(sg7[:, :, :].rearrange("p a b -> p (a b)"), 2)

        ps = stack.enter_context(nc.psum_tensor("ps", [P, 8, 512], F32))

        w_loaded = [sem(f"w_loaded{i}") for i in range(len(WGROUPS))]
        wint_loaded = sem("wint_loaded")
        const_loaded = sem("const_loaded")
        setup_done = sem("setup_done")
        setup_step = sem("setup_step")
        go = sem("go")
        passed = sem("passed")
        first = sem("batch_done")
        batch_done = first
        psum_filled = [sem(f"psum_filled{i}") for i in range(8)]
        psum_taken = [sem(f"psum_taken{i}") for i in range(8)]
        x_loaded = sem("x_loaded")
        ctx_loaded = sem("ctx_loaded")
        chunk_loaded = [sem(f"chunk_loaded{i}") for i in range(NSLOT)]
        out_stored = sem("out_stored")
        ln_stats = sem("ln_stats")
        ln_rstd = sem("ln_rstd")
        xn_ready = sem("xn_ready")
        x_biased = sem("x_biased")
        max_ready = sem("max_ready")
        global_ready = sem("global_ready")
        scol_ready = sem("scol_ready")
        rms_sum = sem("rms_sum")
        rms_ready = sem("rms_ready")
        xr_ready = sem("xr_ready")
        lse_max = sem("lse_max")
        ln_ready = sem("ln_ready")
        ce_ready = sem("ce_ready")
        ev_ready = sem("ev_ready")
        rowsum_ready = sem("rowsum_ready")
        total_ready = sem("total_ready")
        kcol_ready = sem("kcol_ready")
        score_ready = sem("score_ready")
        keypad_ready = sem("keypad_ready")
        max1_ready = sem("max1_ready")
        router_exp = sem("router_exp")
        cw_ready = sem("cw_ready")
        extra_ready = sem("extra_ready")
        conv_ready = sem("conv_ready")
        silu_ready = sem("silu_ready")
        ones_ready = sem("ones_ready")
        abs_ready = sem("abs_ready")
        log_ready = sem("log_ready")
        focus_in = sem("focus_in")
        focus_exp = sem("focus_exp")
        sparse_ready = sem("sparse_ready")
        affine_ready = sem("affine_ready")
        max6_ready = sem("max6_ready")
        h6_ready = sem("h6_ready")
        dve_step = sem("dve_step")
        act_step = sem("act_step")
        pool_step = sem("pool_step")
        last = pool_step

        def bank(key):
            return PLAN[key][0]

        def psb(key):
            return ps[:, PLAN[key][0], :]

        def got(eng, key):
            eng.wait_ge(psum_filled[PLAN[key][0]], PLAN[key][1] + 1)
            return psb(key)

        def in_sbuf(eng, key):
            eng.wait_ge(psum_taken[PLAN[key][0]], PLAN[key][1] + 1)

        def meet(eng, b):
            eng.drain().then_inc(batch_done, 1)
            eng.wait_ge(go, b + 1)
            eng.sem_inc(passed, 1)

        block = stack.enter_context(nc.Block())

        @block.sync
        def _(sp):
            sp.dma_start(cols[:, :], cols_in).then_inc(const_loaded, 16)
            sp.dma_start(rows[:, :], rows_in).then_inc(const_loaded, 16)
            sp.dma_start(const[:, :], const_in).then_inc(const_loaded, 16)
            sp.dma_start(even[:, 0:bn], constb_in).then_inc(const_loaded, 16)
            for i, (a, z) in enumerate(WGROUPS):
                lo, hi = woff[a][0], woff[z][0] + woff[z][1]
                sp.dma_start(weights[:, lo:hi], w_in[:, lo:hi]).then_inc(w_loaded[i], 16)
            sp.dma_start(wint[:, :], wint_in).then_inc(wint_loaded, 16)
            with sp.Fori(0, NB) as b:
                sp.dma_start(x[:, :, :].rearrange("p t d -> p (t d)"),
                             x_in[bass.ds(b * P, P), :]).then_inc(x_loaded, 16)
                sp.dma_start(ctxT[:, :, :].rearrange("p t d -> p (t d)"),
                             ctxT_in[bass.ds(b * P, P), :]).then_inc(ctx_loaded, 16)
                sp.dma_start(ctxs[:, :, :].rearrange("p t d -> p (t d)"),
                             ctxs_in[bass.ds(b * P, P), :]).then_inc(ctx_loaded, 16)
                for k in range(2):
                    sp.dma_start(ctx0[:, k, :], ctx0_in[bass.ds(b * P, P), k * P:(k + 1) * P]).then_inc(ctx_loaded, 16)
                for c in range(12):
                    if c >= NSLOT:
                        got(sp, ("yh", 1) if c < 4 else ("Y5", c - 4, 1))
                    n = CHUNK if c < 2 else 1536
                    sp.dma_start(stream[:, c % NSLOT, 0:n],
                                 stream_in[c * P:(c + 1) * P, 0:n]).then_inc(chunk_loaded[c % NSLOT], 16)
                for i in range(2):
                    in_sbuf(sp, ("Y7", i))
                    sp.dma_start(out[bass.ds(b * P, P), i * 512:(i + 1) * 512],
                                 x[:, 2 * i:2 * i + 2, :].rearrange("p t d -> p (t d)")).then_inc(out_stored, 16)
                sp.wait_ge(out_stored, 32)
                sp.wait_ge(batch_done, 4)
                sp.sem_clear(range(first.num, last.num + 1))
                sp.drain().then_inc(go, 1)

        @block.gpsimd
        def _(pool):
            g = nc.gpsimd
            g.memset(eps6, 1e-6).then_inc(setup_step, 1)
            g.memset(mhalf, -0.5).then_inc(setup_step, 1)
            g.memset(onesk[:, :], 1.0 / K_EFF).then_inc(setup_step, 1)
            g.memset(cw.rearrange("p t e -> p (t e)"), 1.0).then_inc(setup_step, 1)
            g.memset(tb.rearrange("p t e -> p (t e)"), BIG).then_inc(setup_step, 1)
            pool.wait_ge(setup_step, 5)
            pool.wait_ge(const_loaded, 64)
            g.tensor_copy(constb[:, :], even[:, 0:bn]).then_inc(setup_done, 1)
            pool.wait_ge(wint_loaded, 16)
            g.tensor_scalar(wl3, wint[:, :], 1.0 / 127.0, None, ALU.mult).then_inc(setup_done, 1)
            pool.wait_ge(setup_done, 2)

            with pool.Fori(0, NB) as b:
                n = [0]

                def link(ins):
                    n[0] += 1
                    ins.then_inc(pool_step, 1)
                    pool.wait_ge(pool_step, n[0])

                def rstd_of(idx, eps):
                    pool.wait_ge(ln_stats, idx + 1)
                    link(g.tensor_scalar(var, mv[:, :, 1], eps, None, ALU.add))
                    g.tensor_tensor(rstd, var, mhalf, ALU.pow).then_inc(ln_rstd, 1)

                def add_row(idx, name):
                    pool.wait_ge(xn_ready, NT * (idx + 1))
                    g.tensor_tensor(x[:, :, :], x[:, :, :], row(name, NT), ALU.add).then_inc(x_biased, 1)

                rstd_of(0, 1e-5)
                add_row(0, "bo")
                for u in range(2 * NG, NT * NG):
                    for j in range(HG):
                        in_sbuf(pool, ("S", u, j))
                    g.tensor_copy(probs[:, u % 2, 0, 384:512].rearrange("p (j k) -> p j k", j=HG),
                                  probs[:, u % 2, :, 256:288]).then_inc(global_ready, 1)
                rstd_of(1, 1e-5)
                add_row(1, "lb2")
                pool.wait_ge(rms_sum, 1)
                link(g.tensor_scalar(ss, ss, 1e-24, None, ALU.max))
                link(g.tensor_tensor(rmsr, ss, mhalf, ALU.pow))
                g.tensor_scalar(rmsr, rmsr, 16.0, None, ALU.mult).then_inc(rms_ready, 1)
                rstd_of(2, 1e-5)
                g.memset(kr1[:, :, 0:32], 0.0).then_inc(keypad_ready, 1)
                g.memset(kr1[:, :, 32 + S:KEYPAD], 0.0).then_inc(keypad_ready, 1)
                rstd_of(3, 1e-5)
                add_row(3, "convb")
                pool.wait_ge(x_biased, 3)
                pool.wait_ge(cw_ready, 1)
                link(g.tensor_tensor(c46, cw[:, :, 4], cw[:, :, 6], ALU.add))
                for t in range(NT):
                    link(g.tensor_scalar(pa3, xn[:, t, :], 0.0, cw[:, t, 7:8], ALU.max, ALU.mult))
                    link(g.tensor_scalar(pb3, xn[:, t, :], c46[:, t:t + 1], None, ALU.mult))
                    link(g.tensor_tensor(pa3, pa3, pb3, ALU.add))
                    g.tensor_tensor(extra[:, t, :], pa3, x[:, t, :], ALU.add).then_inc(extra_ready, 1)
                    pool.wait_ge(extra_ready, t + 1)
                g.memset(V2[:, :, :, 128:129], 1.0).then_inc(ones_ready, 1)
                g.memset(yin[:, :, :, 16:19], 1.0).then_inc(ones_ready, 1)
                rstd_of(4, 1e-5)
                rstd_of(5, 1e-5)
                rstd_of(6, 1e-5)
                rstd_of(7, 1e-3)
                pool.wait_ge(xn_ready, NT * 8)
                link(g.tensor_tensor(n1, n1, row("gamma", NT), ALU.mult))
                g.tensor_tensor(n1, n1, row("beta", NT), ALU.add).then_inc(affine_ready, 1)
                rstd_of(8, 1e-3)
                pool.wait_ge(xn_ready, NT * 9)
                link(g.tensor_tensor(n2, n2, row("gamma", NT), ALU.mult))
                g.tensor_tensor(n2, n2, row("beta", NT), ALU.add).then_inc(affine_ready, 1)
                in_sbuf(pool, ("nT6", 0))
                in_sbuf(pool, ("nT6", 1))
                g.tensor_tensor(n2, n2, row("b2", NT), ALU.add).then_inc(affine_ready, 1)
                rstd_of(9, 1e-3)
                pool.wait_ge(xn_ready, NT * 10)
                link(g.tensor_tensor(n1, n1, row("gamma", NT), ALU.mult))
                g.tensor_tensor(n1, n1, row("beta", NT), ALU.add).then_inc(affine_ready, 1)
                rstd_of(10, 1e-5)
                meet(pool, b)

        @block.tensor
        def _(pe):
            T = nc.tensor
            ident = K("ident")
            identb = KB("identb")
            pe.wait_ge(setup_done, 1)
            pe.wait_ge(const_loaded, 64)

            def room(key):
                if PLAN[key][1]:
                    pe.wait_ge(psum_taken[PLAN[key][0]], PLAN[key][1])
                return psb(key)

            def full(ins, key):
                ins.then_inc(psum_filled[bank(key)], 1)

            def mm(out_, lhs, rhs, ks, start=True, stop=True):
                ks = list(ks)
                for k in ks:
                    ins = T.matmul(out_, lhs(k), rhs(k), start=start and k == ks[0], stop=stop and k == ks[-1])
                return ins

            def tok(t):
                return slice(t * P, (t + 1) * P)

            def xT(s):
                a, c = room((f"xT{s}", 0)), room((f"xT{s}", 1))
                for t in range(NT):
                    pe.wait_ge(xn_ready, NT * LN_INDEX[s] + t + 1)
                    for h, o in enumerate((a, c)):
                        ins = T.transpose(o[:, tok(t)], xn[:, t, h * P:(h + 1) * P], ident)
                        if t == NT - 1:
                            full(ins, (f"xT{s}", h))

            def transposed(name, src):
                for h in range(2):
                    o = room((name, h))
                    for t in range(NT):
                        ins = T.transpose(o[:, tok(t)], src(t, h), ident)
                    full(ins, (name, h))

            def token_major(key_of, act_T, w, n=D):
                for i in range(2):
                    o = room(key_of(i))
                    for t in (2 * i, 2 * i + 1):
                        ins = mm(o[:, (t % 2) * D:(t % 2) * D + n], lambda k: act_T[:, k, tok(t)],
                                 lambda k: w[:, k, 0:n], range(2))
                    full(ins, key_of(i))

            def chan_major(key, w, c, act_T):
                full(mm(room(key), lambda k: w[:, k, c:c + P], lambda k: act_T[:, k, :], range(2)), key)

            with pe.Fori(0, NB) as b:
                pe.wait_ge(w_loaded[0], 16)
                pe.wait_ge(ctx_loaded, 64)
                for g in range(NG):
                    chan_major(("K", g), W("wk"), g * P, ctxT)
                    in_sbuf(pe, ("K", g))
                    full(T.matmul(room(("F", g)), K("fold"), Kr[:, g, :], start=True, stop=True), ("F", g))
                token_major(lambda i: ("V", i), ctxT, W("wv"))
                full(mm(room("Vg")[:, 0:D],
                        lambda k: ctx0[:, k, :],
                        lambda k: W("wv")[:, k, :], range(2)), "Vg")
                xT(0)
                in_sbuf(pe, ("xT0", 0))
                in_sbuf(pe, ("xT0", 1))
                for g in range(NG):
                    chan_major(("Q", g), W("wq"), g * P, xnT)
                for key in [("F", g) for g in range(NG)] + [("Q", g) for g in range(NG)] + [("V", 0), ("V", 1), "Vg"]:
                    in_sbuf(pe, key)

                def scores(u):
                    qt, g = divmod(u, NG)
                    outs = [room(("S", u, j)) for j in range(HG)]
                    for j, o in enumerate(outs):
                        r = slice(32 * j, 32 * j + 32)
                        q = Qr[r, g, tok(qt)]
                        k0 = max(0, qt - 1) * P
                        w = min(WIN[qt], 256) if qt else S
                        ins = T.matmul(o[:, 0:w], q, Kf[r, g, k0:k0 + w], start=True, stop=False)
                        if qt >= 2:
                            T.matmul(o[:, 256:288], q, Kf[r, g, 0:32], start=False, stop=False)
                    for j, o in enumerate(outs):
                        full(T.matmul(o[:, 0:WIN[qt]], identb, KB("mask0")[:, WOFF[qt]:WOFF[qt] + WIN[qt]],
                                      start=False, stop=True), ("S", u, j))

                def prob_T(n):
                    u, heads = PT_TILES[n]
                    qt = u // NG
                    o = room(("PT", n))
                    if heads is None:
                        pe.wait_ge(global_ready, u - 2 * NG + 1)
                        ins = T.transpose(o[:, 0:P], probs[:, u % 2, 0, 384:512], ident)
                    else:
                        blocks = NT if qt == 0 else 2
                        for i, j in enumerate(heads):
                            for c in range(blocks):
                                ins = T.transpose(o[:, (i * blocks + c) * P:(i * blocks + c + 1) * P],
                                                  probs[:, u % 2, j, tok(c)], ident)
                    full(ins, ("PT", n))

                def prob_V(n):
                    u, heads = PT_TILES[n]
                    qt, g = divmod(u, NG)
                    if ("O", qt) in PLAN and g == 0 and (n == 0 or PT_TILES[n - 1][0] != u):
                        room(("O", qt))
                    o = psb(("O", qt))
                    in_sbuf(pe, ("PT", n))
                    pt = PTs[:, n % 3, :]
                    if heads is None:
                        T.matmul(o[:, g * 64:(g + 1) * 64], pt[:, 0:P], Vg[:, g * 64:(g + 1) * 64],
                                 start=True, stop=False)
                        return
                    blocks = NT if qt == 0 else 2
                    for i, j in enumerate(heads):
                        h = g * HG + j
                        for c in range(blocks):
                            ins = T.matmul(o[:, h * DK:(h + 1) * DK],
                                           pt[:, (i * blocks + c) * P:(i * blocks + c + 1) * P],
                                           V0[:, (max(0, qt - 1) if qt else 0) + c, h * DK:(h + 1) * DK],
                                           start=(qt < 2 and c == 0),
                                           stop=(c == blocks - 1 and (qt < 2 or j == HG - 1)))
                    if g == NG - 1 and heads[-1] == HG - 1:
                        full(ins, ("O", qt))

                scores(0)
                for n, (u, heads) in enumerate(PT_TILES):
                    if n == 0 or PT_TILES[n - 1][0] != u:
                        if u + 1 < NT * NG:
                            scores(u + 1)
                        for j in range(HG):
                            in_sbuf(pe, ("S", u, j))
                    prob_T(n)
                    if n >= 2:
                        prob_V(n - 2)
                prob_V(len(PT_TILES) - 2)
                prob_V(len(PT_TILES) - 1)
                in_sbuf(pe, ("O", NT - 1))
                transposed("OT", lambda t, h: Ot[:, t, h * P:(h + 1) * P])
                in_sbuf(pe, ("OT", 0))
                in_sbuf(pe, ("OT", 1))
                token_major(lambda i: ("Y0", i), OT, W("wo"))

                pe.wait_ge(w_loaded[1], 16)
                pe.wait_ge(scol_ready, 1)
                o = room("R")
                for t in range(NT):
                    ins = T.transpose(o[:, tok(t)], scol[:, t:t + 1].broadcast_to([P, P]), ident)
                full(ins, "R")
                pe.wait_ge(xr_ready, NT)
                transposed("xT1", lambda t, h: xn[:, t, h * P:(h + 1) * P])
                in_sbuf(pe, ("xT1", 0))
                in_sbuf(pe, ("xT1", 1))
                chan_major(("h", "light"), W("lw1"), 0, xlT)

                def heavy_w(m):
                    c = stream[:, m // 4, :]
                    return c[:, 0:1024].rearrange("p (k n) -> p k n", k=2), c[:, 1024:2048].rearrange("p (m n) -> p m n", m=4)

                def branches():
                    for m in range(8):
                        pe.wait_ge(chunk_loaded[m // 4], 16)
                        o = room(("h", m))
                        for k in range(2):
                            ins = T.matmul(o, heavy_w(m)[0][:, k, (m % 4) * P:(m % 4 + 1) * P], xhT[:, k, :],
                                           start=(k == 0), stop=(k == 1))
                            if k == 1:
                                full(ins, ("h", m))
                            yield
                    in_sbuf(pe, ("h", "light"))
                    for i in range(2):
                        o = room(("yl", i))
                        for t in (2 * i, 2 * i + 1):
                            ins = T.matmul(o[:, (t % 2) * D:(t % 2 + 1) * D], hL[:, tok(t)], W("lw2", 1)[:, 0, :],
                                           start=True, stop=True)
                            if t % 2:
                                full(ins, ("yl", i))
                            yield
                    for m in range(8):
                        in_sbuf(pe, ("h", m))
                    for i in range(2):
                        o = room(("yh", i))
                        for t in (2 * i, 2 * i + 1):
                            for m in range(8):
                                ins = T.matmul(o[:, (t % 2) * D:(t % 2 + 1) * D], hH[:, m, tok(t)],
                                               heavy_w(m)[1][:, m % 4, :], start=(m == 0), stop=(m == 7))
                                if t % 2 and m == 7:
                                    full(ins, ("yh", i))
                                yield

                work = branches()
                room("chain")
                done = 0
                share = (8, 8, 20, 16)
                for r in range(ROUNDS):
                    for i in range(ITERS):
                        n = r * ITERS + i
                        pe.wait_ge(rowsum_ready, n + 1)
                        ins = T.matmul(psb("chain")[:, n:n + 1], onesk[:, :], rs[:, n % 2:n % 2 + 1],
                                       start=True, stop=True)
                        if n == ROUNDS * ITERS - 1:
                            full(ins, "chain")
                        else:
                            ins.then_inc(total_ready, 1)
                        for _ in range((i + 1) * share[r] // ITERS - i * share[r] // ITERS):
                            next(work)
                for _ in work:
                    raise AssertionError

                pe.wait_ge(w_loaded[2], 16)
                xT_key = 2
                for h in range(2):
                    chan_major(("KT1", h), W("wred"), h * P, ctxT)
                xT(2)
                for key in (("xT2", 0), ("xT2", 1), ("KT1", 0), ("KT1", 1)):
                    in_sbuf(pe, key)
                pe.wait_ge(keypad_ready, 2)
                for t in range(NT):
                    o = room(("S1", t))[:, 0:KEYW]
                    mm(o, lambda k: xnT[:, k, tok(t)], lambda k: kr1[:, k, t * P:t * P + KEYW], range(2), stop=False)
                    full(T.matmul(o, identb, KB("band")[:, t * KEYW:(t + 1) * KEYW], start=False, stop=True), ("S1", t))
                for t in range(NT):
                    in_sbuf(pe, ("S1", t))
                    o = room(("PT1", t))
                    T.transpose(o[:, 0:P], P1[:, t, 0:P], ident)
                    full(T.transpose(o[0:64, P:2 * P], P1[:, t, P:KEYW], ident), ("PT1", t))
                for i in range(2):
                    o = room(("O1", i))
                    for t in (2 * i, 2 * i + 1):
                        in_sbuf(pe, ("PT1", t))
                        T.matmul(o[:, (t % 2) * D:(t % 2 + 1) * D], PT1[:, t, 0:P], ctxs[:, t, :], start=True, stop=False)
                        ins = T.matmul(o[:, (t % 2) * D:(t % 2 + 1) * D], PT1[0:64, t, P:2 * P], ctxs[0:64, t + 1, :],
                                       start=False, stop=True)
                    full(ins, ("O1", i))

                def router(s, w):
                    key = f"RT{s}"
                    o = room(key)
                    for t in range(NT):
                        ins = mm(o[:, t * 8:t * 8 + 8], lambda k: xnT[:, k, tok(t)], lambda k: w[:, k, :], range(2))
                    full(ins, key)

                xT(3)
                in_sbuf(pe, ("xT3", 0))
                in_sbuf(pe, ("xT3", 1))
                router(3, W("l1r"))

                def down3(e):
                    in_sbuf(pe, ("U3", e))
                    for i in range(2):
                        o = room(("Y3", e, i))
                        for t in (2 * i, 2 * i + 1):
                            ins = T.matmul(o[:, (t % 2) * D:(t % 2 + 1) * D], hid3[:, e % 2, tok(t)],
                                           W("l1d", 4)[:, e, :], start=True, stop=True)
                        full(ins, ("Y3", e, i))

                for e in range(4):
                    chan_major(("G3", e), W("l1g", 8)[:, 2 * e:2 * e + 2, :], 0, xnT)
                    chan_major(("U3", e), W("l1u", 8)[:, 2 * e:2 * e + 2, :], 0, xnT)
                    if e == 0:
                        pe.wait_ge(conv_ready, 1)
                        for i in range(2):
                            o = room(("CT3", i))
                            for t in (2 * i, 2 * i + 1):
                                for h in range(2):
                                    ins = T.transpose(o[:, (t % 2) * D + h * P:(t % 2) * D + (h + 1) * P],
                                                      conv[:, h, tok(t)], ident)
                            full(ins, ("CT3", i))
                    else:
                        down3(e - 1)
                down3(3)

                pe.wait_ge(w_loaded[3], 16)
                token_major(lambda i: ("k4", i), ctxT, W("w2k"))
                token_major(lambda i: ("v4", i), ctxT, W("w2v"))
                xT(4)
                in_sbuf(pe, ("xT4", 0))
                in_sbuf(pe, ("xT4", 1))
                token_major(lambda i: ("q4", i), xnT, W("w2q"))
                pe.wait_ge(sparse_ready, 1)
                pe.wait_ge(ones_ready, 2)
                in_sbuf(pe, ("v4", 0))
                in_sbuf(pe, ("v4", 1))
                for c in range(2):
                    o = room(("KV4", c))
                    for t in range(NT):
                        ins = T.matmul(o[:, 0:129], ym[:, 0, t, c * P:(c + 1) * P], V2[:, t, c, 0:129],
                                       start=(t == 0), stop=(t == NT - 1))
                    full(ins, ("KV4", c))
                pe.wait_ge(sparse_ready, 2)
                transposed("QT4", lambda t, h: ym[:, 1, t, h * P:(h + 1) * P])
                for key in (("KV4", 0), ("KV4", 1), ("QT4", 0), ("QT4", 1)):
                    in_sbuf(pe, key)
                for t in range(NT):
                    o = room(("y4", t))
                    for c in range(2):
                        ins = T.matmul(o[:, c * 136:(c + 1) * 136], qsT[:, c, tok(t)], kvm[:, c, :], start=True, stop=True)
                    full(ins, ("y4", t))
                for t in (2, 3):
                    in_sbuf(pe, ("y4", t))
                transposed("yT4", lambda t, h: y4[:, t, h * P:(h + 1) * P])
                in_sbuf(pe, ("yT4", 0))
                in_sbuf(pe, ("yT4", 1))
                token_major(lambda i: ("O4", i), yT4, W("w2p"))

                xT(5)
                in_sbuf(pe, ("xT5", 0))
                in_sbuf(pe, ("xT5", 1))
                router(5, W("l2r"))

                def expert_w(e, part):
                    return stream[:, e % 2, part * 512:(part + 1) * 512].rearrange("p (k n) -> p k n", k=2)

                def down5(e):
                    for f in range(2):
                        in_sbuf(pe, ("U5", e, f))
                    for i in range(2):
                        o = room(("Y5", e, i))
                        for t in (2 * i, 2 * i + 1):
                            ins = mm(o[:, (t % 2) * D:(t % 2 + 1) * D], lambda f: hid5[:, e % 2, f, tok(t)],
                                     lambda f: expert_w(e, 2)[:, f, :], range(2))
                            if t == NT - 1:
                                full(ins, ("Y5", e, i))
                        if i == 0:
                            full(ins, ("Y5", e, i))

                for e in range(10):
                    pe.wait_ge(chunk_loaded[e % 2], 16 * (e // 2 + 2))
                    for f in range(2):
                        chan_major(("G5", e, f), expert_w(e, 0), f * P, xnT)
                        chan_major(("U5", e, f), expert_w(e, 1), f * P, xnT)
                    if e:
                        down5(e - 1)
                down5(9)

                pe.wait_ge(w_loaded[4], 16)
                for h in range(2):
                    chan_major(("K6", 1, h), W("k2"), h * P, ctxT)
                token_major(lambda i: ("V6", 1, i), ctxT, W("v2"))
                xT(6)
                in_sbuf(pe, ("xT6", 0))
                in_sbuf(pe, ("xT6", 1))
                for h in range(2):
                    chan_major(("K6", 0, h), W("k1"), h * P, xnT)
                    chan_major(("Q6", 0, h), W("q1"), h * P, xnT)
                token_major(lambda i: ("V6", 0, i), xnT, W("v1"))
                for a in range(2):
                    for h in range(2):
                        in_sbuf(pe, ("K6", a, h))
                        in_sbuf(pe, ("Q6", a, h))
                    for t in range(NT):
                        n = (t + 1) * P if a == 0 else S
                        o = room(("S6", a, t))
                        ins = mm(o[:, 0:n], lambda k: Q6[:, k, tok(t)], lambda k: K6[a][:, k, 0:n], range(2), stop=(a == 1))
                        if a == 0:
                            ins = T.matmul(o[:, tok(t)], identb, KB("causal"), start=False, stop=True)
                        full(ins, ("S6", a, t))
                    for i in range(2):
                        in_sbuf(pe, ("V6", a, i))
                    for t in range(NT):
                        nb = t + 1 if a == 0 else NT
                        in_sbuf(pe, ("S6", a, t))
                        p = room(("P6", a, t))
                        for c in range(nb):
                            ins = T.transpose(p[:, tok(c)], P6[:, t, tok(c)], ident)
                        full(ins, ("P6", a, t))
                        if t % 2 == 0:
                            o = room(("O6", a, t // 2))
                        in_sbuf(pe, ("P6", a, t))
                        ins = mm(o[:, (t % 2) * D:(t % 2 + 1) * D], lambda c: PT6[:, t % 2, tok(c)],
                                 lambda c: V6[a][:, c, :], range(nb))
                        if t % 2:
                            full(ins, ("O6", a, t // 2))
                    if a == 0:
                        in_sbuf(pe, ("O6", 0, 0))
                        in_sbuf(pe, ("O6", 0, 1))
                        transposed("aT6", lambda t, h: att[:, t, h * P:(h + 1) * P])
                        in_sbuf(pe, ("aT6", 0))
                        in_sbuf(pe, ("aT6", 1))
                        for h in range(2):
                            chan_major(("Q6", 1, h), W("q2"), h * P, attT)
                pe.wait_ge(affine_ready, 2)
                transposed("nT6", lambda t, h: n2[:, t, h * P:(h + 1) * P])
                in_sbuf(pe, ("nT6", 0))
                in_sbuf(pe, ("nT6", 1))
                for m in range(2):
                    chan_major(("h6", m), W("f1"), m * P, attT)
                pe.wait_ge(h6_ready, 2)
                token_major(lambda i: ("f6", i), h6, W("f2"))

                pe.wait_ge(setup_done, 2)
                xT(7)
                in_sbuf(pe, ("xT7", 0))
                in_sbuf(pe, ("xT7", 1))
                for m in range(6):
                    chan_major(("G7", m), v3(wl3[:, 0:1536], 2), m * P, xnT)
                    chan_major(("U7", m), v3(wl3[:, 1536:3072], 2), m * P, xnT)
                for m in range(6):
                    in_sbuf(pe, ("U7", m))
                for i in range(2):
                    o = room(("Y7", i))
                    for t in (2 * i, 2 * i + 1):
                        ins = mm(o[:, (t % 2) * D:(t % 2 + 1) * D], lambda m: hid7[:, m, tok(t)],
                                 lambda m: v3(wl3[:, 3072:4608], 6)[:, m, :], range(6))
                    full(ins, ("Y7", i))
                meet(pe, b)

        @block.scalar
        def _(act):
            A = nc.scalar.activation
            act.wait_ge(setup_done, 1)
            act.wait_ge(const_loaded, 64)

            def taken(ins, key):
                ins.then_inc(psum_taken[bank(key)], 1)

            def copy(key, dst, src=None):
                o = got(act, key)
                taken(A(dst, o if src is None else src(o), ACT.Copy), key)

            with act.Fori(0, NB) as b:
                n_step = [0]

                def link(ins):
                    n_step[0] += 1
                    ins.then_inc(act_step, 1)
                    act.wait_ge(act_step, n_step[0])

                for g in range(NG):
                    copy(("F", g), Kf[:, g, :])
                copy(("xT0", 0), xnT[:, 0, :])
                for u in range(NT * NG):
                    qt, g = divmod(u, NG)
                    act.wait_ge(max_ready, u + 1)
                    for j in range(HG):
                        h = g * HG + j
                        taken(A(probs[:, u % 2, j, 0:WIN[qt]], psb(("S", u, j))[:, 0:WIN[qt]], ACT.Exp,
                                bias=nm[:, u % 2, j:j + 1], accum_out=den[:, qt, h:h + 1]), ("S", u, j))
                copy(("OT", 0), OT[:, 0, :])

                for t in range(NT):
                    act.wait_ge(xn_ready, NT + t + 1)
                    ins = A(hL[:, 0:D], xn[:, t, :], ACT.Square, accum_out=ss[:, t:t + 1])
                    if t < NT - 1:
                        link(ins)
                ins.then_inc(rms_sum, 1)
                act.wait_ge(rms_sum, 1)
                o = got(act, ("xT1", 0))
                A(xlT[:, 0, :], o, ACT.Copy, scale=col("lgam", 0))
                taken(A(xhT[:, 0, :], o, ACT.Copy, scale=col("hgam", 0)), ("xT1", 0))

                def gelu(key, dst, bias):
                    o = got(act, key)
                    taken(A(dst, o, ACT.Gelu, bias=bias), key)

                gelu(("h", "light"), hL, col("lb1"))
                act.wait_ge(lse_max, 1)
                link(A(hH[:, 7, :], krow, ACT.Exp, bias=nmax, accum_out=lsum))
                A(lnv, lsum, ACT.Ln, scale=1.0 / K_EFF).then_inc(ln_ready, 1)
                for r in range(ROUNDS):
                    act.wait_ge(ce_ready, r + 1)
                    A(ev, ce, ACT.Exp).then_inc(ev_ready, 1)
                    if r < 2:
                        for m in range(4 * r, 4 * r + 4):
                            gelu(("h", m), hH[:, m, :], col("hb1", m))
                    n = ITERS * (r + 1) - 1
                    if r == ROUNDS - 1:
                        got(act, "chain")
                        taken(A(lnv, psb("chain")[:, n:n + 1], ACT.Ln, scale=22026.465794806718), "chain")
                    else:
                        act.wait_ge(total_ready, n + 1)
                        A(lnv, psb("chain")[:, n:n + 1], ACT.Ln, scale=22026.465794806718).then_inc(ln_ready, 1)
                act.wait_ge(kcol_ready, 1)
                A(score, kcol, ACT.Exp).then_inc(score_ready, 1)

                for h in range(2):
                    o = got(act, ("KT1", h))
                    taken(A(kr1[:, h, 32:32 + S], o, ACT.Identity, bias=col("bred", h)), ("KT1", h))
                copy(("xT2", 0), xnT[:, 0, :])
                for t in range(NT):
                    act.wait_ge(max1_ready, t + 1)
                    taken(A(P1[:, t, :], psb(("S1", t))[:, 0:KEYW], ACT.Exp, bias=nm4[:, t:t + 1],
                            accum_out=den4[:, t:t + 1]), ("S1", t))

                copy(("xT3", 0), xnT[:, 0, :])
                o = got(act, "RT3")
                taken(A(sc.rearrange("p t e -> p (t e)"), o[:, 0:32], ACT.Sigmoid), "RT3")
                for e in range(4):
                    o = got(act, ("G3", e))
                    if e >= 2:
                        in_sbuf(act, ("U3", e - 2))
                    taken(A(sg3[:, e % 2, :], o, ACT.Silu), ("G3", e))

                def focus_abs(w):
                    for i in range(2):
                        o = got(act, (w, i))
                        A(fa[:, 2 * i:2 * i + 2, :].rearrange("p t d -> p (t d)"), o, ACT.Abs, scale=0.01).then_inc(abs_ready, 1)

                def focus_rest(w, i):
                    in_sbuf(act, (w, 0))
                    in_sbuf(act, (w, 1))
                    A(fa, fb, ACT.Ln, bias=eps6).then_inc(log_ready, 1)
                    act.wait_ge(focus_in, i + 1)
                    for t in range(NT):
                        A(fb[:, t, :], fa[:, t, :], ACT.Exp, bias=fmax[:, t:t + 1],
                          accum_out=psumm[:, t:t + 1]).then_inc(focus_exp, 1)

                focus_abs("k4")
                for i in range(2):
                    copy(("v4", i), V2[:, 2 * i:2 * i + 2, :, 0:P],
                         lambda o: o.rearrange("p (t c n) -> p t c n", t=2, c=2))
                copy(("xT4", 0), xnT[:, 0, :])
                focus_rest("k4", 0)
                act.wait_ge(sparse_ready, 1)
                focus_abs("q4")
                focus_rest("q4", 1)
                copy(("QT4", 0), qsT[:, 0, :])
                copy(("QT4", 1), qsT[:, 1, :])
                copy(("yT4", 0), yT4[:, 0, :])
                copy(("yT4", 1), yT4[:, 1, :])

                copy(("xT5", 0), xnT[:, 0, :])
                in_sbuf(act, "RT5")
                A(sc.rearrange("p t e -> p (t e)"), sc.rearrange("p t e -> p (t e)"), ACT.Exp).then_inc(router_exp, 1)
                for e in range(10):
                    for f in range(2):
                        o = got(act, ("G5", e, f))
                        if e:
                            in_sbuf(act, ("U5", e - 1, f))
                        taken(A(sg5[:, f, :], o, ACT.Silu), ("G5", e, f))

                for h in range(2):
                    copy(("K6", 1, h), K6[1][:, h, :])
                for i in range(2):
                    copy(("V6", 1, i), V6[1][:, 2 * i:2 * i + 2, :].rearrange("p t d -> p (t d)"))
                copy(("xT6", 0), xnT[:, 0, :])
                scale = float(S) ** -0.5

                def q_scaled(a, h):
                    o = got(act, ("Q6", a, h))
                    taken(A(Q6[:, h, :], o, ACT.Copy, scale=scale), ("Q6", a, h))

                for h in range(2):
                    copy(("K6", 0, h), K6[0][:, h, :])
                    q_scaled(0, h)
                for i in range(2):
                    copy(("V6", 0, i), V6[0][:, 2 * i:2 * i + 2, :].rearrange("p t d -> p (t d)"))
                for a in range(2):
                    for t in range(NT):
                        n = (t + 1) * P if a == 0 else S
                        act.wait_ge(max6_ready, NT * a + t + 1)
                        taken(A(P6[:, t, 0:n], psb(("S6", a, t))[:, 0:n], ACT.Exp, bias=nm4[:, t:t + 1],
                                accum_out=den4[:, t:t + 1]), ("S6", a, t))
                    if a == 0:
                        copy(("aT6", 0), attT[:, 0, :])
                        copy(("aT6", 1), attT[:, 1, :])
                        for h in range(2):
                            q_scaled(1, h)
                copy(("nT6", 0), attT[:, 0, :])
                copy(("nT6", 1), attT[:, 1, :])
                for m in range(2):
                    o = got(act, ("h6", m))
                    taken(A(v6[:, m, :], o, ACT.Identity, bias=col("b1", m)), ("h6", m))

                copy(("xT7", 0), xnT[:, 0, :])
                for m in range(6):
                    o = got(act, ("G7", m))
                    if m >= 2:
                        in_sbuf(act, ("U7", m - 2))
                    taken(A(sg7[:, m % 2, :], o, ACT.Silu), ("G7", m))
                meet(act, b)

        @block.vector
        def _(dve):
            V = nc.vector
            dve.wait_ge(setup_done, 1)
            dve.wait_ge(const_loaded, 64)

            def taken(ins, key):
                ins.then_inc(psum_taken[bank(key)], 1)

            with dve.Fori(0, NB) as b:
                n_step = [0]

                def link(ins):
                    n_step[0] += 1
                    ins.then_inc(dve_step, 1)
                    dve.wait_ge(dve_step, n_step[0])

                def flat(ap):
                    return ap.rearrange("p t d -> p (t d)")

                def two(o):
                    return o.rearrange("p (t d) -> p t d", t=2)

                def copy(key, dst):
                    taken(V.tensor_copy(dst, got(dve, key)), key)

                def norm(s, src, dst):
                    idx = LN_INDEX[s]
                    for t in range(NT):
                        link(V.bn_stats(stats[:, t, :], src[:, t, :]))
                    for t in range(NT):
                        ins = V.bn_aggr(mv[:, t, :], stats[:, t, :])
                    ins.then_inc(ln_stats, 1)
                    dve.wait_ge(ln_rstd, idx + 1)
                    for t in range(NT):
                        V.tensor_scalar(dst[:, t, :], src[:, t, :], mv[:, t, 0:1], rstd[:, t:t + 1],
                                        ALU.subtract, ALU.mult).then_inc(xn_ready, 1)

                for g in range(NG):
                    o = got(dve, ("K", g))
                    taken(V.scalar_tensor_tensor(Kr[:, g, :], o, col("bk", g), K("rope"), ALU.add, ALU.mult), ("K", g))
                for i in range(2):
                    o = got(dve, ("V", i))
                    taken(V.tensor_tensor(V0[:, 2 * i:2 * i + 2, :], two(o), row("bv", 2), ALU.add), ("V", i))
                o = got(dve, "Vg")
                link(V.tensor_tensor(Vg, o[:, 0:D], row("bv"), ALU.add))
                taken(V.tensor_tensor(Vg, Vg, K("gmask"), ALU.mult), "Vg")
                dve.wait_ge(x_loaded, 16)
                norm(0, x, xn)
                copy(("xT0", 1), xnT[:, 1, :])
                for g in range(NG):
                    o = got(dve, ("Q", g))
                    taken(V.scalar_tensor_tensor(Qr[:, g, :], o, col("bq", g), K("rope"), ALU.add, ALU.mult), ("Q", g))

                def row_max(u):
                    for j in range(HG):
                        got(dve, ("S", u, j))
                    V.reduce_max(nm[:, u % 2, :], ps[:, 0:HG, 0:WIN[u // NG]], AX_X, negate=True).then_inc(max_ready, 1)

                row_max(0)
                for n, (u, heads) in enumerate(PT_TILES):
                    qt = u // NG
                    if (n == 0 or PT_TILES[n - 1][0] != u) and u + 1 < NT * NG:
                        row_max(u + 1)
                    w = P if heads is None else S
                    o = got(dve, ("PT", n))
                    taken(V.tensor_copy(PTs[:, n % 3, 0:w], o[:, 0:w]), ("PT", n))
                    if n >= 2:
                        out_tile(dve, V, got, taken, link, n - 2, rden, den, Ot)
                out_tile(dve, V, got, taken, link, len(PT_TILES) - 2, rden, den, Ot)
                out_tile(dve, V, got, taken, link, len(PT_TILES) - 1, rden, den, Ot)
                copy(("OT", 1), OT[:, 1, :])
                dve.wait_ge(x_biased, 1)

                def add_to_x(name):
                    for i in range(2):
                        o = got(dve, (name, i))
                        xs = flat(x[:, 2 * i:2 * i + 2, :])
                        taken(V.tensor_tensor(xs, xs, o, ALU.add), (name, i))
                    in_sbuf(dve, (name, 0))
                    in_sbuf(dve, (name, 1))

                add_to_x("Y0")

                norm(1, x, xn)
                for t in range(NT):
                    dve.wait_ge(xn_ready, NT + t + 1)
                    ins = V.tensor_tensor_reduce(out=hH[:, 0, 0:D], in0=xn[:, t, :], in1=row("rt"), scale=1.0,
                                                 scalar=0.0, op0=ALU.mult, op1=ALU.add, accum_out=scol[:, t:t + 1])
                    if t < NT - 1:
                        link(ins)
                ins.then_inc(scol_ready, 1)
                dve.wait_ge(scol_ready, 1)
                dve.wait_ge(rms_ready, 1)
                for t in range(NT):
                    V.tensor_scalar(xn[:, t, :], xn[:, t, :], rmsr[:, t:t + 1], None, ALU.mult).then_inc(xr_ready, 1)
                copy("R", srow)
                o = got(dve, ("xT1", 1))
                V.tensor_scalar(xlT[:, 1, :], o, col("lgam", 1), None, ALU.mult)
                taken(V.tensor_scalar(xhT[:, 1, :], o, col("hgam", 1), None, ALU.mult), ("xT1", 1))
                got(dve, ("h", "light"))
                in_sbuf(dve, "R")
                link(V.tensor_scalar(krow, srow, LOG_N_K, None, ALU.min))
                V.reduce_max(nmax, krow, AX_X, negate=True).then_inc(lse_max, 1)
                dve.wait_ge(lse_max, 1)
                dve.wait_ge(ln_ready, 1)
                link(V.scalar_tensor_tensor(lsh[:, 0:1], lnv, -SHIFT, nmax, ALU.add, ALU.subtract))
                for r in range(ROUNDS):
                    V.tensor_scalar(ce, scol, lsh[:, r % 2:r % 2 + 1], 60.0, ALU.subtract, ALU.min).then_inc(ce_ready, 1)
                    dve.wait_ge(ev_ready, r + 1)
                    for i in range(ITERS):
                        n = r * ITERS + i
                        if i == 0:
                            level = EXP_SHIFT
                        else:
                            dve.wait_ge(total_ready, n)
                            level = psb("chain")[:, n - 1:n]
                        V.tensor_scalar(jc, ev, level, 0.0, ALU.min, ALU.add,
                                        accum_out=rs[:, n % 2:n % 2 + 1]).then_inc(rowsum_ready, 1)
                        dve.wait_ge(rowsum_ready, n + 1)
                    if r == ROUNDS - 1:
                        in_sbuf(dve, "chain")
                    else:
                        dve.wait_ge(ln_ready, r + 2)
                    link(V.scalar_tensor_tensor(lsh[:, (r + 1) % 2:(r + 1) % 2 + 1], lnv, -(SHIFT + 10.0),
                                                lsh[:, r % 2:r % 2 + 1], ALU.add, ALU.add))
                link(V.tensor_scalar(lfin, lsh[:, 0:1], SHIFT, None, ALU.add))
                link(V.tensor_scalar(krow, srow, lfin, 0.0, ALU.subtract, ALU.min))
                link(V.tensor_scalar(krow, krow, -103.97, None, ALU.max))
                link(V.tensor_scalar(kcol, scol, lfin, 0.0, ALU.subtract, ALU.min))
                V.tensor_scalar(kcol, kcol, -103.97, None, ALU.max).then_inc(kcol_ready, 1)
                dve.wait_ge(kcol_ready, 1)
                for t in range(NT):
                    w = (NT - 1 - t) * P
                    link(V.scalar_tensor_tensor(jrow, krow, kcol[:, t:t + 1], KB("lt")[:, w:w + S], ALU.is_ge, ALU.mult,
                                                accum_out=rk1[:, t:t + 1]))
                    link(V.scalar_tensor_tensor(jrow, krow, kcol[:, t:t + 1], KB("ge")[:, w:w + S], ALU.is_gt, ALU.mult,
                                                accum_out=rk2[:, t:t + 1]))
                link(V.tensor_tensor(rk1, rk1, rk2, ALU.add))
                link(V.tensor_scalar(rk1, rk1, float(TOP_HEAVY), None, ALU.is_lt))
                dve.wait_ge(score_ready, 1)
                link(V.tensor_scalar(wgt, score, -1.0, 1.0, ALU.mult, ALU.add))
                link(V.tensor_tensor(wgt, wgt, score, ALU.add))
                link(V.tensor_tensor(wgt, wgt, rk1, ALU.mult))
                dve.wait_ge(x_biased, 2)
                add_to_x("yl")
                for i in range(2):
                    o = two(got(dve, ("yh", i)))
                    for t in (2 * i, 2 * i + 1):
                        link(V.tensor_tensor(th, o[:, t % 2, :], row("hb2"), ALU.add))
                        ins = V.scalar_tensor_tensor(x[:, t, :], th, wgt[:, t:t + 1], x[:, t, :], ALU.mult, ALU.add)
                        if t % 2:
                            taken(ins, ("yh", i))
                        else:
                            link(ins)
                    in_sbuf(dve, ("yh", i))

                norm(2, x, xn)
                copy(("xT2", 1), xnT[:, 1, :])
                for t in range(NT):
                    o = got(dve, ("S1", t))
                    V.reduce_max(nm4[:, t:t + 1], o[:, 0:KEYW], AX_X, negate=True).then_inc(max1_ready, 1)
                for t in range(NT):
                    o = got(dve, ("PT1", t))
                    V.tensor_copy(PT1[:, t, 0:P], o[:, 0:P])
                    taken(V.tensor_copy(PT1[0:64, t, P:2 * P], o[0:64, P:2 * P]), ("PT1", t))

                def weighted(key_of, scalar, dst=x):
                    for i in range(2):
                        o = two(got(dve, key_of(i)))
                        for t in (2 * i, 2 * i + 1):
                            ins = V.scalar_tensor_tensor(dst[:, t, :], o[:, t % 2, :], scalar(t), dst[:, t, :],
                                                         ALU.mult, ALU.add)
                        taken(ins, key_of(i))
                    in_sbuf(dve, key_of(1))

                link(V.reciprocal(rden4, den4))
                weighted(lambda i: ("O1", i), lambda t: rden4[:, t:t + 1])
                in_sbuf(dve, ("O1", 0))

                norm(3, x, xn)
                copy(("xT3", 1), xnT[:, 1, :])
                in_sbuf(dve, ("xT3", 0))
                in_sbuf(dve, ("xT3", 1))
                in_sbuf(dve, "RT3")

                def top2():
                    for t in range(NT):
                        ins = V.max(t8[:, t, :], tb[:, t, 0:8])
                    link(ins)
                    link(V.memset(t8[:, :, 2:8], BIG))
                    for t in range(NT):
                        ins = V.match_replace(tr[:, t, 0:14], t8[:, t, :], tb[:, t, 0:14], -BIG)
                    link(ins)
                    link(V.tensor_scalar(tr[:, :, 0:8], tr[:, :, 0:8], -2.9e38, None, ALU.is_le))
                    link(V.tensor_tensor(cw[:, :, 0:8], tr[:, :, 0:8], sc, ALU.mult))

                link(V.tensor_tensor(tb[:, :, 0:8], sc, row("rbias", NT), ALU.add))
                top2()
                link(V.reduce_sum(c46, cw[:, :, 0:8], AX_X))
                link(V.tensor_scalar(c46, c46, 1e-9, None, ALU.add))
                link(V.reciprocal(c46, c46))
                V.tensor_tensor(cw[:, :, 0:8], cw[:, :, 0:8], c46.unsqueeze(2).broadcast_to([P, NT, 8]), ALU.mult).then_inc(cw_ready, 1)
                dve.wait_ge(cw_ready, 1)
                for h in range(2):
                    link(V.tensor_scalar(conv[:, h, :], xnT[:, h, :], col("convw", 4 * h + 3), None, ALU.mult))
                    for k in range(1, 4):
                        ins = V.scalar_tensor_tensor(conv[:, h, k:S], xnT[:, h, 0:S - k], col("convw", 4 * h + 3 - k),
                                                     conv[:, h, k:S], ALU.mult, ALU.add)
                        if h == 1 and k == 3:
                            ins.then_inc(conv_ready, 1)
                        else:
                            link(ins)

                def gated(gkey, ukey, sg, dst):
                    in_sbuf(dve, gkey)
                    o = got(dve, ukey)
                    taken(V.tensor_tensor(dst, sg, o, ALU.mult), ukey)

                dve.wait_ge(extra_ready, NT)
                for e in range(4):
                    gated(("G3", e), ("U3", e), sg3[:, e % 2, :], hid3[:, e % 2, :])
                    if e == 0:
                        for i in range(2):
                            o = got(dve, ("CT3", i))
                            taken(V.tensor_tensor(flat(x[:, 2 * i:2 * i + 2, :]), flat(extra[:, 2 * i:2 * i + 2, :]), o,
                                                  ALU.add), ("CT3", i))
                            in_sbuf(dve, ("CT3", i))
                    else:
                        weighted(lambda i: ("Y3", e - 1, i), lambda t: cw[:, t, e - 1:e])
                weighted(lambda i: ("Y3", 3, i), lambda t: cw[:, t, 3:4])
                in_sbuf(dve, ("Y3", 3, 0))

                def focus(w, i):
                    for j in range(2):
                        o = two(got(dve, (w, j)))
                        dve.wait_ge(abs_ready, 2 * i + j + 1)
                        for t in (2 * j, 2 * j + 1):
                            ins = V.scalar_tensor_tensor(fb[:, t, :], o[:, t % 2, :], 1.0, fa[:, t, :], ALU.mult, ALU.max,
                                                         accum_out=fsum[:, t:t + 1])
                        taken(ins, (w, j))
                        in_sbuf(dve, (w, j))
                    dve.wait_ge(log_ready, i + 1)
                    link(V.tensor_scalar(fa, fa, col("focus"), None, ALU.mult))
                    V.reduce_max(fmax, fa, AX_X, negate=True).then_inc(focus_in, 1)
                    link(V.tensor_scalar(fsum, fsum, -1.0 / D, -1e-6, ALU.mult, ALU.add))
                    dve.wait_ge(focus_exp, NT * (i + 1))
                    link(V.reciprocal(fco, psumm))
                    link(V.tensor_tensor(fco, fco, fsum, ALU.mult))
                    for t in range(NT):
                        ins = V.tensor_scalar(yin[:, t, :, 0:DK], fb[:, t, :].rearrange("p (h n) -> p h n", h=NH),
                                              fco[:, t:t + 1], None, ALU.mult)
                    link(ins)
                    for t in range(NT):
                        for h in range(NH):
                            ins = V.max(top8[:, t, h, :], yin[:, t, h, 0:DK])
                    link(ins)
                    link(V.memset(top8[:, :, :, 5:8], 1.0))
                    for t in range(NT):
                        for h in range(NH):
                            ins = V.match_replace(yout[:, t, h, :], top8[:, t, h, :], yin[:, t, h, :], 0.0)
                    link(ins)
                    V.tensor_copy(ym[:, i].rearrange("p t (h n) -> p t h n", h=NH),
                                  yout[:, :, :, 0:DK]).then_inc(sparse_ready, 1)
                    dve.wait_ge(sparse_ready, i + 1)

                norm(4, x, xn)
                copy(("xT4", 1), xnT[:, 1, :])
                dve.wait_ge(ones_ready, 2)
                focus("k4", 0)
                focus("q4", 1)
                for c in range(2):
                    o = got(dve, ("KV4", c))
                    bm = K("bmask")
                    V.scalar_tensor_tensor(kvm[:, c, 0:P], o[:, 0:P], 1.0 / S, bm[:, 0:P], ALU.mult, ALU.mult)
                    taken(V.tensor_scalar(kvm[:, c, P:136], bm[:, P:136], o[:, P:P + 1], 1.0 / S, ALU.mult, ALU.mult),
                          ("KV4", c))
                for t in range(NT):
                    o = got(dve, ("y4", t))[:, 0:272].rearrange("p (c n) -> p c n", c=2)
                    link(V.tensor_scalar(zr, o[:, :, P:136], 1e-6, None, ALU.add))
                    link(V.reciprocal(zr, zr))
                    taken(V.tensor_tensor(y4[:, t, :].rearrange("p (c h n) -> p c h n", c=2, h=8),
                                          o[:, :, 0:P].rearrange("p c (h n) -> p c h n", h=8),
                                          zr.unsqueeze(3).broadcast_to([P, 2, 8, DK]), ALU.mult), ("y4", t))
                    in_sbuf(dve, ("y4", t))
                add_to_x("O4")

                norm(5, x, xn)
                copy(("xT5", 1), xnT[:, 1, :])
                o = got(dve, "RT5")[:, 0:32].rearrange("p (t e) -> p t e", t=NT)
                link(V.reduce_max(c46, o, AX_X, negate=True))
                taken(V.tensor_tensor(sc, o, c46.unsqueeze(2).broadcast_to([P, NT, 8]), ALU.add), "RT5")
                in_sbuf(dve, "RT5")
                dve.wait_ge(router_exp, 1)
                link(V.reduce_sum(c46, sc, AX_X))
                link(V.reciprocal(c46, c46))
                link(V.tensor_tensor(sc, sc, c46.unsqueeze(2).broadcast_to([P, NT, 8]), ALU.mult))
                link(V.tensor_copy(tb[:, :, 0:8], sc))
                top2()
                for e in range(10):
                    for f in range(2):
                        gated(("G5", e, f), ("U5", e, f), sg5[:, f, :], hid5[:, e % 2, f, :])
                    if e:
                        weighted(lambda i: ("Y5", e - 1, i), lambda t: cw[:, t, e - 1:e])
                weighted(lambda i: ("Y5", 9, i), lambda t: cw[:, t, 9:10])
                in_sbuf(dve, ("Y5", 9, 0))

                norm(6, x, xn)
                copy(("xT6", 1), xnT[:, 1, :])
                for a in range(2):
                    for t in range(NT):
                        n = (t + 1) * P if a == 0 else S
                        o = got(dve, ("S6", a, t))
                        V.reduce_max(nm4[:, t:t + 1], o[:, 0:n], AX_X, negate=True).then_inc(max6_ready, 1)
                    res = xn if a == 0 else n1
                    if a == 1:
                        dve.wait_ge(affine_ready, 1)
                    for t in range(NT):
                        nb = t + 1 if a == 0 else NT
                        o = got(dve, ("P6", a, t))
                        taken(V.tensor_copy(PT6[:, t % 2, 0:nb * P], o[:, 0:nb * P]), ("P6", a, t))
                        if t % 2:
                            i = t // 2
                            link(V.reciprocal(rden4[:, 2 * i:2 * i + 2], den4[:, 2 * i:2 * i + 2]))
                            o = two(got(dve, ("O6", a, i)))
                            for tt in (2 * i, 2 * i + 1):
                                if a == 0:
                                    ins = V.tensor_scalar(att[:, tt, :], o[:, tt % 2, :], rden4[:, tt:tt + 1], None, ALU.mult)
                                else:
                                    ins = V.scalar_tensor_tensor(n2[:, tt, :], o[:, tt % 2, :], rden4[:, tt:tt + 1],
                                                                 n1[:, tt, :], ALU.mult, ALU.add)
                            taken(ins, ("O6", a, i))
                            in_sbuf(dve, ("O6", a, i))
                    if a == 0:
                        link(V.tensor_tensor(n1, att, xn[:, :, :], ALU.add))
                        norm("6a", n1, n1)
                    else:
                        norm("6b", n2, n2)
                for m in range(2):
                    in_sbuf(dve, ("h6", m))
                    V.scalar_tensor_tensor(h6[:, m, :], v6[:, m, :], 0.2, v6[:, m, :], ALU.mult, ALU.max).then_inc(h6_ready, 1)
                dve.wait_ge(affine_ready, 3)
                for i in range(2):
                    o = two(got(dve, ("f6", i)))
                    taken(V.tensor_tensor(n1[:, 2 * i:2 * i + 2, :], o, n2[:, 2 * i:2 * i + 2, :], ALU.add), ("f6", i))
                in_sbuf(dve, ("f6", 0))
                in_sbuf(dve, ("f6", 1))
                norm("6c", n1, n1)
                dve.wait_ge(affine_ready, 4)
                link(V.scalar_tensor_tensor(x[:, :, :], n1, 0.0, x[:, :, :], ALU.max, ALU.add))

                norm(7, x, xn)
                copy(("xT7", 1), xnT[:, 1, :])
                for m in range(6):
                    gated(("G7", m), ("U7", m), sg7[:, m % 2, :], hid7[:, m, :])
                add_to_x("Y7")
                meet(dve, b)


LOG_N_K = 0.5753641449035618
SHIFT = 20.0
EXP_SHIFT = 485165195.4097903


def out_tile(dve, V, got, taken, link, n, rden, den, Ot):
    u, heads = PT_TILES[n]
    if u % NG == NG - 1 and heads is not None and heads[-1] == HG - 1:
        qt = u // NG
        o = got(dve, ("O", qt))
        link(V.reciprocal(rden, den[:, qt, :]))
        taken(V.tensor_tensor(Ot[:, qt, :].rearrange("p (h n) -> p h n", h=NH),
                              o[:, 0:D].rearrange("p (h n) -> p h n", h=NH),
                              rden.unsqueeze(2).broadcast_to([P, NH, DK]), ALU.mult), ("O", qt))


def _constants(np):
    c = {}
    inv = (1.0 / 10000.0 ** (np.arange(0, DK, 2, dtype=np.float32) / np.float32(DK))).astype(np.float32)
    f = np.arange(S, dtype=np.float32)[:, None] * inv[None, :]
    emb = np.concatenate([f, f], 1)
    cos, sin = np.cos(emb).astype(np.float32), np.sin(emb).astype(np.float32)
    rope = np.zeros((P, S), np.float32)
    for j in range(HG):
        rope[32 * j:32 * j + 16] = cos.T
        rope[32 * j + 16:32 * j + 24] = -sin.T[0:8]
        rope[32 * j + 24:32 * j + 32] = sin.T[8:16]
    c["rope"] = rope * np.float32(0.5)
    r = np.arange(P)
    c["fold"] = ((r[:, None] // 32 == r[None] // 32) & (r[:, None] % 16 == r[None] % 16)).astype(np.float32)
    c["ident"] = np.eye(P, dtype=np.float32)
    c["gmask"] = (r[:, None] // 32 == (np.arange(D)[None] // DK) % HG).astype(np.float32)
    bm = np.zeros((P, 136), np.float32)
    bm[:, :P] = r[:, None] // DK == r[None] // DK
    bm[:, P:] = r[:, None] // DK == np.arange(8)[None]
    c["bmask"] = bm
    i = np.arange(S)[:, None]
    j = np.arange(S)[None]
    blocked = (np.abs(i - j) > 128) | (j > i)
    blocked &= ~((i < 16) | (j < 16))
    m = np.where(blocked, -1e30, 0.0)
    parts = [m[0:128], m[128:256, 0:256]]
    for qt in (2, 3):
        rows = m[qt * P:(qt + 1) * P]
        g = np.full((P, 32), -1e30)
        g[:, 0:16] = rows[:, 0:16]
        parts += [rows[:, (qt - 1) * P:(qt + 1) * P], g]
    c["mask0"] = np.concatenate(parts, 1)
    band = []
    for t in range(NT):
        q = t * P + r[:, None]
        k = t * P - 32 + np.arange(KEYW)[None]
        band.append(np.where((np.abs(q - k) <= 20) & (k >= 0) & (k < S), 0.0, -1e8))
    c["band"] = np.concatenate(band, 1)
    c["causal"] = np.where(r[None] > r[:, None], -1e30, 0.0)
    c["identb"] = np.eye(P)
    lt = (np.arange(896)[None] - 384 < r[:, None])
    c["lt"], c["ge"] = lt * 1.0, 1.0 - lt
    a = np.concatenate([c[n] for n, _ in CONST], 1).astype(np.float32)
    z = np.concatenate([c[n] for n, _ in CONSTB], 1).astype(np.float32)
    return a, z


def _layout(np, i):
    def rows_of(w):
        return w.reshape(-1, P, w.shape[1]).transpose(1, 0, 2).reshape(P, -1)

    def padded_heads(w):
        h = w.reshape((NH, DK) + w.shape[1:])
        partner = np.concatenate([h[:, 1::2], h[:, ::2]], 1)
        return np.concatenate([h, partner], 1).reshape((NH * 32,) + w.shape[1:])

    def reversed_heads(w):
        return w.reshape(NH, DK, D)[:, ::-1].reshape(D, D)

    w = {"wq": rows_of(padded_heads(i["L0_xattn_wq"]).T), "wk": rows_of(padded_heads(i["L0_xattn_wk"]).T),
         "wv": rows_of(i["L0_xattn_wv"].T), "wo": rows_of(i["L0_xattn_wo"].T),
         "lw1": rows_of(i["L0_ffn_light_w1"]), "lw2": rows_of(i["L0_ffn_light_w2"]),
         "wred": rows_of(i["L1_xattn_W_reduce"].T), "l1r": rows_of(i["L1_ffn_Wr"]),
         "l1g": np.concatenate([rows_of(e) for e in i["L1_ffn_Wg"]], 1),
         "l1u": np.concatenate([rows_of(e) for e in i["L1_ffn_Wu"]], 1),
         "l1d": np.concatenate([rows_of(e) for e in i["L1_ffn_Wd"]], 1),
         "w2q": rows_of(reversed_heads(i["L2_xattn_Wq"]).T), "w2k": rows_of(reversed_heads(i["L2_xattn_Wk"]).T),
         "w2v": rows_of(i["L2_xattn_Wv"].T), "w2p": rows_of(i["L2_xattn_Wp"].T), "l2r": rows_of(i["L2_ffn_router_w"]),
         "k1": rows_of(i["L3_xattn_Wk1"]), "q1": rows_of(i["L3_xattn_Wq1"]), "v1": rows_of(i["L3_xattn_Wv1"]),
         "k2": rows_of(i["L3_xattn_Wk2"]), "q2": rows_of(i["L3_xattn_Wq2"]), "v2": rows_of(i["L3_xattn_Wv2"]),
         "f1": rows_of(i["L3_xattn_W1"]), "f2": rows_of(i["L3_xattn_W2"])}
    heavy1, heavy2 = i["L0_ffn_heavy_w1"], i["L0_ffn_heavy_w2"]
    chunks = [np.concatenate([rows_of(heavy1[:, c * 512:(c + 1) * 512]), rows_of(heavy2[c * 512:(c + 1) * 512])], 1)
              for c in range(2)]

    def expert(g, u, d):
        z = np.zeros((P, CHUNK - 1536), g.dtype)
        return np.concatenate([rows_of(g), rows_of(u), rows_of(d), z], 1)

    chunks += [expert(i["L2_ffn_gate_w"][e], i["L2_ffn_up_w"][e], i["L2_ffn_down_w"][e]) for e in range(8)]
    chunks += [expert(i["L2_ffn_shared_gate_w"][:, f], i["L2_ffn_shared_up_w"][:, f], i["L2_ffn_shared_down_w"][f])
               for f in (slice(0, 256), slice(256, 512))]
    c = {"bq": padded_heads(i["L0_xattn_bq"]).reshape(4, P).T, "bk": padded_heads(i["L0_xattn_bk"]).reshape(4, P).T,
         "lgam": i["L0_ffn_light_gamma"].reshape(2, P).T, "hgam": i["L0_ffn_heavy_gamma"].reshape(2, P).T,
         "lb1": i["L0_ffn_light_b1"].reshape(1, P).T, "hb1": i["L0_ffn_heavy_b1"].reshape(8, P).T,
         "bred": i["L1_xattn_b_reduce"].reshape(2, P).T,
         "convw": i["L1_ffn_conv_w"].reshape(4, 2, P).transpose(2, 1, 0).reshape(P, 8),
         "b1": i["L3_xattn_b1"].reshape(2, P).T,
         "focus": np.broadcast_to(np.reshape(i["L2_xattn_focusing_factor"], (1, 1)), (P, 1))}
    r = {"bv": i["L0_xattn_bv"], "bo": i["L0_xattn_bo"], "lb2": i["L0_ffn_light_b2"], "hb2": i["L0_ffn_heavy_b2"],
         "convb": i["L1_ffn_conv_b"], "b2": i["L3_xattn_b2"], "gamma": i["L3_xattn_gamma"],
         "beta": i["L3_xattn_beta"], "rt": i["L0_ffn_routing_token"], "rbias": i["L1_ffn_router_bias"]}
    const, constb = _constants(np)
    ctx = i["ctx_1024"]
    shifted = np.zeros((NB, 5 * P, D), ctx.dtype)
    shifted[:, 32:32 + S] = ctx
    return {
        "x": i["x"].reshape(NB, NT, P, D).transpose(0, 2, 1, 3).reshape(NB * P, NT * D),
        "ctxT": ctx.reshape(NB, S, 2, P).transpose(0, 3, 2, 1).reshape(NB * P, 2 * S),
        "ctxs": shifted.reshape(NB, 5, P, D).transpose(0, 2, 1, 3).reshape(NB * P, 5 * D),
        "ctx0": np.tile(ctx[:, 0:32].reshape(NB, 1, 32, 2, P), (1, HG, 1, 1, 1)).transpose(0, 4, 3, 1, 2).reshape(NB * P, 2 * P),
        "weights": np.concatenate([w[n] for n, _ in WEIGHTS], 1),
        "stream": np.concatenate(chunks, 0),
        "wint": np.concatenate([rows_of(i["L3_ffn_w_gate"].T), rows_of(i["L3_ffn_w_up"].T),
                                rows_of(i["L3_ffn_w_down"].T)], 1),
        "cols": np.concatenate([c[n] for n, _ in COLS], 1),
        "rows": np.broadcast_to(np.concatenate([r[n] for n, _ in ROWS])[None], (P, sum(n for _, n in ROWS))),
        "const": const, "constb": constb}


def kernel(**inputs):
    import numpy as _np
    import concourse.bacc as _bacc
    from concourse import mybir as _mybir
    from concourse.bass_utils import run_bass_kernel_spmd as _run

    nc = _bacc.Bacc("TRN2", target_bir_lowering=False, num_devices=1)
    arrays, args = {}, []
    for name, a in _layout(_np, {k: _np.asarray(v) for k, v in inputs.items()}).items():
        a = _np.ascontiguousarray(a)
        arrays[f"in_{name}"] = a
        args.append(nc.dram_tensor(f"in_{name}", a.shape, _mybir.dt.from_np(a.dtype), kind="ExternalInput").ap())
    args.append(nc.dram_tensor("out_x", (NB * P, NT * D), _mybir.dt.float32, kind="ExternalOutput").ap())
    network(nc, *args)
    r = _run(nc, [arrays], core_ids=[0]).results[0]["out_x"]
    return r.reshape(NB, P, NT, D).transpose(0, 2, 1, 3).reshape(NB, S, D)
```

```python
from contextlib import ExitStack

import concourse.bass as bass
from concourse import mybir

F32 = mybir.dt.float32
BF16 = mybir.dt.bfloat16
I32 = mybir.dt.int32
ALU = mybir.AluOpType
ACT = mybir.ActivationFunctionType
AX_X = mybir.AxisListType.X

P = 128
NB, S, D = 4, 512, 256
NT = S // P
NH, DK = 16, 16
HG = 4
NG = NH // HG
BIG = 3.0e38
K_EFF = 256 * 9.0 / 8.0
TOP_HEAVY = 256
ROUNDS, ITERS = 4, 12
KEYW = 192
KEYPAD = 640
KROW = S + 64
KTILE = (0, P + 32, 2 * P + 32, 3 * P + 32)
WSTART = (0, 0, P, 2 * P + 32)
WIN = (512, 288, 288, 288)
WOFF = (0, 512, 800, 1088)
WBLOCKS = ((0, 128, 256, 384), (0, 160), (32, 160), (0, 128))
WGLOBAL = (None, None, 0, 256)
NSLOT = 3
CHUNK = 2048

WEIGHTS = [("wq", 1024), ("wk", 1024), ("wv", 512), ("wo", 1024),
           ("lw1", 256), ("lw2", 256),
           ("wred", 512), ("l1r", 16), ("l1g", 1024), ("l1u", 1024), ("l1d", 1024),
           ("w2q", 512), ("w2k", 512), ("w2v", 512), ("w2p", 512), ("l2r", 16),
           ("k1", 512), ("q1", 512), ("v1", 512), ("k2", 512), ("q2", 512), ("v2", 512),
           ("f1", 512), ("f2", 512)]
WGROUPS = [("wq", "wo"), ("lw1", "lw2"), ("wred", "l1d"), ("w2q", "l2r"), ("k1", "f2")]
COLS = [("bq", 4), ("bk", 4), ("lgam", 2), ("hgam", 2), ("lb1", 1), ("hb1", 8), ("bred", 2),
        ("convw", 8), ("b1", 2), ("focus", 1)]
ROWS = [("bv", 256), ("bo", 256), ("lb2", 256), ("hb2", 256), ("convb", 256), ("b2", 256),
        ("gamma", 256), ("beta", 256), ("rt", 256), ("rbias", 8)]
CONST = [("rope", 512), ("fold", 128), ("ident", 128), ("bmask", 136)]
CONSTB = [("identb", 128), ("mask0", 1376), ("causal", 128), ("band", 4 * KEYW), ("lt", 896), ("ge", 896)]
FIRSTB = 128 + 1376 + 128


def offsets(table):
    at, out = 0, {}
    for name, n in table:
        out[name] = (at, n)
        at += n
    return out, at


NU = NT * NH // 2


def tiles_of_unit(u):
    qt = u // (NH // 2)
    if qt == 0:
        return [(0,), (1,)]
    return ([None] if qt >= 2 else []) + [(0, 1)]


PT_TILES = [(u, heads) for u in range(NU) for heads in tiles_of_unit(u)]
UNIT_TILES = [[n for n, (v, _) in enumerate(PT_TILES) if v == u] for u in range(NU)]


def psum_plan():
    out = []

    def use(key, bank):
        out.append((key, bank))

    def pair(name, banks):
        for i, bank in enumerate(banks):
            use((name, i), bank)

    use(("K", 0), 2)
    for g in range(NG):
        if g < NG - 1:
            use(("K", g + 1), 2 + (g + 1) % 2)
        else:
            pair("V", (6, 7))
        use(("F", g), 4 + g % 2)
    pair("xT0", (0, 1))
    for g in range(NG):
        use(("Q", g), 2 + g % 2)
    for u in range(NU + 2):
        if u >= 3 and (u - 3) % (NH // 2) == 0:
            use(("O", (u - 3) // (NH // 2)), 7)
        if 2 <= u:
            for n in UNIT_TILES[u - 2]:
                use(("PT", n), 4 + n % 3)
        if u < NU:
            for j in range(2):
                use(("S", u, j), 2 * (u % 2) + j)
        if u >= 9 and (u - 9) % (NH // 2) == 0:
            use(("D", (u - 9) // (NH // 2)), 4 + (UNIT_TILES[u - 2][-1] + 2) % 3)
    pair("Y0", (0, 1))
    use("R", 2)
    pair("xT1", (0, 1))
    use(("h", "light"), 3)
    use("chain", 2)
    for m in range(8):
        use(("h", m), (0, 1, 3)[m % 3])
    pair("k4", (6, 7))
    pair("v4", (0, 1))
    pair("KT1", (3, 0))
    pair("yl", (4, 5))
    pair("yh", (6, 7))
    pair("xT2", (0, 1))
    for t in range(NT):
        use(("S1", t), 4 + t)
    for t in range(NT):
        use(("PT1", t), 2 + t % 2)
    pair("O1", (0, 1))
    pair("xT3", (0, 1))
    use("RT3", 7)
    for e in range(4):
        use(("G3", e), 2 + e % 2)
        use(("U3", e), 4 + e % 2)
        if e == 0:
            pair("CT3", (6, 0))
        else:
            for i in range(2):
                use(("Y3", e - 1, i), (1, 6, 0)[(2 * e + i) % 3])
    for i in range(2):
        use(("Y3", 3, i), (1, 6, 0)[(8 + i) % 3])
    pair("xT4", (0, 1))
    pair("q4", (6, 7))
    for h in range(2):
        use(("K6", 1, h), 4 + h)
    for i in range(2):
        use(("V6", 1, i), i)
    pair("KV4", (2, 3))
    pair("QT4", (4, 5))
    for t in range(NT):
        use(("y4", t), 6 + t % 2)
    pair("yT4", (0, 1))
    pair("O4", (2, 3))
    pair("xT5", (0, 1))
    use("RT5", 7)
    for e in range(10):
        for f in range(2):
            use(("G5", e, f), 2 + f)
            use(("U5", e, f), 4 + f)
        if e:
            for i in range(2):
                use(("Y5", e - 1, i), (6, 7, 0, 1)[(2 * e + i) % 4])
    for i in range(2):
        use(("Y5", 9, i), (6, 7, 0, 1)[(20 + i) % 4])
    pair("xT6", (0, 1))
    for h in range(2):
        use(("K6", 0, h), 2 + h)
        use(("Q6", 0, h), 4 + h)
    for i in range(2):
        use(("V6", 0, i), 6 + i)
    for a in range(2):
        for t in range(NT):
            use(("S6", a, t), 2 + t)
        for t in range(NT):
            use(("P6", a, t), 6 + t % 2)
        for i in range(2):
            use(("O6", a, i), i)
        if a == 0:
            pair("aT6", (2, 3))
            for h in range(2):
                use(("Q6", 1, h), 4 + h)
    pair("nT6", (6, 7))
    for m in range(2):
        use(("h6", m), 2 + m)
    pair("f6", (4, 5))
    pair("xT7", (0, 1))
    for m in range(6):
        use(("G7", m), 2 + m % 2)
        use(("U7", m), 4 + m % 2)
    pair("Y7", (6, 7))
    count, where = [0] * 8, {}
    for key, bank in out:
        assert key not in where, key
        where[key] = (bank, count[bank])
        count[bank] += 1
    return where


PLAN = psum_plan()
LN_INDEX = {0: 0, 1: 1, 2: 2, 3: 3, 4: 4, 5: 5, 6: 6, "6a": 7, "6b": 8, "6c": 9, 7: 10}


def network(nc, x_in, ctxT_in, ctxs_in, w_in, stream_in, wint_in, cols_in, rows_in, const_in, constb_in, out):
    stack = ExitStack()
    with stack:
        def sb(name, shape, dt=F32):
            return stack.enter_context(nc.sbuf_tensor(name, shape, dt))

        def sem(name):
            return stack.enter_context(nc.semaphore(name))

        woff, wn = offsets(WEIGHTS)
        coff, cn = offsets(COLS)
        roff, rn = offsets(ROWS)
        koff, kn = offsets(CONST)
        boff, bn = offsets(CONSTB)
        weights = sb("weights", [P, wn])
        wint = sb("wint", [P, 4608], I32)
        wl3 = wint[:, :].bitcast(F32)
        stream = sb("stream", [P, NSLOT, CHUNK])
        cols = sb("cols", [P, cn])
        rows = sb("rows", [P, rn])
        const = sb("const", [P, kn])
        constb = sb("constb", [P, bn], BF16)

        def W(name, k=2):
            at, n = woff[name]
            return weights[:, at:at + n].rearrange("p (k n) -> p k n", k=k)

        def col(name, i=0):
            return cols[:, coff[name][0] + i:coff[name][0] + i + 1]

        def row(name, n=1):
            at, w = roff[name]
            r = rows[:, at:at + w]
            return r if n == 1 else r.unsqueeze(1).broadcast_to([P, n, w])

        def K(name):
            at, n = koff[name]
            return const[:, at:at + n]

        def KB(name):
            at, n = boff[name]
            return constb[:, at:at + n]

        x = sb("x", [P, NT, D])
        xn = sb("xn", [P, NT, D])
        xnT = sb("xnT", [P, 2, S])
        ctxT = sb("ctxT", [P, 2, S])
        ctxs = sb("ctxs", [P, 5, D])
        small = sb("small", [P, 464])
        onesk = sb("onesk", [P, P])
        EVEN, ODD = 9984, 7168
        even = sb("even", [P, EVEN])
        odd = sb("odd", [P, ODD])
        at_small = [0]

        def sm(n, shape=None):
            a = small[:, at_small[0]:at_small[0] + n]
            at_small[0] += n
            assert at_small[0] <= 464
            return a if shape is None else a.rearrange("p (a b) -> p a b", a=shape)

        class Area:
            def __init__(self, t, size):
                self.t, self.size, self.at = t, size, 0

            def take(self, n):
                a = self.t[:, self.at:self.at + n]
                self.at += n
                assert self.at <= self.size, self.at
                return a

        def v3(ap, a):
            return ap.rearrange("p (a b) -> p a b", a=a)

        eps6 = sm(1)
        mhalf = sm(NT)
        stats = sm(NT * 6, NT)
        mv = sm(NT * 2, NT)
        var = sm(NT)
        rstd = sm(NT)
        nm = sm(4, 2)
        rden4 = sm(NT)
        nm4 = sm(NT)
        den4 = sm(NT)
        ss = sm(NT)
        rmsr = sm(NT)
        scol = sm(NT)
        kcol = sm(NT)
        nmax = sm(1)
        lsum = sm(1)
        lnv = sm(1)
        lsh = sm(2)
        lfin = sm(1)
        ce = sm(NT)
        ev = sm(NT)
        jc = sm(NT)
        rs = sm(2)
        rk1 = sm(NT)
        rk2 = sm(NT)
        score = sm(NT)
        wgt = sm(NT)
        sc = sm(32, NT)
        tb = sm(64, NT)
        t8 = sm(32, NT)
        tr = sm(64, NT)
        cw = sm(40, NT)
        c46 = sm(NT)
        fsum = sm(NT)
        psumm = sm(NT)
        fmax = sm(NT)
        fco = sm(NT)

        ar = Area(even, EVEN)
        Kf = v3(ar.take(NG * KROW), NG)
        Qr = v3(ar.take(NG * S), NG)
        V0 = ar.take(NT * NH * 32).rearrange("p (t h n) -> p t h n", t=NT, h=NH)
        probs = ar.take(4 * S).rearrange("p (a b c) -> p a b c", a=2, b=2)
        Kr = probs.rearrange("p a b c -> p (a b) c")
        PTs = v3(ar.take(3 * S), 3)
        OT = Qr
        ar = Area(odd, ODD)
        Qz = [ar.take(NG * HG * P).rearrange("p (g h n) -> p g h n", g=NG, h=HG) for _ in range(2)]
        rsum = ar.take(S)
        rexp = v3(ar.take(S), NH)
        den = v3(ar.take(NT * NH), NT)
        rden = v3(ar.take(NT * NH), NT)
        ar = Area(even, EVEN)
        kr1 = v3(ar.take(2 * KEYPAD), 2)
        P1 = v3(ar.take(NT * KEYW), NT)
        PT1 = v3(ar.take(NT * 256), NT)
        V2 = ar.take(NT * 2 * 132).rearrange("p (t c n) -> p t c n", t=NT, c=2)
        yin = ar.take(NT * NH * 19).rearrange("p (t h n) -> p t h n", t=NT, h=NH)
        yout_ = ar.take(NT * NH * 19)
        yout = yout_.rearrange("p (t h n) -> p t h n", t=NT, h=NH)
        fa = v3(yout_[:, 0:NT * D], NT)
        fb = v3(ar.take(NT * D), NT)
        ymk = v3(ar.take(NT * D), NT)
        top8 = ar.take(NT * NH * 8).rearrange("p (t h n) -> p t h n", t=NT, h=NH)
        ar2 = Area(even, EVEN)
        ymq = v3(ar2.take(NT * D), NT)
        qsT = v3(ar2.take(2 * S), 2)
        kvm = v3(ar2.take(2 * 136), 2)
        zr = v3(ar2.take(16), 2)
        ym = [ymk, ymq]
        y4 = fb
        yT4 = v3(yin.rearrange("p t h n -> p (t h n)")[:, 0:2 * S], 2)
        ar = Area(even, EVEN)
        K6 = [v3(ar.take(2 * S), 2), v3(odd[:, 3072:3072 + 2 * S], 2)]
        V6 = [v3(ar.take(NT * D), NT), v3(odd[:, 3072 + 2 * S:3072 + 4 * S], NT)]
        Q6 = v3(ar.take(2 * S), 2)
        P6 = v3(ar.take(NT * S), NT)
        PT6 = v3(ar.take(2 * S), 2)
        att = v3(ar.take(NT * D), NT)
        n1 = v3(ar.take(NT * D), NT)
        n2 = att
        attT = K6[0]
        h6 = Q6
        ar = Area(odd, ODD)
        xlT = v3(ar.take(2 * S), 2)
        xhT = v3(ar.take(2 * S), 2)
        hL = ar.take(S)
        hH = v3(ar.take(8 * S), 8)
        srow = ar.take(S)
        krow = xlT[:, 0, :]
        jrow = xlT[:, 1, :]
        th = xhT[:, 0, 0:D]
        ar = Area(odd, ODD)
        sg3 = v3(ar.take(2 * S), 2)
        hid3 = v3(ar.take(2 * S), 2)
        conv = v3(ar.take(2 * S), 2)
        extra = v3(ar.take(NT * D), NT)
        pa3 = ar.take(D)
        pb3 = ar.take(D)
        ar = Area(odd, ODD)
        sg5 = v3(ar.take(2 * S), 2)
        hid5 = ar.take(4 * S).rearrange("p (e f n) -> p e f n", e=2, f=2)
        ar = Area(odd, ODD)
        sg7 = v3(ar.take(2 * S), 2)
        hid7 = v3(ar.take(6 * S), 6)
        v6 = v3(sg7[:, :, :].rearrange("p a b -> p (a b)"), 2)

        ps = stack.enter_context(nc.psum_tensor("ps", [P, 8, 512], F32))

        w_loaded = [sem(f"w_loaded{i}") for i in range(len(WGROUPS))]
        wint_loaded = sem("wint_loaded")
        const_loaded = sem("const_loaded")
        constb_loaded = sem("constb_loaded")
        setup_done = sem("setup_done")
        setup_step = sem("setup_step")
        go = sem("go")
        passed = sem("passed")
        x_loaded = sem("x_loaded")
        xn_loaded = sem("xn_loaded")
        ctxT_loaded = sem("ctxT_loaded")
        ctxs_loaded = sem("ctxs_loaded")
        first_chunks = [sem(f"first_chunk{i}") for i in range(NSLOT)]
        out_stored = sem("out_stored")
        first = sem("batch_done")
        batch_done = first
        psum_filled = [sem(f"psum_filled{i}") for i in range(8)]
        psum_taken = [sem(f"psum_taken{i}") for i in range(8)]
        chunk_loaded = [sem(f"chunk_loaded{i}") for i in range(NSLOT)]
        ln_stats = sem("ln_stats")
        ln_rstd = sem("ln_rstd")
        xn_ready = sem("xn_ready")
        x_biased = sem("x_biased")
        max_ready = sem("max_ready")
        scol_ready = sem("scol_ready")
        rms_sum = sem("rms_sum")
        rms_ready = sem("rms_ready")
        xr_ready = sem("xr_ready")
        lse_max = sem("lse_max")
        ln_ready = sem("ln_ready")
        ce_ready = sem("ce_ready")
        ev_ready = sem("ev_ready")
        rowsum_ready = sem("rowsum_ready")
        total_ready = sem("total_ready")
        kcol_ready = sem("kcol_ready")
        score_ready = sem("score_ready")
        keypad_ready = sem("keypad_ready")
        max1_ready = sem("max1_ready")
        router_exp = sem("router_exp")
        cw_ready = sem("cw_ready")
        extra_ready = sem("extra_ready")
        conv_ready = sem("conv_ready")
        silu_ready = sem("silu_ready")
        ones_ready = sem("ones_ready")
        zeros_ready = sem("zeros_ready")
        queries_spread = sem("queries_spread")
        abs_ready = sem("abs_ready")
        log_ready = sem("log_ready")
        focus_in = sem("focus_in")
        focus_exp = sem("focus_exp")
        sparse_ready = sem("sparse_ready")
        affine_ready = sem("affine_ready")
        max6_ready = sem("max6_ready")
        h6_ready = sem("h6_ready")
        dve_step = sem("dve_step")
        act_step = sem("act_step")
        sums_ready = sem("sums_ready")
        sums_spread = sem("sums_spread")
        rsum_ready = sem("rsum_ready")
        pool_step = sem("pool_step")
        last = pool_step

        def bank(key):
            return PLAN[key][0]

        def psb(key):
            return ps[:, PLAN[key][0], :]

        def got(eng, key):
            eng.wait_ge(psum_filled[PLAN[key][0]], PLAN[key][1] + 1)
            return psb(key)

        def in_sbuf(eng, key):
            eng.wait_ge(psum_taken[PLAN[key][0]], PLAN[key][1] + 1)

        def wait_chunk(eng, c, b):
            if c < NSLOT:
                eng.wait_ge(first_chunks[c], (b + 1) * 16)
            else:
                eng.wait_ge(chunk_loaded[c % NSLOT], 16 * (c // NSLOT))

        def meet(eng, b):
            eng.drain().then_inc(batch_done, 1)
            eng.wait_ge(go, b + 1)
            eng.sem_inc(passed, 1)

        block = stack.enter_context(nc.Block())

        @block.sync
        def _(sp):
            def load_ctxT(b):
                sp.dma_start(ctxT[:, :, :].rearrange("p t d -> p (t d)"), ctxT_in[bass.ds(b * P, P), :]).then_inc(ctxT_loaded, 16)

            def load_ctxs(b):
                sp.dma_start(ctxs[:, :, :].rearrange("p t d -> p (t d)"), ctxs_in[bass.ds(b * P, P), :]).then_inc(ctxs_loaded, 16)

            def load_x(dst, b, loaded):
                sp.dma_start(dst[:, :, :].rearrange("p t d -> p (t d)"), x_in[bass.ds(b * P, P), :]).then_inc(loaded, 16)

            def load_chunk(c, loaded):
                n = CHUNK if c < 2 else 1536
                sp.dma_start(stream[:, c % NSLOT, 0:n], stream_in[c * P:(c + 1) * P, 0:n]).then_inc(loaded, 16)

            def load_weights(i):
                lo, hi = woff[WGROUPS[i][0]][0], woff[WGROUPS[i][1]][0] + woff[WGROUPS[i][1]][1]
                sp.dma_start(weights[:, lo:hi], w_in[:, lo:hi]).then_inc(w_loaded[i], 16)

            sp.dma_start(even[:, 0:FIRSTB], constb_in[:, 0:FIRSTB]).then_inc(constb_loaded, 16)
            load_ctxT(0)
            load_weights(0)
            load_x(xn, 0, xn_loaded)
            sp.dma_start(cols[:, :], cols_in).then_inc(const_loaded, 16)
            sp.dma_start(const[:, :], const_in).then_inc(const_loaded, 16)
            sp.dma_start(rows[:, :], rows_in).then_inc(const_loaded, 16)
            load_weights(1)
            load_x(x, 0, x_loaded)
            sp.dma_start(odd[:, 0:bn - FIRSTB], constb_in[:, FIRSTB:bn]).then_inc(constb_loaded, 16)
            sp.dma_start(wint[:, :], wint_in).then_inc(wint_loaded, 16)
            for c in range(NSLOT):
                load_chunk(c, first_chunks[c])
            for i in range(2, len(WGROUPS)):
                load_weights(i)
            load_ctxs(0)
            with sp.Fori(0, NB) as b:
                for c in range(NSLOT, 12):
                    got(sp, ("yh", 1) if c < 5 else ("Y5", c - 5, 1))
                    load_chunk(c, chunk_loaded[c % NSLOT])
                    if c == 5:
                        load_ctxs(b + 1)
                        load_ctxT(b + 1)
                for c in range(NSLOT):
                    got(sp, ("Y5", c + 7, 1))
                    load_chunk(c, first_chunks[c])
                for h in range(2):
                    got(sp, ("xT7", h))
                load_x(xn, b + 1, xn_loaded)
                for i in range(2):
                    in_sbuf(sp, ("Y7", i))
                    sp.dma_start(out[bass.ds(b * P, P), i * 512:(i + 1) * 512],
                                 x[:, 2 * i:2 * i + 2, :].rearrange("p t d -> p (t d)")).then_inc(out_stored, 16)
                sp.wait_ge(batch_done, 4)
                sp.sem_clear(range(first.num, last.num + 1))
                sp.drain().then_inc(go, 1)
                sp.wait_ge(out_stored, (b + 1) * 32)
                load_x(x, b + 1, x_loaded)
            for loaded in [x_loaded, xn_loaded, ctxT_loaded, ctxs_loaded] + first_chunks:
                sp.wait_ge(loaded, (NB + 1) * 16)
            sp.wait_ge(out_stored, NB * 32)

        @block.gpsimd
        def _(pool):
            g = nc.gpsimd
            g.memset(eps6, 1e-6).then_inc(setup_step, 1)
            g.memset(mhalf, -0.5).then_inc(setup_step, 1)
            g.memset(onesk[:, :], 1.0 / K_EFF).then_inc(setup_step, 1)
            g.memset(cw.rearrange("p t e -> p (t e)"), 1.0).then_inc(setup_step, 1)
            g.memset(tb.rearrange("p t e -> p (t e)"), BIG).then_inc(setup_step, 1)
            pool.wait_ge(setup_step, 5)
            pool.wait_ge(constb_loaded, 32)
            g.tensor_copy(constb[:, 0:FIRSTB], even[:, 0:FIRSTB]).then_inc(setup_done, 1)
            g.tensor_copy(constb[:, FIRSTB:bn], odd[:, 0:bn - FIRSTB]).then_inc(setup_done, 1)
            pool.wait_ge(wint_loaded, 16)
            g.tensor_scalar(wl3, wint[:, :], 1.0 / 127.0, None, ALU.mult).then_inc(setup_done, 1)
            pool.wait_ge(setup_done, 3)

            with pool.Fori(0, NB) as b:
                n = [0]

                def link(ins):
                    n[0] += 1
                    ins.then_inc(pool_step, 1)
                    pool.wait_ge(pool_step, n[0])

                def rstd_of(idx, eps):
                    pool.wait_ge(ln_stats, idx + 1)
                    link(g.tensor_scalar(var, mv[:, :, 1], eps, None, ALU.add))
                    g.tensor_tensor(rstd, var, mhalf, ALU.pow).then_inc(ln_rstd, 1)

                def add_row(idx, name):
                    pool.wait_ge(xn_ready, NT * (idx + 1))
                    g.tensor_tensor(x[:, :, :], x[:, :, :], row(name, NT), ALU.add).then_inc(x_biased, 1)

                for half in Qz:
                    g.memset(half[:, :, :, :], 0.0).then_inc(zeros_ready, 1)
                g.memset(V0[:, :, :, DK:32], 0.0).then_inc(zeros_ready, 1)
                rstd_of(0, 1e-5)
                pool.wait_ge(x_loaded, (b + 1) * 16)
                g.tensor_tensor(x[:, :, :], x[:, :, :], row("bo", NT), ALU.add).then_inc(x_biased, 1)
                pool.wait_ge(x_biased, 1)
                for key in [("Q", g_) for g_ in range(NG)]:
                    in_sbuf(pool, key)
                pool.wait_ge(zeros_ready, 3)

                def spread_queries(qt):
                    if qt >= 2:
                        got(pool, ("S", (NH // 2) * (qt - 1) - 1, 1))
                    for j in range(HG):
                        r = slice(32 * j, 32 * j + 32)
                        g.tensor_copy(Qz[qt % 2][r, :, j, :], Qr[r, :, qt * P:(qt + 1) * P]).then_inc(queries_spread, 1)
                    pool.wait_ge(queries_spread, HG * (qt + 1))

                pool.wait_ge(queries_spread, HG)
                for qt in range(1, NT):
                    spread_queries(qt)
                rstd_of(1, 1e-5)
                add_row(1, "lb2")
                pool.wait_ge(rms_sum, 1)
                link(g.tensor_scalar(ss, ss, 1e-24, None, ALU.max))
                link(g.tensor_tensor(rmsr, ss, mhalf, ALU.pow))
                g.tensor_scalar(rmsr, rmsr, 16.0, None, ALU.mult).then_inc(rms_ready, 1)
                g.memset(V2[:, :, :, 128:129], 1.0).then_inc(ones_ready, 1)
                g.memset(yin[:, :, :, 16:19], 1.0).then_inc(ones_ready, 1)
                rstd_of(2, 1e-5)
                g.memset(kr1[:, :, 0:32], 0.0).then_inc(keypad_ready, 1)
                g.memset(kr1[:, :, 32 + S:KEYPAD], 0.0).then_inc(keypad_ready, 1)
                rstd_of(3, 1e-5)
                add_row(3, "convb")
                pool.wait_ge(x_biased, 3)
                pool.wait_ge(cw_ready, 1)
                link(g.tensor_tensor(c46, cw[:, :, 4], cw[:, :, 6], ALU.add))
                for t in range(NT):
                    link(g.tensor_scalar(pa3, xn[:, t, :], 0.0, cw[:, t, 7:8], ALU.max, ALU.mult))
                    link(g.tensor_scalar(pb3, xn[:, t, :], c46[:, t:t + 1], None, ALU.mult))
                    link(g.tensor_tensor(pa3, pa3, pb3, ALU.add))
                    g.tensor_tensor(extra[:, t, :], pa3, x[:, t, :], ALU.add).then_inc(extra_ready, 1)
                    pool.wait_ge(extra_ready, t + 1)
                rstd_of(4, 1e-5)
                rstd_of(5, 1e-5)
                rstd_of(6, 1e-5)
                rstd_of(7, 1e-3)
                pool.wait_ge(xn_ready, NT * 8)
                link(g.tensor_tensor(n1, n1, row("gamma", NT), ALU.mult))
                g.tensor_tensor(n1, n1, row("beta", NT), ALU.add).then_inc(affine_ready, 1)
                rstd_of(8, 1e-3)
                pool.wait_ge(xn_ready, NT * 9)
                link(g.tensor_tensor(n2, n2, row("gamma", NT), ALU.mult))
                g.tensor_tensor(n2, n2, row("beta", NT), ALU.add).then_inc(affine_ready, 1)
                in_sbuf(pool, ("nT6", 0))
                in_sbuf(pool, ("nT6", 1))
                g.tensor_tensor(n2, n2, row("b2", NT), ALU.add).then_inc(affine_ready, 1)
                rstd_of(9, 1e-3)
                pool.wait_ge(xn_ready, NT * 10)
                link(g.tensor_tensor(n1, n1, row("gamma", NT), ALU.mult))
                g.tensor_tensor(n1, n1, row("beta", NT), ALU.add).then_inc(affine_ready, 1)
                rstd_of(10, 1e-5)
                meet(pool, b)

        @block.tensor
        def _(pe):
            T = nc.tensor
            ident = K("ident")
            identb = KB("identb")
            pe.wait_ge(const_loaded, 48)

            def room(key):
                if PLAN[key][1]:
                    pe.wait_ge(psum_taken[PLAN[key][0]], PLAN[key][1])
                return psb(key)

            def full(ins, key):
                ins.then_inc(psum_filled[bank(key)], 1)

            def mm(out_, lhs, rhs, ks, start=True, stop=True):
                ks = list(ks)
                for k in ks:
                    ins = T.matmul(out_, lhs(k), rhs(k), start=start and k == ks[0], stop=stop and k == ks[-1])
                return ins

            def tok(t):
                return slice(t * P, (t + 1) * P)

            def xT(s):
                a, c = room((f"xT{s}", 0)), room((f"xT{s}", 1))
                for t in range(NT):
                    pe.wait_ge(xn_ready, NT * LN_INDEX[s] + t + 1)
                    for h, o in enumerate((a, c)):
                        ins = T.transpose(o[:, tok(t)], xn[:, t, h * P:(h + 1) * P], ident)
                        if t == NT - 1:
                            full(ins, (f"xT{s}", h))

            def transposed(name, src):
                for h in range(2):
                    o = room((name, h))
                    for t in range(NT):
                        ins = T.transpose(o[:, tok(t)], src(t, h), ident)
                    full(ins, (name, h))

            def token_major(key_of, act_T, w, n=D):
                for i in range(2):
                    o = room(key_of(i))
                    for t in (2 * i, 2 * i + 1):
                        ins = mm(o[:, (t % 2) * D:(t % 2) * D + n], lambda k: act_T[:, k, tok(t)],
                                 lambda k: w[:, k, 0:n], range(2))
                    full(ins, key_of(i))

            def chan_major(key, w, c, act_T):
                full(mm(room(key), lambda k: w[:, k, c:c + P], lambda k: act_T[:, k, :], range(2)), key)

            with pe.Fori(0, NB) as b:
                pe.wait_ge(w_loaded[0], 16)
                pe.wait_ge(ctxT_loaded, (b + 1) * 16)
                chan_major(("K", 0), W("wk"), 0, ctxT)
                for g in range(NG):
                    if g < NG - 1:
                        chan_major(("K", g + 1), W("wk"), (g + 1) * P, ctxT)
                    else:
                        token_major(lambda i: ("V", i), ctxT, W("wv"))
                    in_sbuf(pe, ("K", g))
                    full(T.matmul(room(("F", g)), K("fold"), Kr[:, g, :], start=True, stop=True), ("F", g))
                xT(0)
                in_sbuf(pe, ("xT0", 0))
                in_sbuf(pe, ("xT0", 1))
                for g in range(NG):
                    chan_major(("Q", g), W("wq"), g * P, xnT)
                pe.wait_ge(zeros_ready, 3)
                pe.wait_ge(setup_done, 1)
                for key in [("F", g) for g in range(NG)] + [("Q", g) for g in range(NG)] + [("V", 0), ("V", 1)]:
                    in_sbuf(pe, key)

                def scores(u):
                    qt, hp = divmod(u, NH // 2)
                    if hp == 0:
                        pe.wait_ge(queries_spread, HG * (qt + 1))
                    outs = [room(("S", u, j)) for j in range(2)]
                    for j, o in enumerate(outs):
                        g, i = divmod(2 * hp + j, HG)
                        q = Qz[qt % 2][:, g, i, :]
                        if qt:
                            T.matmul(o[:, 0:WIN[qt]], q, Kf[:, g, WSTART[qt]:WSTART[qt] + WIN[qt]], start=True, stop=False)
                        else:
                            T.matmul(o[:, 0:P], q, Kf[:, g, 0:P], start=True, stop=False)
                            T.matmul(o[:, P:S], q, Kf[:, g, KTILE[1]:KTILE[1] + 3 * P], start=False, stop=False)
                    for j, o in enumerate(outs):
                        full(T.matmul(o[:, 0:WIN[qt]], identb, KB("mask0")[:, WOFF[qt]:WOFF[qt] + WIN[qt]],
                                      start=False, stop=True), ("S", u, j))

                def prob_T(n):
                    u, heads = PT_TILES[n]
                    qt = u // (NH // 2)
                    o = room(("PT", n))
                    if heads is None:
                        for j in range(2):
                            ins = T.transpose(o[0:32, tok(j)], probs[:, u % 2, j, WGLOBAL[qt]:WGLOBAL[qt] + 32], ident)
                    else:
                        for i, j in enumerate(heads):
                            for c, at in enumerate(WBLOCKS[qt]):
                                ins = T.transpose(o[:, tok(i * len(WBLOCKS[qt]) + c)], probs[:, u % 2, j, at:at + P], ident)
                    full(ins, ("PT", n))

                def prob_V(u):
                    qt, hp = divmod(u, NH // 2)
                    o = room(("O", qt)) if hp == 0 else psb(("O", qt))
                    for n in UNIT_TILES[u]:
                        in_sbuf(pe, ("PT", n))
                    blocks = NT if qt == 0 else 2
                    for j in range(2):
                        h = 2 * hp + j
                        oh = o[32 * (h % HG):32 * (h % HG) + 32, tok(h // HG)]
                        if qt >= 2:
                            T.matmul(oh, V0[0:32, 0, h, :], PTs[0:32, UNIT_TILES[u][0] % 3, tok(j)],
                                     start=True, stop=False)
                        n = UNIT_TILES[u][j if qt == 0 else -1]
                        for c in range(blocks):
                            ins = T.matmul(oh, V0[:, max(0, qt - 1) + c, h, :],
                                           PTs[:, n % 3, tok(c if qt == 0 else j * blocks + c)],
                                           start=(qt < 2 and c == 0), stop=(c == blocks - 1))
                    if hp == NH // 2 - 1:
                        full(ins, ("O", qt))

                def sums_T(qt):
                    pe.wait_ge(sums_spread, qt + 1)
                    o = room(("D", qt))
                    for g in range(NG):
                        ins = T.transpose(o[:, tok(g)], rexp[:, HG * g:HG * g + HG, :].rearrange("p h n -> p (h n)"), ident)
                    full(ins, ("D", qt))

                for u in range(NU + 2):
                    if u >= 3:
                        prob_V(u - 3)
                    if u >= 2:
                        for j in range(2):
                            in_sbuf(pe, ("S", u - 2, j))
                        for n in UNIT_TILES[u - 2]:
                            prob_T(n)
                    if u < NU:
                        scores(u)
                    if u >= 9 and (u - 9) % (NH // 2) == 0:
                        sums_T((u - 9) // (NH // 2))
                prob_V(NU - 1)
                for i in range(2):
                    o = room(("Y0", i))
                    for t in (2 * i, 2 * i + 1):
                        in_sbuf(pe, ("O", t))
                        ins = mm(o[:, (t % 2) * D:(t % 2 + 1) * D], lambda g: OT[:, g, tok(t)],
                                 lambda g: W("wo", 4)[:, g, :], range(NG))
                    full(ins, ("Y0", i))

                pe.wait_ge(w_loaded[1], 16)
                pe.wait_ge(w_loaded[2], 16)
                pe.wait_ge(w_loaded[3], 16)
                pe.wait_ge(scol_ready, 1)
                o = room("R")
                for t in range(NT):
                    ins = T.transpose(o[:, tok(t)], scol[:, t:t + 1].broadcast_to([P, P]), ident)
                full(ins, "R")
                pe.wait_ge(xr_ready, NT)
                transposed("xT1", lambda t, h: xn[:, t, h * P:(h + 1) * P])
                in_sbuf(pe, ("xT1", 0))
                in_sbuf(pe, ("xT1", 1))
                chan_major(("h", "light"), W("lw1"), 0, xlT)

                def heavy_w(m):
                    c = stream[:, m // 4, :]
                    return c[:, 0:1024].rearrange("p (k n) -> p k n", k=2), c[:, 1024:2048].rearrange("p (m n) -> p m n", m=4)

                def branches():
                    for m in range(8):
                        wait_chunk(pe, m // 4, b)
                        o = room(("h", m))
                        for k in range(2):
                            ins = T.matmul(o, heavy_w(m)[0][:, k, (m % 4) * P:(m % 4 + 1) * P], xhT[:, k, :],
                                           start=(k == 0), stop=(k == 1))
                            if k == 1:
                                full(ins, ("h", m))
                            yield
                    for name, w in (("k4", W("w2k")), ("v4", W("w2v"))):
                        for i in range(2):
                            o = room((name, i))
                            for t in (2 * i, 2 * i + 1):
                                for k in range(2):
                                    ins = T.matmul(o[:, (t % 2) * D:(t % 2 + 1) * D], ctxT[:, k, tok(t)], w[:, k, :],
                                                   start=(k == 0), stop=(k == 1))
                                    if t % 2 and k == 1:
                                        full(ins, (name, i))
                                    yield
                    for h in range(2):
                        o = room(("KT1", h))
                        for k in range(2):
                            ins = T.matmul(o, W("wred")[:, k, tok(h)], ctxT[:, k, :], start=(k == 0), stop=(k == 1))
                            if k == 1:
                                full(ins, ("KT1", h))
                            yield
                    in_sbuf(pe, ("h", "light"))
                    for i in range(2):
                        o = room(("yl", i))
                        for t in (2 * i, 2 * i + 1):
                            ins = T.matmul(o[:, (t % 2) * D:(t % 2 + 1) * D], hL[:, tok(t)], W("lw2", 1)[:, 0, :],
                                           start=True, stop=True)
                            if t % 2:
                                full(ins, ("yl", i))
                            yield
                    for m in range(8):
                        in_sbuf(pe, ("h", m))
                    for i in range(2):
                        o = room(("yh", i))
                        for t in (2 * i, 2 * i + 1):
                            for m in range(8):
                                ins = T.matmul(o[:, (t % 2) * D:(t % 2 + 1) * D], hH[:, m, tok(t)],
                                               heavy_w(m)[1][:, m % 4, :], start=(m == 0), stop=(m == 7))
                                if t % 2 and m == 7:
                                    full(ins, ("yh", i))
                                yield

                work = branches()
                room("chain")
                done = 0
                share = (16, 20, 18, 18)
                for r in range(ROUNDS):
                    for i in range(ITERS):
                        n = r * ITERS + i
                        pe.wait_ge(rowsum_ready, n + 1)
                        ins = T.matmul(psb("chain")[:, n:n + 1], onesk[:, :], rs[:, n % 2:n % 2 + 1],
                                       start=True, stop=True)
                        if n == ROUNDS * ITERS - 1:
                            full(ins, "chain")
                        else:
                            ins.then_inc(total_ready, 1)
                        for _ in range((i + 1) * share[r] // ITERS - i * share[r] // ITERS):
                            next(work)
                for _ in work:
                    raise AssertionError

                xT(2)
                for key in (("xT2", 0), ("xT2", 1), ("KT1", 0), ("KT1", 1)):
                    in_sbuf(pe, key)
                pe.wait_ge(keypad_ready, 2)
                pe.wait_ge(setup_done, 2)
                for t in range(NT):
                    o = room(("S1", t))[:, 0:KEYW]
                    mm(o, lambda k: xnT[:, k, tok(t)], lambda k: kr1[:, k, t * P:t * P + KEYW], range(2), stop=False)
                    full(T.matmul(o, identb, KB("band")[:, t * KEYW:(t + 1) * KEYW], start=False, stop=True), ("S1", t))
                for t in range(NT):
                    in_sbuf(pe, ("S1", t))
                    o = room(("PT1", t))
                    T.transpose(o[:, 0:P], P1[:, t, 0:P], ident)
                    full(T.transpose(o[0:64, P:2 * P], P1[:, t, P:KEYW], ident), ("PT1", t))
                pe.wait_ge(ctxs_loaded, (b + 1) * 16)
                for i in range(2):
                    o = room(("O1", i))
                    for t in (2 * i, 2 * i + 1):
                        in_sbuf(pe, ("PT1", t))
                        T.matmul(o[:, (t % 2) * D:(t % 2 + 1) * D], PT1[:, t, 0:P], ctxs[:, t, :], start=True, stop=False)
                        ins = T.matmul(o[:, (t % 2) * D:(t % 2 + 1) * D], PT1[0:64, t, P:2 * P], ctxs[0:64, t + 1, :],
                                       start=False, stop=True)
                    full(ins, ("O1", i))

                def router(s, w):
                    key = f"RT{s}"
                    o = room(key)
                    for t in range(NT):
                        ins = mm(o[:, t * 8:t * 8 + 8], lambda k: xnT[:, k, tok(t)], lambda k: w[:, k, :], range(2))
                    full(ins, key)

                xT(3)
                in_sbuf(pe, ("xT3", 0))
                in_sbuf(pe, ("xT3", 1))
                router(3, W("l1r"))

                def down3(e):
                    in_sbuf(pe, ("U3", e))
                    for i in range(2):
                        o = room(("Y3", e, i))
                        for t in (2 * i, 2 * i + 1):
                            ins = T.matmul(o[:, (t % 2) * D:(t % 2 + 1) * D], hid3[:, e % 2, tok(t)],
                                           W("l1d", 4)[:, e, :], start=True, stop=True)
                        full(ins, ("Y3", e, i))

                for e in range(4):
                    chan_major(("G3", e), W("l1g", 8)[:, 2 * e:2 * e + 2, :], 0, xnT)
                    chan_major(("U3", e), W("l1u", 8)[:, 2 * e:2 * e + 2, :], 0, xnT)
                    if e == 0:
                        pe.wait_ge(conv_ready, 1)
                        for i in range(2):
                            o = room(("CT3", i))
                            for t in (2 * i, 2 * i + 1):
                                for h in range(2):
                                    ins = T.transpose(o[:, (t % 2) * D + h * P:(t % 2) * D + (h + 1) * P],
                                                      conv[:, h, tok(t)], ident)
                            full(ins, ("CT3", i))
                    else:
                        down3(e - 1)
                down3(3)

                xT(4)
                in_sbuf(pe, ("xT4", 0))
                in_sbuf(pe, ("xT4", 1))
                token_major(lambda i: ("q4", i), xnT, W("w2q"))
                pe.wait_ge(w_loaded[4], 16)
                for h in range(2):
                    chan_major(("K6", 1, h), W("k2"), h * P, ctxT)
                token_major(lambda i: ("V6", 1, i), ctxT, W("v2"))
                pe.wait_ge(sparse_ready, 1)
                pe.wait_ge(ones_ready, 2)
                in_sbuf(pe, ("v4", 0))
                in_sbuf(pe, ("v4", 1))
                for c in range(2):
                    o = room(("KV4", c))
                    for t in range(NT):
                        ins = T.matmul(o[:, 0:129], ymk[:, t, c * P:(c + 1) * P], V2[:, t, c, 0:129],
                                       start=(t == 0), stop=(t == NT - 1))
                    full(ins, ("KV4", c))
                pe.wait_ge(sparse_ready, 2)
                transposed("QT4", lambda t, h: ymq[:, t, h * P:(h + 1) * P])
                for key in (("KV4", 0), ("KV4", 1), ("QT4", 0), ("QT4", 1)):
                    in_sbuf(pe, key)
                for t in range(NT):
                    o = room(("y4", t))
                    for c in range(2):
                        ins = T.matmul(o[:, c * 136:(c + 1) * 136], qsT[:, c, tok(t)], kvm[:, c, :], start=True, stop=True)
                    full(ins, ("y4", t))
                for t in (2, 3):
                    in_sbuf(pe, ("y4", t))
                transposed("yT4", lambda t, h: y4[:, t, h * P:(h + 1) * P])
                in_sbuf(pe, ("yT4", 0))
                in_sbuf(pe, ("yT4", 1))
                token_major(lambda i: ("O4", i), yT4, W("w2p"))

                xT(5)
                in_sbuf(pe, ("xT5", 0))
                in_sbuf(pe, ("xT5", 1))
                router(5, W("l2r"))

                def expert_w(e, part):
                    return stream[:, (e + 2) % NSLOT, part * 512:(part + 1) * 512].rearrange("p (k n) -> p k n", k=2)

                def down5(e):
                    for f in range(2):
                        in_sbuf(pe, ("U5", e, f))
                    for i in range(2):
                        o = room(("Y5", e, i))
                        for t in (2 * i, 2 * i + 1):
                            ins = mm(o[:, (t % 2) * D:(t % 2 + 1) * D], lambda f: hid5[:, e % 2, f, tok(t)],
                                     lambda f: expert_w(e, 2)[:, f, :], range(2))
                            if t == NT - 1:
                                full(ins, ("Y5", e, i))
                        if i == 0:
                            full(ins, ("Y5", e, i))

                for e in range(10):
                    wait_chunk(pe, e + 2, b)
                    for f in range(2):
                        chan_major(("G5", e, f), expert_w(e, 0), f * P, xnT)
                        chan_major(("U5", e, f), expert_w(e, 1), f * P, xnT)
                    if e:
                        down5(e - 1)
                down5(9)

                xT(6)
                in_sbuf(pe, ("xT6", 0))
                in_sbuf(pe, ("xT6", 1))
                for h in range(2):
                    chan_major(("K6", 0, h), W("k1"), h * P, xnT)
                    chan_major(("Q6", 0, h), W("q1"), h * P, xnT)
                token_major(lambda i: ("V6", 0, i), xnT, W("v1"))
                for a in range(2):
                    for h in range(2):
                        in_sbuf(pe, ("K6", a, h))
                        in_sbuf(pe, ("Q6", a, h))
                    for t in range(NT):
                        n = (t + 1) * P if a == 0 else S
                        o = room(("S6", a, t))
                        ins = mm(o[:, 0:n], lambda k: Q6[:, k, tok(t)], lambda k: K6[a][:, k, 0:n], range(2), stop=(a == 1))
                        if a == 0:
                            ins = T.matmul(o[:, tok(t)], identb, KB("causal"), start=False, stop=True)
                        full(ins, ("S6", a, t))
                    for i in range(2):
                        in_sbuf(pe, ("V6", a, i))
                    for t in range(NT):
                        nb = t + 1 if a == 0 else NT
                        in_sbuf(pe, ("S6", a, t))
                        p = room(("P6", a, t))
                        for c in range(nb):
                            ins = T.transpose(p[:, tok(c)], P6[:, t, tok(c)], ident)
                        full(ins, ("P6", a, t))
                        if t % 2 == 0:
                            o = room(("O6", a, t // 2))
                        in_sbuf(pe, ("P6", a, t))
                        ins = mm(o[:, (t % 2) * D:(t % 2 + 1) * D], lambda c: PT6[:, t % 2, tok(c)],
                                 lambda c: V6[a][:, c, :], range(nb))
                        if t % 2:
                            full(ins, ("O6", a, t // 2))
                    if a == 0:
                        in_sbuf(pe, ("O6", 0, 0))
                        in_sbuf(pe, ("O6", 0, 1))
                        transposed("aT6", lambda t, h: att[:, t, h * P:(h + 1) * P])
                        in_sbuf(pe, ("aT6", 0))
                        in_sbuf(pe, ("aT6", 1))
                        for h in range(2):
                            chan_major(("Q6", 1, h), W("q2"), h * P, attT)
                pe.wait_ge(affine_ready, 2)
                transposed("nT6", lambda t, h: n2[:, t, h * P:(h + 1) * P])
                in_sbuf(pe, ("nT6", 0))
                in_sbuf(pe, ("nT6", 1))
                for m in range(2):
                    chan_major(("h6", m), W("f1"), m * P, attT)
                pe.wait_ge(h6_ready, 2)
                token_major(lambda i: ("f6", i), h6, W("f2"))

                pe.wait_ge(setup_done, 3)
                xT(7)
                in_sbuf(pe, ("xT7", 0))
                in_sbuf(pe, ("xT7", 1))
                for m in range(6):
                    chan_major(("G7", m), v3(wl3[:, 0:1536], 2), m * P, xnT)
                    chan_major(("U7", m), v3(wl3[:, 1536:3072], 2), m * P, xnT)
                for m in range(6):
                    in_sbuf(pe, ("U7", m))
                for i in range(2):
                    o = room(("Y7", i))
                    for t in (2 * i, 2 * i + 1):
                        ins = mm(o[:, (t % 2) * D:(t % 2 + 1) * D], lambda m: hid7[:, m, tok(t)],
                                 lambda m: v3(wl3[:, 3072:4608], 6)[:, m, :], range(6))
                    full(ins, ("Y7", i))
                meet(pe, b)

        @block.scalar
        def _(act):
            A = nc.scalar.activation
            act.wait_ge(const_loaded, 48)

            def taken(ins, key):
                ins.then_inc(psum_taken[bank(key)], 1)

            def copy(key, dst, src=None):
                o = got(act, key)
                taken(A(dst, o if src is None else src(o), ACT.Copy), key)

            with act.Fori(0, NB) as b:
                n_step = [0]

                def link(ins):
                    n_step[0] += 1
                    ins.then_inc(act_step, 1)
                    act.wait_ge(act_step, n_step[0])

                def focus_abs(w):
                    for i in range(2):
                        o = got(act, (w, i))
                        A(fa[:, 2 * i:2 * i + 2, :].rearrange("p t d -> p (t d)"), o, ACT.Abs, scale=0.01).then_inc(abs_ready, 1)

                def focus_rest(w, i):
                    in_sbuf(act, (w, 0))
                    in_sbuf(act, (w, 1))
                    A(fa, fb, ACT.Ln, bias=eps6).then_inc(log_ready, 1)
                    act.wait_ge(focus_in, i + 1)
                    for t in range(NT):
                        A(fb[:, t, :], fa[:, t, :], ACT.Exp, bias=fmax[:, t:t + 1],
                          accum_out=psumm[:, t:t + 1]).then_inc(focus_exp, 1)

                for g in range(NG):
                    o = got(act, ("F", g))
                    A(Kf[:, g, 0:P], o[:, 0:P], ACT.Copy)
                    A(Kf[:, g, P:P + 32], o[:, 0:32], ACT.Copy)
                    A(Kf[:, g, S + 32:S + 64], o[:, 0:32], ACT.Copy)
                    taken(A(Kf[:, g, KTILE[1]:KTILE[1] + 3 * P], o[:, P:S], ACT.Copy), ("F", g))
                copy(("xT0", 0), xnT[:, 0, :])

                def global_tile(u):
                    n = UNIT_TILES[u][0]
                    if PT_TILES[n][1] is None:
                        o = got(act, ("PT", n))
                        taken(A(PTs[0:32, n % 3, 0:2 * P], o[0:32, 0:2 * P], ACT.Copy), ("PT", n))

                def spread_sums(qt):
                    act.wait_ge(sums_ready, qt + 1)
                    if qt:
                        got(act, ("D", qt - 1))
                    A(rexp, rden[:, qt, :].unsqueeze(2).broadcast_to([P, NH, 32]), ACT.Copy).then_inc(sums_spread, 1)

                act.wait_ge(zeros_ready, 3)
                for key in [("Q", g) for g in range(NG)]:
                    in_sbuf(act, key)
                for j in range(HG // 2, HG):
                    r = slice(32 * j, 32 * j + 32)
                    A(Qz[0][r, :, j, :], Qr[r, :, 0:P], ACT.Copy).then_inc(queries_spread, 1)
                for u in range(NU):
                    qt, hp = divmod(u, NH // 2)
                    if u >= 9 and (u - 9) % (NH // 2) == 0:
                        spread_sums((u - 9) // (NH // 2))
                    if u >= 10 and (u - 10) % (NH // 2) == 0:
                        if u > 10:
                            in_sbuf(act, ("O", (u - 18) // (NH // 2)))
                        copy(("D", (u - 10) // (NH // 2)), rsum)
                    act.wait_ge(max_ready, u + 1)
                    for j in range(2):
                        h = 2 * hp + j
                        taken(A(probs[:, u % 2, j, 0:WIN[qt]], psb(("S", u, j))[:, 0:WIN[qt]], ACT.Exp,
                                bias=nm[:, u % 2, j:j + 1], accum_out=den[:, qt, h:h + 1]), ("S", u, j))
                    if u >= 1:
                        global_tile(u - 1)
                global_tile(NU - 1)
                spread_sums(NT - 1)
                in_sbuf(act, ("O", NT - 2))
                copy(("D", NT - 1), rsum)

                for t in range(NT):
                    act.wait_ge(xn_ready, NT + t + 1)
                    ins = A(hL[:, 0:D], xn[:, t, :], ACT.Square, accum_out=ss[:, t:t + 1])
                    if t < NT - 1:
                        link(ins)
                ins.then_inc(rms_sum, 1)
                act.wait_ge(rms_sum, 1)
                o = got(act, ("xT1", 0))
                A(xlT[:, 0, :], o, ACT.Copy, scale=col("lgam", 0))
                taken(A(xhT[:, 0, :], o, ACT.Copy, scale=col("hgam", 0)), ("xT1", 0))

                def gelu(key, dst, bias):
                    o = got(act, key)
                    taken(A(dst, o, ACT.Gelu, bias=bias), key)

                gelu(("h", "light"), hL, col("lb1"))
                act.wait_ge(lse_max, 1)
                link(A(hH[:, 7, :], krow, ACT.Exp, bias=nmax, accum_out=lsum))
                A(lnv, lsum, ACT.Ln, scale=1.0 / K_EFF).then_inc(ln_ready, 1)
                for r in range(ROUNDS):
                    act.wait_ge(ce_ready, r + 1)
                    A(ev, ce, ACT.Exp).then_inc(ev_ready, 1)
                    if r == 0:
                        for m in range(8):
                            gelu(("h", m), hH[:, m, :], col("hb1", m))
                    if r == 1:
                        focus_abs("k4")
                        for i in range(2):
                            copy(("v4", i), V2[:, 2 * i:2 * i + 2, :, 0:P],
                                 lambda o: o.rearrange("p (t c n) -> p t c n", t=2, c=2))
                        for h in range(2):
                            o = got(act, ("KT1", h))
                            taken(A(kr1[:, h, 32:32 + S], o, ACT.Identity, bias=col("bred", h)), ("KT1", h))
                    if r == 2:
                        focus_rest("k4", 0)
                    n = ITERS * (r + 1) - 1
                    if r == ROUNDS - 1:
                        got(act, "chain")
                        taken(A(lnv, psb("chain")[:, n:n + 1], ACT.Ln, scale=22026.465794806718), "chain")
                    else:
                        act.wait_ge(total_ready, n + 1)
                        A(lnv, psb("chain")[:, n:n + 1], ACT.Ln, scale=22026.465794806718).then_inc(ln_ready, 1)
                act.wait_ge(kcol_ready, 1)
                A(score, kcol, ACT.Exp).then_inc(score_ready, 1)

                copy(("xT2", 0), xnT[:, 0, :])
                for t in range(NT):
                    act.wait_ge(max1_ready, t + 1)
                    taken(A(P1[:, t, :], psb(("S1", t))[:, 0:KEYW], ACT.Exp, bias=nm4[:, t:t + 1],
                            accum_out=den4[:, t:t + 1]), ("S1", t))

                copy(("xT3", 0), xnT[:, 0, :])
                o = got(act, "RT3")
                taken(A(sc.rearrange("p t e -> p (t e)"), o[:, 0:32], ACT.Sigmoid), "RT3")
                for e in range(4):
                    o = got(act, ("G3", e))
                    if e >= 2:
                        in_sbuf(act, ("U3", e - 2))
                    taken(A(sg3[:, e % 2, :], o, ACT.Silu), ("G3", e))

                copy(("xT4", 0), xnT[:, 0, :])
                act.wait_ge(sparse_ready, 1)
                focus_abs("q4")
                focus_rest("q4", 1)
                for h in range(2):
                    copy(("K6", 1, h), K6[1][:, h, :])
                for i in range(2):
                    copy(("V6", 1, i), V6[1][:, 2 * i:2 * i + 2, :].rearrange("p t d -> p (t d)"))
                copy(("QT4", 0), qsT[:, 0, :])
                copy(("QT4", 1), qsT[:, 1, :])
                copy(("yT4", 0), yT4[:, 0, :])
                copy(("yT4", 1), yT4[:, 1, :])

                copy(("xT5", 0), xnT[:, 0, :])
                in_sbuf(act, "RT5")
                A(sc.rearrange("p t e -> p (t e)"), sc.rearrange("p t e -> p (t e)"), ACT.Exp).then_inc(router_exp, 1)
                for e in range(10):
                    for f in range(2):
                        o = got(act, ("G5", e, f))
                        if e:
                            in_sbuf(act, ("U5", e - 1, f))
                        taken(A(sg5[:, f, :], o, ACT.Silu), ("G5", e, f))

                copy(("xT6", 0), xnT[:, 0, :])
                scale = float(S) ** -0.5

                def q_scaled(a, h):
                    o = got(act, ("Q6", a, h))
                    taken(A(Q6[:, h, :], o, ACT.Copy, scale=scale), ("Q6", a, h))

                for h in range(2):
                    copy(("K6", 0, h), K6[0][:, h, :])
                    q_scaled(0, h)
                for i in range(2):
                    copy(("V6", 0, i), V6[0][:, 2 * i:2 * i + 2, :].rearrange("p t d -> p (t d)"))
                for a in range(2):
                    for t in range(NT):
                        n = (t + 1) * P if a == 0 else S
                        act.wait_ge(max6_ready, NT * a + t + 1)
                        taken(A(P6[:, t, 0:n], psb(("S6", a, t))[:, 0:n], ACT.Exp, bias=nm4[:, t:t + 1],
                                accum_out=den4[:, t:t + 1]), ("S6", a, t))
                    if a == 0:
                        copy(("aT6", 0), attT[:, 0, :])
                        copy(("aT6", 1), attT[:, 1, :])
                        for h in range(2):
                            q_scaled(1, h)
                copy(("nT6", 0), attT[:, 0, :])
                copy(("nT6", 1), attT[:, 1, :])
                for m in range(2):
                    o = got(act, ("h6", m))
                    taken(A(v6[:, m, :], o, ACT.Identity, bias=col("b1", m)), ("h6", m))

                copy(("xT7", 0), xnT[:, 0, :])
                for m in range(6):
                    o = got(act, ("G7", m))
                    if m >= 2:
                        in_sbuf(act, ("U7", m - 2))
                    taken(A(sg7[:, m % 2, :], o, ACT.Silu), ("G7", m))
                meet(act, b)

        @block.vector
        def _(dve):
            V = nc.vector
            dve.wait_ge(const_loaded, 48)

            def taken(ins, key):
                ins.then_inc(psum_taken[bank(key)], 1)

            with dve.Fori(0, NB) as b:
                n_step = [0]

                def link(ins):
                    n_step[0] += 1
                    ins.then_inc(dve_step, 1)
                    dve.wait_ge(dve_step, n_step[0])

                def flat(ap):
                    return ap.rearrange("p t d -> p (t d)")

                def two(o):
                    return o.rearrange("p (t d) -> p t d", t=2)

                def copy(key, dst):
                    taken(V.tensor_copy(dst, got(dve, key)), key)

                def norm(s, src, dst):
                    idx = LN_INDEX[s]
                    for t in range(NT):
                        n_step[0] += 1
                        V.bn_stats(stats[:, t, :], src[:, t, :]).then_inc(dve_step, 1)
                    for t in range(NT):
                        dve.wait_ge(dve_step, n_step[0] - NT + 1 + t)
                        ins = V.bn_aggr(mv[:, t, :], stats[:, t, :])
                    ins.then_inc(ln_stats, 1)
                    dve.wait_ge(ln_rstd, idx + 1)
                    for t in range(NT):
                        V.tensor_scalar(dst[:, t, :], src[:, t, :], mv[:, t, 0:1], rstd[:, t:t + 1],
                                        ALU.subtract, ALU.mult).then_inc(xn_ready, 1)

                dve.wait_ge(xn_loaded, (b + 1) * 16)
                norm(0, xn, xn)
                for g in range(NG):
                    o = got(dve, ("K", g))
                    taken(V.scalar_tensor_tensor(Kr[:, g, :], o, col("bk", g), K("rope"), ALU.add, ALU.mult), ("K", g))
                for i in range(2):
                    o = got(dve, ("V", i))
                    for t in (2 * i, 2 * i + 1):
                        ins = V.tensor_tensor(V0[:, t, :, 0:DK], two(o)[:, t % 2, :].rearrange("p (h n) -> p h n", h=NH),
                                              row("bv").rearrange("p (h n) -> p h n", h=NH), ALU.add)
                    taken(ins, ("V", i))
                copy(("xT0", 1), xnT[:, 1, :])
                for g in range(NG):
                    o = got(dve, ("Q", g))
                    taken(V.scalar_tensor_tensor(Qr[:, g, :], o, col("bq", g), K("rope"), ALU.add, ALU.mult), ("Q", g))

                def row_max(u):
                    for j in range(2):
                        got(dve, ("S", u, j))
                    V.reduce_max(nm[:, u % 2, :], ps[:, 2 * (u % 2):2 * (u % 2) + 2, 0:WIN[u // (NH // 2)]], AX_X,
                                 negate=True).then_inc(max_ready, 1)

                for g in range(NG):
                    in_sbuf(dve, ("Q", g))
                dve.wait_ge(zeros_ready, 3)
                for j in range(HG // 2):
                    r = slice(32 * j, 32 * j + 32)
                    V.tensor_copy(Qz[0][r, :, j, :], Qr[r, :, 0:P]).then_inc(queries_spread, 1)

                def out_tile(qt):
                    in_sbuf(dve, ("D", qt))
                    taken(V.tensor_tensor(OT[:, :, qt * P:(qt + 1) * P],
                                          got(dve, ("O", qt)).rearrange("p (g n) -> p g n", g=NG),
                                          rsum.rearrange("p (g n) -> p g n", g=NG), ALU.mult), ("O", qt))

                for u in range(NU + 2):
                    if u >= 9 and (u - 9) % (NH // 2) == 0:
                        qt = (u - 9) // (NH // 2)
                        for j in range(2):
                            in_sbuf(dve, ("S", u - 2, j))
                        V.reciprocal(rden[:, qt, :], den[:, qt, :]).then_inc(sums_ready, 1)
                    if u >= 2:
                        for n in UNIT_TILES[u - 2]:
                            if PT_TILES[n][1] is not None:
                                o = got(dve, ("PT", n))
                                taken(V.tensor_copy(PTs[:, n % 3, :], o), ("PT", n))
                    if u >= 10 and (u - 10) % (NH // 2) == 0:
                        out_tile((u - 10) // (NH // 2))
                    if u < NU:
                        row_max(u)
                out_tile(NT - 1)
                dve.wait_ge(x_biased, 1)

                def add_to_x(name):
                    for i in range(2):
                        o = got(dve, (name, i))
                        xs = flat(x[:, 2 * i:2 * i + 2, :])
                        taken(V.tensor_tensor(xs, xs, o, ALU.add), (name, i))
                    in_sbuf(dve, (name, 0))
                    in_sbuf(dve, (name, 1))

                add_to_x("Y0")

                norm(1, x, xn)
                for t in range(NT):
                    dve.wait_ge(xn_ready, NT + t + 1)
                    ins = V.tensor_tensor_reduce(out=hH[:, 0, 0:D], in0=xn[:, t, :], in1=row("rt"), scale=1.0,
                                                 scalar=0.0, op0=ALU.mult, op1=ALU.add, accum_out=scol[:, t:t + 1])
                    if t < NT - 1:
                        link(ins)
                ins.then_inc(scol_ready, 1)
                dve.wait_ge(scol_ready, 1)
                dve.wait_ge(rms_ready, 1)
                for t in range(NT):
                    V.tensor_scalar(xn[:, t, :], xn[:, t, :], rmsr[:, t:t + 1], None, ALU.mult).then_inc(xr_ready, 1)
                copy("R", srow)
                o = got(dve, ("xT1", 1))
                V.tensor_scalar(xlT[:, 1, :], o, col("lgam", 1), None, ALU.mult)
                taken(V.tensor_scalar(xhT[:, 1, :], o, col("hgam", 1), None, ALU.mult), ("xT1", 1))
                def focus(w, i):
                    for j in range(2):
                        o = two(got(dve, (w, j)))
                        dve.wait_ge(abs_ready, 2 * i + j + 1)
                        for t in (2 * j, 2 * j + 1):
                            ins = V.scalar_tensor_tensor(fb[:, t, :], o[:, t % 2, :], 1.0, fa[:, t, :], ALU.mult, ALU.max,
                                                         accum_out=fsum[:, t:t + 1])
                            if t % 2:
                                taken(ins, (w, j))
                            yield
                        in_sbuf(dve, (w, j))
                    link(V.tensor_scalar(fsum, fsum, -1.0 / D, -1e-6, ALU.mult, ALU.add))
                    yield
                    yield
                    dve.wait_ge(log_ready, i + 1)
                    link(V.tensor_scalar(fa, fa, col("focus"), None, ALU.mult))
                    yield
                    V.reduce_max(fmax, fa, AX_X, negate=True).then_inc(focus_in, 1)
                    yield
                    yield
                    yield
                    dve.wait_ge(focus_exp, NT * (i + 1))
                    link(V.reciprocal(fco, psumm))
                    link(V.tensor_tensor(fco, fco, fsum, ALU.mult))
                    yield
                    for t in range(NT):
                        ins = V.tensor_scalar(yin[:, t, :, 0:DK], fb[:, t, :].rearrange("p (h n) -> p h n", h=NH),
                                              fco[:, t:t + 1], None, ALU.mult)
                        yield
                    link(ins)
                    for t in range(NT):
                        for h in range(NH):
                            ins = V.max(top8[:, t, h, :], yin[:, t, h, 0:DK])
                            if h % 4 == 3 and (t, h) != (NT - 1, NH - 1):
                                yield
                    link(ins)
                    link(V.memset(top8[:, :, :, 5:8], 1.0))
                    yield
                    for t in range(NT):
                        for h in range(NH):
                            ins = V.match_replace(yout[:, t, h, :], top8[:, t, h, :], yin[:, t, h, :], 0.0)
                            if h % 4 == 3 and (t, h) != (NT - 1, NH - 1):
                                yield
                    link(ins)
                    V.tensor_copy(ym[i].rearrange("p t (h n) -> p t h n", h=NH),
                                  yout[:, :, :, 0:DK]).then_inc(sparse_ready, 1)

                got(dve, ("h", "light"))
                in_sbuf(dve, "R")
                link(V.tensor_scalar(krow, srow, LOG_N_K, None, ALU.min))
                V.reduce_max(nmax, krow, AX_X, negate=True).then_inc(lse_max, 1)
                dve.wait_ge(lse_max, 1)
                dve.wait_ge(ln_ready, 1)
                link(V.scalar_tensor_tensor(lsh[:, 0:1], lnv, -SHIFT, nmax, ALU.add, ALU.subtract))
                dve.wait_ge(ones_ready, 2)
                keys = focus("k4", 0)
                for r in range(ROUNDS):
                    V.tensor_scalar(ce, scol, lsh[:, r % 2:r % 2 + 1], 60.0, ALU.subtract, ALU.min).then_inc(ce_ready, 1)
                    dve.wait_ge(ev_ready, r + 1)
                    for i in range(ITERS):
                        n = r * ITERS + i
                        if i == 0:
                            level = EXP_SHIFT
                        else:
                            dve.wait_ge(total_ready, n)
                            level = psb("chain")[:, n - 1:n]
                        V.tensor_scalar(jc, ev, level, 0.0, ALU.min, ALU.add,
                                        accum_out=rs[:, n % 2:n % 2 + 1]).then_inc(rowsum_ready, 1)
                        if r >= 2:
                            next(keys, None)
                        dve.wait_ge(rowsum_ready, n + 1)
                    if r == ROUNDS - 1:
                        in_sbuf(dve, "chain")
                    else:
                        dve.wait_ge(ln_ready, r + 2)
                    link(V.scalar_tensor_tensor(lsh[:, (r + 1) % 2:(r + 1) % 2 + 1], lnv, -(SHIFT + 10.0),
                                                lsh[:, r % 2:r % 2 + 1], ALU.add, ALU.add))
                link(V.tensor_scalar(lfin, lsh[:, 0:1], SHIFT, None, ALU.add))
                link(V.tensor_scalar(krow, srow, lfin, 0.0, ALU.subtract, ALU.min))
                link(V.tensor_scalar(krow, krow, -103.97, None, ALU.max))
                link(V.tensor_scalar(kcol, scol, lfin, 0.0, ALU.subtract, ALU.min))
                V.tensor_scalar(kcol, kcol, -103.97, None, ALU.max).then_inc(kcol_ready, 1)
                dve.wait_ge(kcol_ready, 1)
                dve.wait_ge(setup_done, 2)
                for t in range(NT):
                    w = (NT - 1 - t) * P
                    link(V.scalar_tensor_tensor(jrow, krow, kcol[:, t:t + 1], KB("lt")[:, w:w + S], ALU.is_ge, ALU.mult,
                                                accum_out=rk1[:, t:t + 1]))
                    link(V.scalar_tensor_tensor(jrow, krow, kcol[:, t:t + 1], KB("ge")[:, w:w + S], ALU.is_gt, ALU.mult,
                                                accum_out=rk2[:, t:t + 1]))
                link(V.tensor_tensor(rk1, rk1, rk2, ALU.add))
                link(V.tensor_scalar(rk1, rk1, float(TOP_HEAVY), None, ALU.is_lt))
                dve.wait_ge(score_ready, 1)
                link(V.tensor_scalar(wgt, score, -1.0, 1.0, ALU.mult, ALU.add))
                link(V.tensor_tensor(wgt, wgt, score, ALU.add))
                link(V.tensor_tensor(wgt, wgt, rk1, ALU.mult))
                dve.wait_ge(x_biased, 2)
                add_to_x("yl")
                for i in range(2):
                    o = two(got(dve, ("yh", i)))
                    for t in (2 * i, 2 * i + 1):
                        link(V.tensor_tensor(th, o[:, t % 2, :], row("hb2"), ALU.add))
                        ins = V.scalar_tensor_tensor(x[:, t, :], th, wgt[:, t:t + 1], x[:, t, :], ALU.mult, ALU.add)
                        if t % 2:
                            taken(ins, ("yh", i))
                        else:
                            link(ins)
                    in_sbuf(dve, ("yh", i))

                norm(2, x, xn)
                copy(("xT2", 1), xnT[:, 1, :])
                for t in range(NT):
                    o = got(dve, ("S1", t))
                    V.reduce_max(nm4[:, t:t + 1], o[:, 0:KEYW], AX_X, negate=True).then_inc(max1_ready, 1)
                for t in range(NT):
                    o = got(dve, ("PT1", t))
                    V.tensor_copy(PT1[:, t, 0:P], o[:, 0:P])
                    taken(V.tensor_copy(PT1[0:64, t, P:2 * P], o[0:64, P:2 * P]), ("PT1", t))

                def weighted(key_of, scalar, dst=x):
                    for i in range(2):
                        o = two(got(dve, key_of(i)))
                        for t in (2 * i, 2 * i + 1):
                            ins = V.scalar_tensor_tensor(dst[:, t, :], o[:, t % 2, :], scalar(t), dst[:, t, :],
                                                         ALU.mult, ALU.add)
                        taken(ins, key_of(i))
                    in_sbuf(dve, key_of(1))

                link(V.reciprocal(rden4, den4))
                weighted(lambda i: ("O1", i), lambda t: rden4[:, t:t + 1])
                in_sbuf(dve, ("O1", 0))

                norm(3, x, xn)
                copy(("xT3", 1), xnT[:, 1, :])
                in_sbuf(dve, ("xT3", 0))
                in_sbuf(dve, ("xT3", 1))
                in_sbuf(dve, "RT3")

                def top2():
                    for t in range(NT):
                        ins = V.max(t8[:, t, :], tb[:, t, 0:8])
                    link(ins)
                    link(V.memset(t8[:, :, 2:8], BIG))
                    for t in range(NT):
                        ins = V.match_replace(tr[:, t, 0:14], t8[:, t, :], tb[:, t, 0:14], -BIG)
                    link(ins)
                    link(V.tensor_scalar(tr[:, :, 0:8], tr[:, :, 0:8], -2.9e38, None, ALU.is_le))
                    link(V.tensor_tensor(cw[:, :, 0:8], tr[:, :, 0:8], sc, ALU.mult))

                link(V.tensor_tensor(tb[:, :, 0:8], sc, row("rbias", NT), ALU.add))
                top2()
                link(V.reduce_sum(c46, cw[:, :, 0:8], AX_X))
                link(V.tensor_scalar(c46, c46, 1e-9, None, ALU.add))
                link(V.reciprocal(c46, c46))
                V.tensor_tensor(cw[:, :, 0:8], cw[:, :, 0:8], c46.unsqueeze(2).broadcast_to([P, NT, 8]), ALU.mult).then_inc(cw_ready, 1)
                dve.wait_ge(cw_ready, 1)
                for h in range(2):
                    link(V.tensor_scalar(conv[:, h, :], xnT[:, h, :], col("convw", 4 * h + 3), None, ALU.mult))
                    for k in range(1, 4):
                        ins = V.scalar_tensor_tensor(conv[:, h, k:S], xnT[:, h, 0:S - k], col("convw", 4 * h + 3 - k),
                                                     conv[:, h, k:S], ALU.mult, ALU.add)
                        if h == 1 and k == 3:
                            ins.then_inc(conv_ready, 1)
                        else:
                            link(ins)

                def gated(gkey, ukey, sg, dst):
                    in_sbuf(dve, gkey)
                    o = got(dve, ukey)
                    next(keys, None)
                    taken(V.tensor_tensor(dst, sg, o, ALU.mult), ukey)

                dve.wait_ge(extra_ready, NT)
                for e in range(4):
                    gated(("G3", e), ("U3", e), sg3[:, e % 2, :], hid3[:, e % 2, :])
                    if e == 0:
                        for i in range(2):
                            o = got(dve, ("CT3", i))
                            taken(V.tensor_tensor(flat(x[:, 2 * i:2 * i + 2, :]), flat(extra[:, 2 * i:2 * i + 2, :]), o,
                                                  ALU.add), ("CT3", i))
                            in_sbuf(dve, ("CT3", i))
                    else:
                        weighted(lambda i: ("Y3", e - 1, i), lambda t: cw[:, t, e - 1:e])
                    for _ in range(5):
                        next(keys, None)
                for _ in keys:
                    pass
                weighted(lambda i: ("Y3", 3, i), lambda t: cw[:, t, 3:4])
                in_sbuf(dve, ("Y3", 3, 0))

                norm(4, x, xn)
                copy(("xT4", 1), xnT[:, 1, :])
                for _ in focus("q4", 1):
                    pass
                dve.wait_ge(sparse_ready, 2)
                for c in range(2):
                    o = got(dve, ("KV4", c))
                    bm = K("bmask")
                    V.scalar_tensor_tensor(kvm[:, c, 0:P], o[:, 0:P], 1.0 / S, bm[:, 0:P], ALU.mult, ALU.mult)
                    taken(V.tensor_scalar(kvm[:, c, P:136], bm[:, P:136], o[:, P:P + 1], 1.0 / S, ALU.mult, ALU.mult),
                          ("KV4", c))
                for t in range(NT):
                    o = got(dve, ("y4", t))[:, 0:272].rearrange("p (c n) -> p c n", c=2)
                    link(V.tensor_scalar(zr, o[:, :, P:136], 1e-6, None, ALU.add))
                    link(V.reciprocal(zr, zr))
                    taken(V.tensor_tensor(y4[:, t, :].rearrange("p (c h n) -> p c h n", c=2, h=8),
                                          o[:, :, 0:P].rearrange("p c (h n) -> p c h n", h=8),
                                          zr.unsqueeze(3).broadcast_to([P, 2, 8, DK]), ALU.mult), ("y4", t))
                    in_sbuf(dve, ("y4", t))
                add_to_x("O4")

                norm(5, x, xn)
                copy(("xT5", 1), xnT[:, 1, :])
                o = got(dve, "RT5")[:, 0:32].rearrange("p (t e) -> p t e", t=NT)
                link(V.reduce_max(c46, o, AX_X, negate=True))
                taken(V.tensor_tensor(sc, o, c46.unsqueeze(2).broadcast_to([P, NT, 8]), ALU.add), "RT5")
                in_sbuf(dve, "RT5")
                dve.wait_ge(router_exp, 1)
                link(V.reduce_sum(c46, sc, AX_X))
                link(V.reciprocal(c46, c46))
                link(V.tensor_tensor(sc, sc, c46.unsqueeze(2).broadcast_to([P, NT, 8]), ALU.mult))
                link(V.tensor_copy(tb[:, :, 0:8], sc))
                top2()
                for e in range(10):
                    for f in range(2):
                        gated(("G5", e, f), ("U5", e, f), sg5[:, f, :], hid5[:, e % 2, f, :])
                    if e:
                        weighted(lambda i: ("Y5", e - 1, i), lambda t: cw[:, t, e - 1:e])
                weighted(lambda i: ("Y5", 9, i), lambda t: cw[:, t, 9:10])
                in_sbuf(dve, ("Y5", 9, 0))

                norm(6, x, xn)
                copy(("xT6", 1), xnT[:, 1, :])
                for a in range(2):
                    for t in range(NT):
                        n = (t + 1) * P if a == 0 else S
                        o = got(dve, ("S6", a, t))
                        V.reduce_max(nm4[:, t:t + 1], o[:, 0:n], AX_X, negate=True).then_inc(max6_ready, 1)
                    res = xn if a == 0 else n1
                    if a == 1:
                        dve.wait_ge(affine_ready, 1)
                    for t in range(NT):
                        nb = t + 1 if a == 0 else NT
                        o = got(dve, ("P6", a, t))
                        taken(V.tensor_copy(PT6[:, t % 2, 0:nb * P], o[:, 0:nb * P]), ("P6", a, t))
                        if t % 2:
                            i = t // 2
                            link(V.reciprocal(rden4[:, 2 * i:2 * i + 2], den4[:, 2 * i:2 * i + 2]))
                            o = two(got(dve, ("O6", a, i)))
                            for tt in (2 * i, 2 * i + 1):
                                if a == 0:
                                    ins = V.tensor_scalar(att[:, tt, :], o[:, tt % 2, :], rden4[:, tt:tt + 1], None, ALU.mult)
                                else:
                                    ins = V.scalar_tensor_tensor(n2[:, tt, :], o[:, tt % 2, :], rden4[:, tt:tt + 1],
                                                                 n1[:, tt, :], ALU.mult, ALU.add)
                            taken(ins, ("O6", a, i))
                            in_sbuf(dve, ("O6", a, i))
                    if a == 0:
                        link(V.tensor_tensor(n1, att, xn[:, :, :], ALU.add))
                        norm("6a", n1, n1)
                    else:
                        norm("6b", n2, n2)
                for m in range(2):
                    in_sbuf(dve, ("h6", m))
                    V.scalar_tensor_tensor(h6[:, m, :], v6[:, m, :], 0.2, v6[:, m, :], ALU.mult, ALU.max).then_inc(h6_ready, 1)
                dve.wait_ge(affine_ready, 3)
                for i in range(2):
                    o = two(got(dve, ("f6", i)))
                    taken(V.tensor_tensor(n1[:, 2 * i:2 * i + 2, :], o, n2[:, 2 * i:2 * i + 2, :], ALU.add), ("f6", i))
                in_sbuf(dve, ("f6", 0))
                in_sbuf(dve, ("f6", 1))
                norm("6c", n1, n1)
                dve.wait_ge(affine_ready, 4)
                link(V.scalar_tensor_tensor(x[:, :, :], n1, 0.0, x[:, :, :], ALU.max, ALU.add))

                norm(7, x, xn)
                copy(("xT7", 1), xnT[:, 1, :])
                for m in range(6):
                    gated(("G7", m), ("U7", m), sg7[:, m % 2, :], hid7[:, m, :])
                add_to_x("Y7")
                meet(dve, b)


LOG_N_K = 0.5753641449035618
SHIFT = 20.0
EXP_SHIFT = 485165195.4097903


def _constants(np):
    c = {}
    inv = (1.0 / 10000.0 ** (np.arange(0, DK, 2, dtype=np.float32) / np.float32(DK))).astype(np.float32)
    f = np.arange(S, dtype=np.float32)[:, None] * inv[None, :]
    emb = np.concatenate([f, f], 1)
    cos, sin = np.cos(emb).astype(np.float32), np.sin(emb).astype(np.float32)
    rope = np.zeros((P, S), np.float32)
    for j in range(HG):
        rope[32 * j:32 * j + 16] = cos.T
        rope[32 * j + 16:32 * j + 24] = -sin.T[0:8]
        rope[32 * j + 24:32 * j + 32] = sin.T[8:16]
    c["rope"] = rope * np.float32(0.5)
    r = np.arange(P)
    c["fold"] = ((r[:, None] // 32 == r[None] // 32) & (r[:, None] % 16 == r[None] % 16)).astype(np.float32)
    c["ident"] = np.eye(P, dtype=np.float32)
    bm = np.zeros((P, 136), np.float32)
    bm[:, :P] = r[:, None] // DK == r[None] // DK
    bm[:, P:] = r[:, None] // DK == np.arange(8)[None]
    c["bmask"] = bm
    i = np.arange(S)[:, None]
    j = np.arange(S)[None]
    blocked = (np.abs(i - j) > 128) | (j > i)
    blocked &= ~((i < 16) | (j < 16))
    m = np.where(blocked, -1e30, 0.0)
    none = np.full((P, 32), -1e30)
    g = [np.concatenate([m[qt * P:(qt + 1) * P, 0:16], none[:, 0:16]], 1) for qt in range(NT)]
    parts = [m[0:128], m[128:256, 0:128], none, m[128:256, 128:256],
             g[2], m[256:384, 128:384], m[384:512, 256:512], g[3]]
    c["mask0"] = np.concatenate(parts, 1)
    band = []
    for t in range(NT):
        q = t * P + r[:, None]
        k = t * P - 32 + np.arange(KEYW)[None]
        band.append(np.where((np.abs(q - k) <= 20) & (k >= 0) & (k < S), 0.0, -1e8))
    c["band"] = np.concatenate(band, 1)
    c["causal"] = np.where(r[None] > r[:, None], -1e30, 0.0)
    c["identb"] = np.eye(P)
    lt = (np.arange(896)[None] - 384 < r[:, None])
    c["lt"], c["ge"] = lt * 1.0, 1.0 - lt
    a = np.concatenate([c[n] for n, _ in CONST], 1).astype(np.float32)
    z = np.concatenate([c[n] for n, _ in CONSTB], 1).astype(np.float32)
    return a, z


def _layout(np, i):
    def rows_of(w):
        return w.reshape(-1, P, w.shape[1]).transpose(1, 0, 2).reshape(P, -1)

    def padded_heads(w):
        h = w.reshape((NH, DK) + w.shape[1:])
        partner = np.concatenate([h[:, 1::2], h[:, ::2]], 1)
        return np.concatenate([h, partner], 1).reshape((NH * 32,) + w.shape[1:])

    def zero_rows(w):
        h = w.reshape(NH, DK, D)
        return np.concatenate([h, np.zeros_like(h)], 1).reshape(NH * 32, D)

    def reversed_heads(w):
        return w.reshape(NH, DK, D)[:, ::-1].reshape(D, D)

    w = {"wq": rows_of(padded_heads(i["L0_xattn_wq"]).T), "wk": rows_of(padded_heads(i["L0_xattn_wk"]).T),
         "wv": rows_of(i["L0_xattn_wv"].T), "wo": rows_of(zero_rows(i["L0_xattn_wo"].T)),
         "lw1": rows_of(i["L0_ffn_light_w1"]), "lw2": rows_of(i["L0_ffn_light_w2"]),
         "wred": rows_of(i["L1_xattn_W_reduce"].T), "l1r": rows_of(i["L1_ffn_Wr"]),
         "l1g": np.concatenate([rows_of(e) for e in i["L1_ffn_Wg"]], 1),
         "l1u": np.concatenate([rows_of(e) for e in i["L1_ffn_Wu"]], 1),
         "l1d": np.concatenate([rows_of(e) for e in i["L1_ffn_Wd"]], 1),
         "w2q": rows_of(reversed_heads(i["L2_xattn_Wq"]).T), "w2k": rows_of(reversed_heads(i["L2_xattn_Wk"]).T),
         "w2v": rows_of(i["L2_xattn_Wv"].T), "w2p": rows_of(i["L2_xattn_Wp"].T), "l2r": rows_of(i["L2_ffn_router_w"]),
         "k1": rows_of(i["L3_xattn_Wk1"]), "q1": rows_of(i["L3_xattn_Wq1"]), "v1": rows_of(i["L3_xattn_Wv1"]),
         "k2": rows_of(i["L3_xattn_Wk2"]), "q2": rows_of(i["L3_xattn_Wq2"]), "v2": rows_of(i["L3_xattn_Wv2"]),
         "f1": rows_of(i["L3_xattn_W1"]), "f2": rows_of(i["L3_xattn_W2"])}
    heavy1, heavy2 = i["L0_ffn_heavy_w1"], i["L0_ffn_heavy_w2"]
    chunks = [np.concatenate([rows_of(heavy1[:, c * 512:(c + 1) * 512]), rows_of(heavy2[c * 512:(c + 1) * 512])], 1)
              for c in range(2)]

    def expert(g, u, d):
        z = np.zeros((P, CHUNK - 1536), g.dtype)
        return np.concatenate([rows_of(g), rows_of(u), rows_of(d), z], 1)

    chunks += [expert(i["L2_ffn_gate_w"][e], i["L2_ffn_up_w"][e], i["L2_ffn_down_w"][e]) for e in range(8)]
    chunks += [expert(i["L2_ffn_shared_gate_w"][:, f], i["L2_ffn_shared_up_w"][:, f], i["L2_ffn_shared_down_w"][f])
               for f in (slice(0, 256), slice(256, 512))]
    c = {"bq": padded_heads(i["L0_xattn_bq"]).reshape(4, P).T, "bk": padded_heads(i["L0_xattn_bk"]).reshape(4, P).T,
         "lgam": i["L0_ffn_light_gamma"].reshape(2, P).T, "hgam": i["L0_ffn_heavy_gamma"].reshape(2, P).T,
         "lb1": i["L0_ffn_light_b1"].reshape(1, P).T, "hb1": i["L0_ffn_heavy_b1"].reshape(8, P).T,
         "bred": i["L1_xattn_b_reduce"].reshape(2, P).T,
         "convw": i["L1_ffn_conv_w"].reshape(4, 2, P).transpose(2, 1, 0).reshape(P, 8),
         "b1": i["L3_xattn_b1"].reshape(2, P).T,
         "focus": np.broadcast_to(np.reshape(i["L2_xattn_focusing_factor"], (1, 1)), (P, 1))}
    r = {"bv": i["L0_xattn_bv"], "bo": i["L0_xattn_bo"], "lb2": i["L0_ffn_light_b2"], "hb2": i["L0_ffn_heavy_b2"],
         "convb": i["L1_ffn_conv_b"], "b2": i["L3_xattn_b2"], "gamma": i["L3_xattn_gamma"],
         "beta": i["L3_xattn_beta"], "rt": i["L0_ffn_routing_token"], "rbias": i["L1_ffn_router_bias"]}
    const, constb = _constants(np)
    def again(a):
        return np.concatenate([a, a[:1]])

    ctx = again(i["ctx_1024"])
    shifted = np.zeros((NB + 1, 5 * P, D), ctx.dtype)
    shifted[:, 32:32 + S] = ctx
    return {
        "x": again(i["x"]).reshape(-1, NT, P, D).transpose(0, 2, 1, 3).reshape(-1, NT * D),
        "ctxT": ctx.reshape(-1, S, 2, P).transpose(0, 3, 2, 1).reshape(-1, 2 * S),
        "ctxs": shifted.reshape(-1, 5, P, D).transpose(0, 2, 1, 3).reshape(-1, 5 * D),
        "weights": np.concatenate([w[n] for n, _ in WEIGHTS], 1),
        "stream": np.concatenate(chunks, 0),
        "wint": np.concatenate([rows_of(i["L3_ffn_w_gate"].T), rows_of(i["L3_ffn_w_up"].T),
                                rows_of(i["L3_ffn_w_down"].T)], 1),
        "cols": np.concatenate([c[n] for n, _ in COLS], 1),
        "rows": np.broadcast_to(np.concatenate([r[n] for n, _ in ROWS])[None], (P, sum(n for _, n in ROWS))),
        "const": const, "constb": constb}


def kernel(**inputs):
    import numpy as _np
    import concourse.bacc as _bacc
    from concourse import mybir as _mybir
    from concourse.bass_utils import run_bass_kernel_spmd as _run

    nc = _bacc.Bacc("TRN2", target_bir_lowering=False, num_devices=1)
    arrays, args = {}, []
    for name, a in _layout(_np, {k: _np.asarray(v) for k, v in inputs.items()}).items():
        a = _np.ascontiguousarray(a)
        arrays[f"in_{name}"] = a
        args.append(nc.dram_tensor(f"in_{name}", a.shape, _mybir.dt.from_np(a.dtype), kind="ExternalInput").ap())
    args.append(nc.dram_tensor("out_x", (NB * P, NT * D), _mybir.dt.float32, kind="ExternalOutput").ap())
    network(nc, *args)
    r = _run(nc, [arrays], core_ids=[0]).results[0]["out_x"]
    return r.reshape(NB, P, NT, D).transpose(0, 2, 1, 3).reshape(NB, S, D)
```

```python
from contextlib import ExitStack

import concourse.bass as bass
from concourse import mybir

F32 = mybir.dt.float32
BF16 = mybir.dt.bfloat16
I32 = mybir.dt.int32
ALU = mybir.AluOpType
ACT = mybir.ActivationFunctionType
AX_X = mybir.AxisListType.X

P = 128
NB, S, D = 4, 512, 256
NT = S // P
NH, DK = 16, 16
HG = 4
NG = NH // HG
BIG = 3.0e38
K_EFF = 256 * 9.0 / 8.0
TOP_HEAVY = 256
ROUNDS, ITERS = 4, 12
KEYW = 192
KEYPAD = 640
KROW = S + 64
KTILE = (0, P + 32, 2 * P + 32, 3 * P + 32)
WSTART = (0, 0, P, 2 * P + 32)
WIN = (512, 288, 288, 288)
WOFF = (0, 512, 800, 1088)
WBLOCKS = ((0, 128, 256, 384), (0, 160), (32, 160), (0, 128))
WGLOBAL = (None, None, 0, 256)
FIRST = P + 16 * (NT - 1)
NSLOT = 3
CHUNK = 2048

WEIGHTS = [("wk", 1024), ("wv", 512), ("wq", 1024), ("wo", 1024),
           ("lw1", 256), ("lw2", 256),
           ("wred", 512), ("l1r", 16), ("l1g", 1024), ("l1u", 1024), ("l1d", 1024),
           ("w2q", 512), ("w2k", 512), ("w2v", 512), ("w2p", 512), ("l2r", 16),
           ("k1", 512), ("q1", 512), ("v1", 512), ("k2", 512), ("q2", 512), ("v2", 512),
           ("f1", 512), ("f2", 512)]
WGROUPS = [("wk", "wv"), ("wq", "wo"), ("lw1", "lw2"), ("wred", "l1d"), ("w2q", "l2r"), ("k1", "f2")]
COLS = [("bq", 4), ("bk", 4), ("lgam", 2), ("hgam", 2), ("lb1", 1), ("hb1", 8), ("bred", 2),
        ("convw", 8), ("b1", 2), ("focus", 1)]
ROWS = [("bv", 256), ("bo", 256), ("lb2", 256), ("hb2", 256), ("convb", 256), ("b2", 256),
        ("gamma", 256), ("beta", 256), ("rt", 256), ("rbias", 8)]
CONST = [("rope", 512), ("fold", 128), ("ident", 128), ("bmask", 136)]
CONSTB = [("identb", 128), ("mask0", 1376), ("causal", 128), ("band", 4 * KEYW), ("lt", 896), ("ge", 896)]
FIRSTB = 128 + 1376 + 128 + 4 * KEYW


def offsets(table):
    at, out = 0, {}
    for name, n in table:
        out[name] = (at, n)
        at += n
    return out, at


NU = NT * NH // 2


def tiles_of_unit(u):
    qt = u // (NH // 2)
    return ([None] if qt >= 2 else []) + [(0, 1)]


PT_TILES = [(u, heads) for u in range(NU) for heads in tiles_of_unit(u)]
UNIT_TILES = [[n for n, (v, _) in enumerate(PT_TILES) if v == u] for u in range(NU)]


def psum_plan():
    out = []

    def use(key, bank):
        out.append((key, bank))

    def pair(name, banks):
        for i, bank in enumerate(banks):
            use((name, i), bank)

    use(("K", 0), 2)
    for g in range(NG):
        if g < NG - 1:
            use(("K", g + 1), 2 + (g + 1) % 2)
        else:
            pair("xT0", (0, 1))
        use(("F", g), 4 + g % 2)
    for g in range(NG):
        use(("Q", g), (2, 3, 0, 1)[g])
    pair("V", (6, 7))
    for u in range(NU + 2):
        if u >= 3 and (u - 3) % (NH // 2) == 0:
            use(("O", (u - 3) // (NH // 2)), 7)
        if 2 <= u:
            for n in UNIT_TILES[u - 2]:
                use(("PT", n), 4 + n % 3)
        if u < NU:
            for j in range(2):
                use(("S", u, j), 2 * (u % 2) + j)
        if u >= 9 and (u - 9) % (NH // 2) == 0:
            use(("D", (u - 9) // (NH // 2)), 4 + (UNIT_TILES[u - 2][-1] + 2) % 3)
    pair("Y0", (0, 1))
    pair("v4", (4, 5))
    pair("KT1", (6, 7))
    use("R", 2)
    pair("xT1", (0, 1))
    use(("h", "light"), 3)
    use("chain", 2)
    pair("k4", (6, 7))
    for m in range(8):
        use(("h", m), (0, 1, 3)[m % 3])
    pair("yl", (4, 5))
    pair("yh", (6, 7))
    pair("xT2", (0, 1))
    for t in range(NT):
        use(("S1", t), 4 + t)
    for t in range(NT):
        use(("PT1", t), 2 + t % 2)
    pair("O1", (0, 1))
    pair("xT3", (0, 1))
    use("RT3", 7)
    for e in range(4):
        use(("G3", e), 2 + e % 2)
        use(("U3", e), 4 + e % 2)
        if e == 0:
            pair("CT3", (6, 0))
        else:
            for i in range(2):
                use(("Y3", e - 1, i), (1, 6, 0)[(2 * e + i) % 3])
    for i in range(2):
        use(("Y3", 3, i), (1, 6, 0)[(8 + i) % 3])
    pair("xT4", (0, 1))
    pair("q4", (6, 7))
    for h in range(2):
        use(("K6", 1, h), 4 + h)
    for i in range(2):
        use(("V6", 1, i), i)
    pair("KV4", (2, 3))
    pair("QT4", (4, 5))
    for t in range(NT):
        use(("y4", t), 6 + t % 2)
    pair("yT4", (0, 1))
    pair("O4", (2, 3))
    pair("xT5", (0, 1))
    use("RT5", 7)
    for e in range(10):
        for f in range(2):
            use(("G5", e, f), 2 + f)
            use(("U5", e, f), 4 + f)
        if e:
            for i in range(2):
                use(("Y5", e - 1, i), (6, 7, 0, 1)[(2 * e + i) % 4])
    for i in range(2):
        use(("Y5", 9, i), (6, 7, 0, 1)[(20 + i) % 4])
    pair("xT6", (0, 1))
    for h in range(2):
        use(("K6", 0, h), 2 + h)
        use(("Q6", 0, h), 4 + h)
    for i in range(2):
        use(("V6", 0, i), 6 + i)
    for a in range(2):
        for t in range(NT):
            use(("S6", a, t), 2 + t)
        for t in range(NT):
            use(("P6", a, t), 6 + t % 2)
        for i in range(2):
            use(("O6", a, i), i)
        if a == 0:
            pair("aT6", (2, 3))
            for h in range(2):
                use(("Q6", 1, h), 4 + h)
    pair("nT6", (6, 7))
    for m in range(2):
        use(("h6", m), 2 + m)
    pair("f6", (4, 5))
    pair("xT7", (0, 1))
    for m in range(6):
        use(("G7", m), 2 + m % 2)
        use(("U7", m), 4 + m % 2)
    pair("Y7", (6, 7))
    count, where = [0] * 8, {}
    for key, bank in out:
        assert key not in where, key
        where[key] = (bank, count[bank])
        count[bank] += 1
    return where


PLAN = psum_plan()
LN_INDEX = {0: 0, 1: 1, 2: 2, 3: 3, 4: 4, 5: 5, 6: 6, "6a": 7, "6b": 8, "6c": 9, 7: 10}


def network(nc, x_in, ctxT_in, ctxs_in, w_in, stream_in, wint_in, cols_in, rows_in, const_in, constb_in, out):
    stack = ExitStack()
    with stack:
        def sb(name, shape, dt=F32):
            return stack.enter_context(nc.sbuf_tensor(name, shape, dt))

        def sem(name):
            return stack.enter_context(nc.semaphore(name))

        woff, wn = offsets(WEIGHTS)
        coff, cn = offsets(COLS)
        roff, rn = offsets(ROWS)
        koff, kn = offsets(CONST)
        boff, bn = offsets(CONSTB)
        weights = sb("weights", [P, wn])
        wint = sb("wint", [P, 4608], I32)
        wl3 = wint[:, :].bitcast(F32)
        stream = sb("stream", [P, NSLOT, CHUNK])
        cols = sb("cols", [P, cn])
        rows = sb("rows", [P, rn])
        const = sb("const", [P, kn])
        constb = sb("constb", [P, bn], BF16)

        def W(name, k=2):
            at, n = woff[name]
            return weights[:, at:at + n].rearrange("p (k n) -> p k n", k=k)

        def col(name, i=0):
            return cols[:, coff[name][0] + i:coff[name][0] + i + 1]

        def row(name, n=1):
            at, w = roff[name]
            r = rows[:, at:at + w]
            return r if n == 1 else r.unsqueeze(1).broadcast_to([P, n, w])

        def K(name):
            at, n = koff[name]
            return const[:, at:at + n]

        def KB(name):
            at, n = boff[name]
            return constb[:, at:at + n]

        x = sb("x", [P, NT, D])
        xn = sb("xn", [P, NT, D])
        xnT_ = sb("xnT", [P, 2, 4 + S])
        xnT = xnT_[:, :, 4:4 + S]
        ctxT = sb("ctxT", [P, 2, S])
        ctxs = sb("ctxs", [P, 5, D])
        small = sb("small", [P, 464])
        onesk = sb("onesk", [P, P])
        EVEN, ODD = 9984, 7168
        even = sb("even", [P, EVEN])
        odd = sb("odd", [P, ODD])
        at_small = [0]

        def sm(n, shape=None):
            a = small[:, at_small[0]:at_small[0] + n]
            at_small[0] += n
            assert at_small[0] <= 464
            return a if shape is None else a.rearrange("p (a b) -> p a b", a=shape)

        class Area:
            def __init__(self, t, size):
                self.t, self.size, self.at = t, size, 0

            def take(self, n):
                a = self.t[:, self.at:self.at + n]
                self.at += n
                assert self.at <= self.size, self.at
                return a

        def v3(ap, a):
            return ap.rearrange("p (a b) -> p a b", a=a)

        eps6 = sm(1)
        mhalf = sm(NT)
        stats = sm(NT * 6, NT)
        mv = sm(NT * 2, NT)
        var = sm(NT)
        rstd = sm(NT)
        nm = sm(4, 2)
        rden4 = sm(NT)
        nm4 = sm(NT)
        den4 = sm(NT)
        ss = sm(NT)
        rmsr = sm(NT)
        scol = sm(NT)
        kcol = sm(NT)
        nmax = sm(1)
        lsum = sm(1)
        lnv = sm(1)
        lspare = sm(1)
        lsh = sm(2)
        lfin = sm(1)
        ce = sm(NT)
        ev = sm(NT)
        jc = sm(NT)
        rs = sm(2)
        rk1 = sm(NT)
        rk2 = sm(NT)
        score = sm(NT)
        wgt = sm(NT)
        sc = sm(32, NT)
        tb = sm(64, NT)
        t8 = sm(32, NT)
        tr = sm(64, NT)
        cw = sm(40, NT)
        c46 = sm(NT)
        fsum = sm(NT)
        psumm = sm(NT)
        fmax = sm(NT)
        fco = sm(NT)

        ar = Area(even, EVEN)
        Kf = v3(ar.take(NG * KROW), NG)
        Qr = v3(ar.take(NG * S), NG)
        V0 = ar.take(NT * NH * 32).rearrange("p (t h n) -> p t h n", t=NT, h=NH)
        probs = ar.take(4 * S).rearrange("p (a b c) -> p a b c", a=2, b=2)
        Kr = probs.rearrange("p a b c -> p (a b) c")
        PTs = v3(ar.take(3 * S), 3)
        OT = Qr
        ar = Area(odd, ODD)
        Qz = [ar.take(NG * HG * P).rearrange("p (g h n) -> p g h n", g=NG, h=HG) for _ in range(2)]
        rsum = ar.take(S)
        rexp = v3(ar.take(S), NH)
        den = v3(ar.take(NT * NH), NT)
        rden = v3(ar.take(NT * NH), NT)
        last_staged = ar.take(bn - FIRSTB)
        ar = Area(even, EVEN)
        kr1 = v3(ar.take(2 * KEYPAD), 2)
        P1 = v3(ar.take(NT * KEYW), NT)
        PT1 = v3(ar.take(NT * 256), NT)
        V2 = ar.take(NT * 2 * 132).rearrange("p (t c n) -> p t c n", t=NT, c=2)
        yin = ar.take(NT * NH * 19).rearrange("p (t h n) -> p t h n", t=NT, h=NH)
        yout_ = ar.take(NT * NH * 19)
        yout = yout_.rearrange("p (t h n) -> p t h n", t=NT, h=NH)
        fa = v3(yout_[:, 0:NT * D], NT)
        fb = v3(ar.take(NT * D), NT)
        ymk = v3(ar.take(NT * D), NT)
        top8 = ar.take(NT * NH * 8).rearrange("p (t h n) -> p t h n", t=NT, h=NH)
        ar2 = Area(even, EVEN)
        ymq = v3(ar2.take(NT * D), NT)
        qsT = v3(ar2.take(2 * S), 2)
        kvm = v3(ar2.take(2 * 136), 2)
        zr = v3(ar2.take(16), 2)
        ym = [ymk, ymq]
        y4 = fb
        yT4 = v3(yin.rearrange("p t h n -> p (t h n)")[:, 0:2 * S], 2)
        ar = Area(even, EVEN)
        K6 = [v3(ar.take(2 * S), 2), v3(odd[:, 3072:3072 + 2 * S], 2)]
        V6 = [v3(ar.take(NT * D), NT), v3(odd[:, 3072 + 2 * S:3072 + 4 * S], NT)]
        Q6 = v3(ar.take(2 * S), 2)
        P6 = v3(ar.take(NT * S), NT)
        PT6 = v3(ar.take(2 * S), 2)
        att = v3(ar.take(NT * D), NT)
        n1 = v3(ar.take(NT * D), NT)
        n2 = att
        attT = K6[0]
        h6 = Q6
        ar = Area(odd, ODD)
        xlT = v3(ar.take(2 * S), 2)
        xhT = v3(ar.take(2 * S), 2)
        hL = ar.take(S)
        hH = v3(ar.take(8 * S), 8)
        srow = ar.take(S)
        krow = even[:, 9120:9120 + S]
        ar = Area(odd, ODD)
        sg3 = v3(ar.take(2 * S), 2)
        hid3 = v3(ar.take(2 * S), 2)
        taps = v3(ar.take(4 * P), 4)
        conv = ar.take(S)
        extra = v3(ar.take(NT * D), NT)
        ar = Area(odd, ODD)
        sg5 = v3(ar.take(2 * S), 2)
        hid5 = ar.take(4 * S).rearrange("p (e f n) -> p e f n", e=2, f=2)
        ar = Area(odd, ODD)
        sg7 = v3(ar.take(2 * S), 2)
        hid7 = v3(ar.take(6 * S), 6)
        v6 = v3(sg7[:, :, :].rearrange("p a b -> p (a b)"), 2)

        ps = stack.enter_context(nc.psum_tensor("ps", [P, 8, 512], F32))

        w_loaded = [sem(f"w_loaded{i}") for i in range(len(WGROUPS))]
        wint_loaded = sem("wint_loaded")
        const_loaded = sem("const_loaded")
        constb_loaded = [sem(f"constb_loaded{i}") for i in range(2)]
        setup_done = sem("setup_done")
        setup_step = sem("setup_step")
        go = sem("go")
        passed = sem("passed")
        x_loaded = sem("x_loaded")
        xn_loaded = sem("xn_loaded")
        ctxT_loaded = sem("ctxT_loaded")
        ctxs_loaded = sem("ctxs_loaded")
        first_chunks = [sem(f"first_chunk{i}") for i in range(NSLOT)]
        out_stored = sem("out_stored")
        first = sem("batch_done")
        batch_done = first
        psum_filled = [sem(f"psum_filled{i}") for i in range(8)]
        psum_taken = [sem(f"psum_taken{i}") for i in range(8)]
        chunk_loaded = [sem(f"chunk_loaded{i}") for i in range(NSLOT)]
        ln_stats = sem("ln_stats")
        ln_rstd = sem("ln_rstd")
        xn_ready = sem("xn_ready")
        x_biased = sem("x_biased")
        max_ready = sem("max_ready")
        scol_ready = sem("scol_ready")
        rms_sum = sem("rms_sum")
        rms_ready = sem("rms_ready")
        xr_ready = sem("xr_ready")
        lse_max = sem("lse_max")
        ln_ready = sem("ln_ready")
        ce_ready = sem("ce_ready")
        ev_ready = sem("ev_ready")
        rowsum_ready = sem("rowsum_ready")
        total_ready = sem("total_ready")
        kcol_ready = sem("kcol_ready")
        score_ready = sem("score_ready")
        rank_ready = sem("rank_ready")
        keypad_ready = sem("keypad_ready")
        max1_ready = sem("max1_ready")
        router_exp = sem("router_exp")
        cw_ready = sem("cw_ready")
        extra_ready = sem("extra_ready")
        taps_ready = sem("taps_ready")
        conv_ready = sem("conv_ready")
        ones_ready = sem("ones_ready")
        zeros_ready = sem("zeros_ready")
        queries_spread = sem("queries_spread")
        abs_ready = sem("abs_ready")
        log_ready = sem("log_ready")
        focus_in = sem("focus_in")
        focus_exp = sem("focus_exp")
        sparse_ready = sem("sparse_ready")
        max6_ready = sem("max6_ready")
        h6_ready = sem("h6_ready")
        dve_step = sem("dve_step")
        act_step = sem("act_step")
        sums_ready = sem("sums_ready")
        sums_spread = sem("sums_spread")
        pool_step = sem("pool_step")
        last = pool_step

        def bank(key):
            return PLAN[key][0]

        def psb(key):
            return ps[:, PLAN[key][0], :]

        def got(eng, key):
            eng.wait_ge(psum_filled[PLAN[key][0]], PLAN[key][1] + 1)
            return psb(key)

        def in_sbuf(eng, key):
            eng.wait_ge(psum_taken[PLAN[key][0]], PLAN[key][1] + 1)

        def wait_chunk(eng, c, b):
            if c < NSLOT:
                eng.wait_ge(first_chunks[c], (b + 1) * 16)
            else:
                eng.wait_ge(chunk_loaded[c % NSLOT], 16 * (c // NSLOT))

        def meet(eng, b):
            eng.drain().then_inc(batch_done, 1)
            eng.wait_ge(go, b + 1)
            eng.sem_inc(passed, 1)

        block = stack.enter_context(nc.Block())

        @block.sync
        def _(sp):
            def load_ctxT(b):
                sp.dma_start(ctxT[:, :, :].rearrange("p t d -> p (t d)"), ctxT_in[bass.ds(b * P, P), :]).then_inc(ctxT_loaded, 16)

            def load_ctxs(b):
                sp.dma_start(ctxs[:, :, :].rearrange("p t d -> p (t d)"), ctxs_in[bass.ds(b * P, P), :]).then_inc(ctxs_loaded, 16)

            def load_x(dst, b, loaded):
                sp.dma_start(dst[:, :, :].rearrange("p t d -> p (t d)"), x_in[bass.ds(b * P, P), :]).then_inc(loaded, 16)

            def load_chunk(c, loaded):
                n = CHUNK if c < 2 else 1536
                sp.dma_start(stream[:, c % NSLOT, 0:n], stream_in[c * P:(c + 1) * P, 0:n]).then_inc(loaded, 16)

            def load_weights(i):
                lo, hi = woff[WGROUPS[i][0]][0], woff[WGROUPS[i][1]][0] + woff[WGROUPS[i][1]][1]
                sp.dma_start(weights[:, lo:hi], w_in[:, lo:hi]).then_inc(w_loaded[i], 16)

            load_ctxT(0)
            load_weights(0)
            sp.dma_start(cols[:, :], cols_in).then_inc(const_loaded, 16)
            sp.dma_start(const[:, :], const_in).then_inc(const_loaded, 16)
            load_x(xn, 0, xn_loaded)
            sp.dma_start(rows[:, :], rows_in).then_inc(const_loaded, 16)
            sp.dma_start(even[:, 0:FIRSTB], constb_in[:, 0:FIRSTB]).then_inc(constb_loaded[0], 16)
            sp.dma_start(last_staged, constb_in[:, FIRSTB:bn]).then_inc(constb_loaded[1], 16)
            sp.dma_start(wint[:, :], wint_in).then_inc(wint_loaded, 16)
            load_weights(1)
            load_x(x, 0, x_loaded)
            load_weights(2)
            for c in range(NSLOT):
                load_chunk(c, first_chunks[c])
            for i in range(3, len(WGROUPS)):
                load_weights(i)
            load_ctxs(0)
            with sp.Fori(0, NB) as b:
                for c in range(NSLOT, 12):
                    got(sp, ("yh", 1) if c < 5 else ("Y5", c - 5, 1))
                    load_chunk(c, chunk_loaded[c % NSLOT])
                    if c == 5:
                        load_ctxs(b + 1)
                        load_ctxT(b + 1)
                for c in range(NSLOT):
                    got(sp, ("Y5", c + 7, 1))
                    load_chunk(c, first_chunks[c])
                for h in range(2):
                    got(sp, ("xT7", h))
                load_x(xn, b + 1, xn_loaded)
                for i in range(2):
                    in_sbuf(sp, ("Y7", i))
                    sp.dma_start(out[bass.ds(b * P, P), i * 512:(i + 1) * 512],
                                 x[:, 2 * i:2 * i + 2, :].rearrange("p t d -> p (t d)")).then_inc(out_stored, 16)
                sp.wait_ge(batch_done, 4)
                sp.sem_clear(range(first.num, last.num + 1))
                sp.drain().then_inc(go, 1)
                sp.wait_ge(out_stored, (b + 1) * 32)
                load_x(x, b + 1, x_loaded)
            for loaded in [x_loaded, xn_loaded, ctxT_loaded, ctxs_loaded] + first_chunks:
                sp.wait_ge(loaded, (NB + 1) * 16)
            sp.wait_ge(out_stored, NB * 32)

        @block.gpsimd
        def _(pool):
            g = nc.gpsimd
            g.memset(eps6, 1e-6).then_inc(setup_step, 1)
            g.memset(mhalf, -0.5).then_inc(setup_step, 1)
            g.memset(onesk[:, :], 1.0 / K_EFF).then_inc(setup_step, 1)
            g.memset(xnT_[:, :, 0:4], 0.0).then_inc(setup_step, 1)
            g.memset(cw.rearrange("p t e -> p (t e)"), 1.0).then_inc(setup_step, 1)
            g.memset(tb.rearrange("p t e -> p (t e)"), BIG).then_inc(setup_step, 1)
            pool.wait_ge(setup_step, 6)
            with pool.Fori(0, NB) as b:
                n = [0]

                def link(ins):
                    n[0] += 1
                    ins.then_inc(pool_step, 1)
                    pool.wait_ge(pool_step, n[0])

                def rstd_of(idx, eps):
                    pool.wait_ge(ln_stats, idx + 1)
                    link(g.tensor_scalar(var, mv[:, :, 1], eps, None, ALU.add))
                    g.tensor_tensor(rstd, var, mhalf, ALU.pow).then_inc(ln_rstd, 1)

                def add_row(name):
                    g.tensor_tensor(x[:, :, :], x[:, :, :], row(name, NT), ALU.add).then_inc(x_biased, 1)

                for half in Qz:
                    g.memset(half[:, :, :, :], 0.0).then_inc(zeros_ready, 1)
                g.memset(V0[:, :, :, DK:32], 0.0).then_inc(zeros_ready, 1)
                rstd_of(0, 1e-5)
                pool.wait_ge(x_loaded, (b + 1) * 16)
                add_row("bo")
                pool.wait_ge(x_biased, 1)
                for key in [("Q", g_) for g_ in range(NG)]:
                    in_sbuf(pool, key)
                pool.wait_ge(zeros_ready, 3)

                def spread_queries(qt):
                    if qt >= 2:
                        got(pool, ("S", (NH // 2) * (qt - 1) - 1, 1))
                    for j in range(HG):
                        r = slice(32 * j, 32 * j + 32)
                        g.tensor_copy(Qz[qt % 2][r, :, j, :], Qr[r, :, qt * P:(qt + 1) * P]).then_inc(queries_spread, 1)
                    pool.wait_ge(queries_spread, HG * (qt + 1))

                pool.wait_ge(queries_spread, HG)
                for qt in range(1, NT):
                    spread_queries(qt)
                rstd_of(1, 1e-5)
                pool.wait_ge(rms_sum, 1)
                link(g.tensor_scalar(ss, ss, 1e-24, None, ALU.max))
                link(g.tensor_tensor(rmsr, ss, mhalf, ALU.pow))
                g.tensor_scalar(rmsr, rmsr, 16.0, None, ALU.mult).then_inc(rms_ready, 1)
                g.memset(V2[:, :, :, 128:129], 1.0).then_inc(ones_ready, 1)
                g.memset(yin[:, :, :, 16:19], 1.0).then_inc(ones_ready, 1)
                pool.wait_ge(xn_ready, NT * 2)
                add_row("lb2")
                pool.wait_ge(x_biased, 2)
                rstd_of(2, 1e-5)
                for i in range(2):
                    got(pool, ("yh", i))
                for i in range(4):
                    g.tensor_scalar(taps[:, i, :], K("ident"), col("convw", i), None, ALU.mult).then_inc(taps_ready, 1)
                g.memset(kr1[:, :, 0:32], 0.0).then_inc(keypad_ready, 1)
                g.memset(kr1[:, :, 32 + S:KEYPAD], 0.0).then_inc(keypad_ready, 1)
                rstd_of(3, 1e-5)
                pool.wait_ge(xn_ready, NT * 4)
                add_row("convb")
                rstd_of(4, 1e-5)
                rstd_of(5, 1e-5)
                rstd_of(6, 1e-5)
                rstd_of(7, 1e-3)
                rstd_of(8, 1e-3)
                rstd_of(9, 1e-3)
                rstd_of(10, 1e-5)
                meet(pool, b)

        @block.tensor
        def _(pe):
            T = nc.tensor
            ident = K("ident")
            identb = KB("identb")
            pe.wait_ge(const_loaded, 48)

            def room(key):
                if PLAN[key][1]:
                    pe.wait_ge(psum_taken[PLAN[key][0]], PLAN[key][1])
                return psb(key)

            def full(ins, key):
                ins.then_inc(psum_filled[bank(key)], 1)

            def mm(out_, lhs, rhs, ks, start=True, stop=True):
                ks = list(ks)
                for k in ks:
                    ins = T.matmul(out_, lhs(k), rhs(k), start=start and k == ks[0], stop=stop and k == ks[-1])
                return ins

            def tok(t):
                return slice(t * P, (t + 1) * P)

            def keep_clock(key, n):
                o = room(key)
                for _ in range(n):
                    T.matmul(o, identb, KB("mask0")[:, 0:512], start=True, stop=True)

            def xT(s, then=None, wait=18):
                keep_clock((f"xT{s}", 0), wait)
                a, c = room((f"xT{s}", 0)), room((f"xT{s}", 1))
                for t in range(NT):
                    pe.wait_ge(xn_ready, NT * LN_INDEX[s] + t + 1)
                    for h, o in enumerate((a, c)):
                        ins = T.transpose(o[:, tok(t)], xn[:, t, h * P:(h + 1) * P], ident)
                        if t == NT - 1:
                            full(ins, (f"xT{s}", h))
                if then is not None:
                    keep_clock(then, 4)

            def transposed(name, src):
                for h in range(2):
                    o = room((name, h))
                    for t in range(NT):
                        ins = T.transpose(o[:, tok(t)], src(t, h), ident)
                    full(ins, (name, h))

            def vector(o, name):
                T.matmul(o, ident, row(name), start=True, stop=False)

            def token_major(key_of, act_T, w, bias=None):
                for i in range(2):
                    o = room(key_of(i))
                    for t in (2 * i, 2 * i + 1):
                        ot = o[:, (t % 2) * D:(t % 2 + 1) * D]
                        if bias is not None:
                            vector(ot, bias)
                        ins = mm(ot, lambda k: act_T[:, k, tok(t)], lambda k: w[:, k, :], range(2), start=bias is None)
                    full(ins, key_of(i))

            def chan_major(key, w, c, act_T):
                full(mm(room(key), lambda k: w[:, k, c:c + P], lambda k: act_T[:, k, :], range(2)), key)

            with pe.Fori(0, NB) as b:
                pe.wait_ge(w_loaded[0], 16)
                pe.wait_ge(ctxT_loaded, (b + 1) * 16)
                chan_major(("K", 0), W("wk"), 0, ctxT)
                for g in range(NG):
                    if g < NG - 1:
                        chan_major(("K", g + 1), W("wk"), (g + 1) * P, ctxT)
                    else:
                        xT(0, wait=0)
                    in_sbuf(pe, ("K", g))
                    full(T.matmul(room(("F", g)), K("fold"), Kr[:, g, :], start=True, stop=True), ("F", g))
                pe.wait_ge(w_loaded[1], 16)
                in_sbuf(pe, ("xT0", 0))
                in_sbuf(pe, ("xT0", 1))
                for g in range(NG):
                    chan_major(("Q", g), W("wq"), g * P, xnT)
                token_major(lambda i: ("V", i), ctxT, W("wv"))
                pe.wait_ge(zeros_ready, 3)
                pe.wait_ge(setup_done, 1)
                for key in [("F", g) for g in range(NG)] + [("Q", g) for g in range(NG)]:
                    in_sbuf(pe, key)

                def scores(u):
                    qt, hp = divmod(u, NH // 2)
                    if hp == 0:
                        pe.wait_ge(queries_spread, HG * (qt + 1))
                    outs = [room(("S", u, j)) for j in range(2)]
                    for j, o in enumerate(outs):
                        g, i = divmod(2 * hp + j, HG)
                        q = Qz[qt % 2][:, g, i, :]
                        if qt:
                            T.matmul(o[:, 0:WIN[qt]], q, Kf[:, g, WSTART[qt]:WSTART[qt] + WIN[qt]], start=True, stop=False)
                        else:
                            T.matmul(o[:, 0:P], q, Kf[:, g, 0:P], start=True, stop=False)
                            T.matmul(o[:, P:S], q, Kf[:, g, KTILE[1]:KTILE[1] + 3 * P], start=False, stop=False)
                    for j, o in enumerate(outs):
                        full(T.matmul(o[:, 0:WIN[qt]], identb, KB("mask0")[:, WOFF[qt]:WOFF[qt] + WIN[qt]],
                                      start=False, stop=True), ("S", u, j))

                def prob_T(n):
                    u, heads = PT_TILES[n]
                    qt = u // (NH // 2)
                    o = room(("PT", n))
                    if heads is None:
                        for j in range(2):
                            ins = T.transpose(o[0:32, tok(j)], probs[:, u % 2, j, WGLOBAL[qt]:WGLOBAL[qt] + 32], ident)
                    else:
                        for i, j in enumerate(heads):
                            if qt == 0:
                                T.transpose(o[:, FIRST * i:FIRST * i + P], probs[:, u % 2, j, 0:P], ident)
                                for c in range(NT - 1):
                                    ins = T.transpose(o[:, FIRST * i + P + 16 * c:FIRST * i + P + 16 * c + 16],
                                                      probs[0:16, u % 2, j, P * (c + 1):P * (c + 2)], ident[0:16, 0:16])
                                continue
                            for c, at in enumerate(WBLOCKS[qt]):
                                ins = T.transpose(o[:, tok(i * len(WBLOCKS[qt]) + c)], probs[:, u % 2, j, at:at + P], ident)
                    full(ins, ("PT", n))

                def prob_V(u):
                    qt, hp = divmod(u, NH // 2)
                    o = room(("O", qt)) if hp == 0 else psb(("O", qt))
                    for n in UNIT_TILES[u]:
                        in_sbuf(pe, ("PT", n))
                    for j in range(2):
                        h = 2 * hp + j
                        oh = o[32 * (h % HG):32 * (h % HG) + 32, tok(h // HG)]
                        pt = PTs[:, UNIT_TILES[u][-1] % 3, :]
                        if qt == 0:
                            T.matmul(oh, V0[:, 0, h, :], pt[:, FIRST * j:FIRST * j + P], start=True, stop=False)
                            for c in range(NT - 1):
                                at = FIRST * j + P + 16 * c
                                ins = T.matmul(oh[:, 0:16], V0[:, c + 1, h, :], pt[:, at:at + 16],
                                               start=False, stop=(c == NT - 2))
                            continue
                        if qt >= 2:
                            T.matmul(oh, V0[0:32, 0, h, :], PTs[0:32, UNIT_TILES[u][0] % 3, tok(j)],
                                     start=True, stop=False)
                        for c in range(2):
                            ins = T.matmul(oh, V0[:, qt - 1 + c, h, :], pt[:, tok(2 * j + c)],
                                           start=(qt < 2 and c == 0), stop=(c == 1))
                    if hp == NH // 2 - 1:
                        full(ins, ("O", qt))

                def sums_T(qt):
                    pe.wait_ge(sums_spread, qt + 1)
                    o = room(("D", qt))
                    for g in range(NG):
                        ins = T.transpose(o[:, tok(g)], rexp[:, HG * g:HG * g + HG, :].rearrange("p h n -> p (h n)"), ident)
                    full(ins, ("D", qt))

                for u in range(NU + 2):
                    if u == 3:
                        in_sbuf(pe, ("V", 0))
                        in_sbuf(pe, ("V", 1))
                    if u >= 3:
                        prob_V(u - 3)
                    if u >= 2:
                        for j in range(2):
                            in_sbuf(pe, ("S", u - 2, j))
                        for n in UNIT_TILES[u - 2]:
                            prob_T(n)
                    if u < NU:
                        scores(u)
                    if u >= 9 and (u - 9) % (NH // 2) == 0:
                        sums_T((u - 9) // (NH // 2))
                prob_V(NU - 1)
                for i in range(2):
                    o = room(("Y0", i))
                    for t in (2 * i, 2 * i + 1):
                        in_sbuf(pe, ("O", t))
                        ot = o[:, (t % 2) * D:(t % 2 + 1) * D]
                        ins = mm(ot, lambda g: OT[:, g, tok(t)], lambda g: W("wo", 4)[:, g, :], range(NG))
                    full(ins, ("Y0", i))

                for i in (2, 3, 4):
                    pe.wait_ge(w_loaded[i], 16)
                token_major(lambda i: ("v4", i), ctxT, W("w2v"))
                for h in range(2):
                    chan_major(("KT1", h), W("wred"), h * P, ctxT)
                pe.wait_ge(scol_ready, 1)
                o = room("R")
                for t in range(NT):
                    ins = T.transpose(o[:, tok(t)], scol[:, t:t + 1].broadcast_to([P, P]), ident)
                full(ins, "R")
                pe.wait_ge(xr_ready, NT)
                transposed("xT1", lambda t, h: xn[:, t, h * P:(h + 1) * P])
                in_sbuf(pe, ("xT1", 0))
                in_sbuf(pe, ("xT1", 1))
                chan_major(("h", "light"), W("lw1"), 0, xlT)

                def heavy_w(m):
                    c = stream[:, m // 4, :]
                    return c[:, 0:1024].rearrange("p (k n) -> p k n", k=2), c[:, 1024:2048].rearrange("p (m n) -> p m n", m=4)

                def branches():
                    for i in range(2):
                        o = room(("k4", i))
                        for t in (2 * i, 2 * i + 1):
                            for k in range(2):
                                ins = T.matmul(o[:, (t % 2) * D:(t % 2 + 1) * D], ctxT[:, k, tok(t)], W("w2k")[:, k, :],
                                               start=(k == 0), stop=(k == 1))
                                if t % 2 and k == 1:
                                    full(ins, ("k4", i))
                                yield
                    for m in range(8):
                        wait_chunk(pe, m // 4, b)
                        o = room(("h", m))
                        for k in range(2):
                            ins = T.matmul(o, heavy_w(m)[0][:, k, (m % 4) * P:(m % 4 + 1) * P], xhT[:, k, :],
                                           start=(k == 0), stop=(k == 1))
                            if k == 1:
                                full(ins, ("h", m))
                            yield
                    in_sbuf(pe, ("h", "light"))
                    for i in range(2):
                        o = room(("yl", i))
                        for t in (2 * i, 2 * i + 1):
                            ins = T.matmul(o[:, (t % 2) * D:(t % 2 + 1) * D], hL[:, tok(t)], W("lw2", 1)[:, 0, :],
                                           start=True, stop=True)
                            if t % 2:
                                full(ins, ("yl", i))
                            yield
                    for m in range(8):
                        in_sbuf(pe, ("h", m))
                    for i in range(2):
                        o = room(("yh", i))
                        for t in (2 * i, 2 * i + 1):
                            ot = o[:, (t % 2) * D:(t % 2 + 1) * D]
                            vector(ot, "hb2")
                            for m in range(8):
                                ins = T.matmul(ot, hH[:, m, tok(t)], heavy_w(m)[1][:, m % 4, :],
                                               start=False, stop=(m == 7))
                                if t % 2 and m == 7:
                                    full(ins, ("yh", i))
                                yield

                work = branches()
                room("chain")
                done = 0
                share = (16, 12, 16, 16)
                for r in range(ROUNDS):
                    for i in range(ITERS):
                        n = r * ITERS + i
                        pe.wait_ge(rowsum_ready, n + 1)
                        ins = T.matmul(psb("chain")[:, n:n + 1], onesk[:, :], rs[:, n % 2:n % 2 + 1],
                                       start=True, stop=True)
                        if n == ROUNDS * ITERS - 1:
                            full(ins, "chain")
                        else:
                            ins.then_inc(total_ready, 1)
                        for _ in range((i + 1) * share[r] // ITERS - i * share[r] // ITERS):
                            next(work)
                for _ in work:
                    raise AssertionError

                xT(2, ("S1", 0), wait=58)
                for key in (("xT2", 0), ("xT2", 1), ("KT1", 0), ("KT1", 1)):
                    in_sbuf(pe, key)
                pe.wait_ge(keypad_ready, 2)
                pe.wait_ge(setup_done, 2)
                for t in range(NT):
                    o = room(("S1", t))[:, 0:KEYW]
                    mm(o, lambda k: xnT[:, k, tok(t)], lambda k: kr1[:, k, t * P:t * P + KEYW], range(2), stop=False)
                    full(T.matmul(o, identb, KB("band")[:, t * KEYW:(t + 1) * KEYW], start=False, stop=True), ("S1", t))
                for t in range(NT):
                    in_sbuf(pe, ("S1", t))
                    o = room(("PT1", t))
                    T.transpose(o[:, 0:P], P1[:, t, 0:P], ident)
                    full(T.transpose(o[0:64, P:2 * P], P1[:, t, P:KEYW], ident), ("PT1", t))
                pe.wait_ge(ctxs_loaded, (b + 1) * 16)
                for i in range(2):
                    o = room(("O1", i))
                    for t in (2 * i, 2 * i + 1):
                        in_sbuf(pe, ("PT1", t))
                        T.matmul(o[:, (t % 2) * D:(t % 2 + 1) * D], PT1[:, t, 0:P], ctxs[:, t, :], start=True, stop=False)
                        ins = T.matmul(o[:, (t % 2) * D:(t % 2 + 1) * D], PT1[0:64, t, P:2 * P], ctxs[0:64, t + 1, :],
                                       start=False, stop=True)
                    full(ins, ("O1", i))

                def router(s, w):
                    key = f"RT{s}"
                    o = room(key)
                    for t in range(NT):
                        ins = mm(o[:, t * 8:t * 8 + 8], lambda k: xnT[:, k, tok(t)], lambda k: w[:, k, :], range(2))
                    full(ins, key)

                xT(3, "RT3")
                in_sbuf(pe, ("xT3", 0))
                in_sbuf(pe, ("xT3", 1))
                router(3, W("l1r"))

                def down3(e):
                    in_sbuf(pe, ("U3", e))
                    for i in range(2):
                        o = room(("Y3", e, i))
                        for t in (2 * i, 2 * i + 1):
                            ins = T.matmul(o[:, (t % 2) * D:(t % 2 + 1) * D], hid3[:, e % 2, tok(t)],
                                           W("l1d", 4)[:, e, :], start=True, stop=True)
                        full(ins, ("Y3", e, i))

                for e in range(4):
                    chan_major(("G3", e), W("l1g", 8)[:, 2 * e:2 * e + 2, :], 0, xnT)
                    chan_major(("U3", e), W("l1u", 8)[:, 2 * e:2 * e + 2, :], 0, xnT)
                    if e == 0:
                        pe.wait_ge(taps_ready, 4)
                        pe.wait_ge(conv_ready, 1)
                        for i in range(2):
                            o = room(("CT3", i))
                            for t in (2 * i, 2 * i + 1):
                                ot = o[:, (t % 2) * D:(t % 2 + 1) * D]
                                for k in range(4):
                                    at = 4 + t * P - k
                                    T.matmul(ot[:, 0:P], xnT_[:, 0, at:at + P], taps[:, 3 - k, :],
                                             start=(k == 0), stop=(k == 3))
                                ins = T.transpose(ot[:, P:D], conv[:, tok(t)], ident)
                            full(ins, ("CT3", i))
                    else:
                        down3(e - 1)
                down3(3)

                xT(4, ("q4", 0))
                in_sbuf(pe, ("xT4", 0))
                in_sbuf(pe, ("xT4", 1))
                token_major(lambda i: ("q4", i), xnT, W("w2q"))
                pe.wait_ge(w_loaded[5], 16)
                for h in range(2):
                    chan_major(("K6", 1, h), W("k2"), h * P, ctxT)
                token_major(lambda i: ("V6", 1, i), ctxT, W("v2"))
                keep_clock(("KV4", 0), 62)
                pe.wait_ge(sparse_ready, 1)
                pe.wait_ge(ones_ready, 2)
                in_sbuf(pe, ("v4", 0))
                in_sbuf(pe, ("v4", 1))
                for c in range(2):
                    o = room(("KV4", c))
                    for t in range(NT):
                        ins = T.matmul(o[:, 0:129], ymk[:, t, c * P:(c + 1) * P], V2[:, t, c, 0:129],
                                       start=(t == 0), stop=(t == NT - 1))
                    full(ins, ("KV4", c))
                pe.wait_ge(sparse_ready, 2)
                transposed("QT4", lambda t, h: ymq[:, t, h * P:(h + 1) * P])
                keep_clock(("y4", 0), 5)
                for key in (("KV4", 0), ("KV4", 1), ("QT4", 0), ("QT4", 1)):
                    in_sbuf(pe, key)
                for t in range(NT):
                    o = room(("y4", t))
                    for c in range(2):
                        ins = T.matmul(o[:, c * 136:(c + 1) * 136], qsT[:, c, tok(t)], kvm[:, c, :], start=True, stop=True)
                    full(ins, ("y4", t))
                keep_clock(("yT4", 0), 6)
                for t in (2, 3):
                    in_sbuf(pe, ("y4", t))
                transposed("yT4", lambda t, h: y4[:, t, h * P:(h + 1) * P])
                keep_clock(("O4", 0), 4)
                in_sbuf(pe, ("yT4", 0))
                in_sbuf(pe, ("yT4", 1))
                token_major(lambda i: ("O4", i), yT4, W("w2p"))

                xT(5, "RT5")
                in_sbuf(pe, ("xT5", 0))
                in_sbuf(pe, ("xT5", 1))
                router(5, W("l2r"))

                def expert_w(e, part):
                    return stream[:, (e + 2) % NSLOT, part * 512:(part + 1) * 512].rearrange("p (k n) -> p k n", k=2)

                def down5(e):
                    for f in range(2):
                        in_sbuf(pe, ("U5", e, f))
                    for i in range(2):
                        o = room(("Y5", e, i))
                        for t in (2 * i, 2 * i + 1):
                            ins = mm(o[:, (t % 2) * D:(t % 2 + 1) * D], lambda f: hid5[:, e % 2, f, tok(t)],
                                     lambda f: expert_w(e, 2)[:, f, :], range(2))
                            if t == NT - 1:
                                full(ins, ("Y5", e, i))
                        if i == 0:
                            full(ins, ("Y5", e, i))

                for e in range(10):
                    wait_chunk(pe, e + 2, b)
                    for f in range(2):
                        chan_major(("G5", e, f), expert_w(e, 0), f * P, xnT)
                        chan_major(("U5", e, f), expert_w(e, 1), f * P, xnT)
                    if e:
                        down5(e - 1)
                down5(9)

                xT(6, ("K6", 0, 0))
                in_sbuf(pe, ("xT6", 0))
                in_sbuf(pe, ("xT6", 1))
                for h in range(2):
                    chan_major(("K6", 0, h), W("k1"), h * P, xnT)
                    chan_major(("Q6", 0, h), W("q1"), h * P, xnT)
                token_major(lambda i: ("V6", 0, i), xnT, W("v1"))
                for a in range(2):
                    for h in range(2):
                        in_sbuf(pe, ("K6", a, h))
                        in_sbuf(pe, ("Q6", a, h))
                    for t in range(NT):
                        n = (t + 1) * P if a == 0 else S
                        o = room(("S6", a, t))
                        ins = mm(o[:, 0:n], lambda k: Q6[:, k, tok(t)], lambda k: K6[a][:, k, 0:n], range(2), stop=(a == 1))
                        if a == 0:
                            ins = T.matmul(o[:, tok(t)], identb, KB("causal"), start=False, stop=True)
                        full(ins, ("S6", a, t))
                    for i in range(2):
                        in_sbuf(pe, ("V6", a, i))
                    for t in range(NT + 1):
                        if t < NT:
                            in_sbuf(pe, ("S6", a, t))
                            p = room(("P6", a, t))
                            for c in range(t + 1 if a == 0 else NT):
                                ins = T.transpose(p[:, tok(c)], P6[:, t, tok(c)], ident)
                            full(ins, ("P6", a, t))
                        if t:
                            r = t - 1
                            if r % 2 == 0:
                                o = room(("O6", a, r // 2))
                            in_sbuf(pe, ("P6", a, r))
                            ins = mm(o[:, (r % 2) * D:(r % 2 + 1) * D], lambda c: PT6[:, r % 2, tok(c)],
                                     lambda c: V6[a][:, c, :], range(r + 1 if a == 0 else NT))
                            if r % 2:
                                full(ins, ("O6", a, r // 2))
                    if a == 0:
                        in_sbuf(pe, ("O6", 0, 0))
                        in_sbuf(pe, ("O6", 0, 1))
                        transposed("aT6", lambda t, h: att[:, t, h * P:(h + 1) * P])
                        in_sbuf(pe, ("aT6", 0))
                        in_sbuf(pe, ("aT6", 1))
                        for h in range(2):
                            chan_major(("Q6", 1, h), W("q2"), h * P, attT)
                keep_clock(("nT6", 0), 27)
                pe.wait_ge(xn_ready, NT * (LN_INDEX["6b"] + 1))
                transposed("nT6", lambda t, h: n2[:, t, h * P:(h + 1) * P])
                keep_clock(("h6", 0), 4)
                in_sbuf(pe, ("nT6", 0))
                in_sbuf(pe, ("nT6", 1))
                for m in range(2):
                    chan_major(("h6", m), W("f1"), m * P, attT)
                pe.wait_ge(h6_ready, 2)
                token_major(lambda i: ("f6", i), h6, W("f2"), "b2")

                pe.wait_ge(setup_done, 3)
                xT(7, ("G7", 0), wait=46)
                in_sbuf(pe, ("xT7", 0))
                in_sbuf(pe, ("xT7", 1))
                for m in range(6):
                    chan_major(("G7", m), v3(wl3[:, 0:1536], 2), m * P, xnT)
                    chan_major(("U7", m), v3(wl3[:, 1536:3072], 2), m * P, xnT)
                for m in range(6):
                    in_sbuf(pe, ("U7", m))
                for i in range(2):
                    o = room(("Y7", i))
                    for t in (2 * i, 2 * i + 1):
                        ins = mm(o[:, (t % 2) * D:(t % 2 + 1) * D], lambda m: hid7[:, m, tok(t)],
                                 lambda m: v3(wl3[:, 3072:4608], 6)[:, m, :], range(6))
                    full(ins, ("Y7", i))
                for _ in range(8):
                    T.matmul(psb(("xT7", 0)), identb, KB("mask0")[:, 0:512], start=True, stop=True)
                meet(pe, b)

        @block.scalar
        def _(act):
            A = nc.scalar.activation
            act.wait_ge(const_loaded, 48)
            act.wait_ge(setup_step, 6)
            act.wait_ge(constb_loaded[0], 16)
            A(constb[:, 0:FIRSTB], even[:, 0:FIRSTB], ACT.Copy).then_inc(setup_done, 1)
            act.wait_ge(constb_loaded[1], 16)
            A(constb[:, FIRSTB:bn], last_staged, ACT.Copy).then_inc(setup_done, 1)
            act.wait_ge(wint_loaded, 16)
            A(wl3, wint[:, :], ACT.Copy, scale=1.0 / 127.0).then_inc(setup_done, 1)
            act.wait_ge(setup_done, 3)

            def taken(ins, key):
                ins.then_inc(psum_taken[bank(key)], 1)

            def copy(key, dst, src=None):
                o = got(act, key)
                taken(A(dst, o if src is None else src(o), ACT.Copy), key)

            with act.Fori(0, NB) as b:
                n_step = [0]

                def link(ins):
                    n_step[0] += 1
                    ins.then_inc(act_step, 1)
                    act.wait_ge(act_step, n_step[0])

                def focus_abs(w):
                    for i in range(2):
                        o = got(act, (w, i))
                        A(fa[:, 2 * i:2 * i + 2, :].rearrange("p t d -> p (t d)"), o, ACT.Abs, scale=0.01).then_inc(abs_ready, 1)

                def focus_rest(w, i):
                    in_sbuf(act, (w, 0))
                    in_sbuf(act, (w, 1))
                    A(fa, fb, ACT.Ln, bias=eps6).then_inc(log_ready, 1)
                    act.wait_ge(focus_in, i + 1)
                    for t in range(NT):
                        A(fb[:, t, :], fa[:, t, :], ACT.Exp, bias=fmax[:, t:t + 1],
                          accum_out=psumm[:, t:t + 1]).then_inc(focus_exp, 1)

                for g in range(NG):
                    if g == NG - 1:
                        copy(("xT0", 0), xnT[:, 0, :])
                    o = got(act, ("F", g))
                    A(Kf[:, g, 0:P], o[:, 0:P], ACT.Copy)
                    A(Kf[:, g, P:P + 32], o[:, 0:32], ACT.Copy)
                    A(Kf[:, g, S + 32:S + 64], o[:, 0:32], ACT.Copy)
                    taken(A(Kf[:, g, KTILE[1]:KTILE[1] + 3 * P], o[:, P:S], ACT.Copy), ("F", g))

                def global_tile(u):
                    n = UNIT_TILES[u][0]
                    if PT_TILES[n][1] is None:
                        o = got(act, ("PT", n))
                        taken(A(PTs[0:32, n % 3, 0:2 * P], o[0:32, 0:2 * P], ACT.Copy), ("PT", n))

                def spread_sums(qt):
                    act.wait_ge(sums_ready, qt + 1)
                    if qt:
                        got(act, ("D", qt - 1))
                    A(rexp, rden[:, qt, :].unsqueeze(2).broadcast_to([P, NH, 32]), ACT.Copy).then_inc(sums_spread, 1)

                act.wait_ge(zeros_ready, 3)
                for key in [("Q", g) for g in range(NG)]:
                    in_sbuf(act, key)
                for j in range(HG // 2, HG):
                    r = slice(32 * j, 32 * j + 32)
                    A(Qz[0][r, :, j, :], Qr[r, :, 0:P], ACT.Copy).then_inc(queries_spread, 1)
                for u in range(NU):
                    qt, hp = divmod(u, NH // 2)
                    if u >= 9 and (u - 9) % (NH // 2) == 0:
                        spread_sums((u - 9) // (NH // 2))
                    if u >= 10 and (u - 10) % (NH // 2) == 0:
                        if u > 10:
                            in_sbuf(act, ("O", (u - 18) // (NH // 2)))
                        copy(("D", (u - 10) // (NH // 2)), rsum)
                    act.wait_ge(max_ready, u + 1)
                    for j in range(2):
                        h = 2 * hp + j
                        taken(A(probs[:, u % 2, j, 0:WIN[qt]], psb(("S", u, j))[:, 0:WIN[qt]], ACT.Exp,
                                bias=nm[:, u % 2, j:j + 1], accum_out=den[:, qt, h:h + 1]), ("S", u, j))
                    if u >= 1:
                        global_tile(u - 1)
                global_tile(NU - 1)
                spread_sums(NT - 1)
                in_sbuf(act, ("O", NT - 2))
                copy(("D", NT - 1), rsum)

                for i in range(2):
                    copy(("v4", i), V2[:, 2 * i:2 * i + 2, :, 0:P],
                         lambda o: o.rearrange("p (t c n) -> p t c n", t=2, c=2))
                for t in range(NT):
                    act.wait_ge(xn_ready, NT + t + 1)
                    ins = A(hL[:, 0:D], xn[:, t, :], ACT.Square, accum_out=ss[:, t:t + 1])
                    if t < NT - 1:
                        link(ins)
                ins.then_inc(rms_sum, 1)
                for h in range(2):
                    o = got(act, ("KT1", h))
                    taken(A(kr1[:, h, 32:32 + S], o, ACT.Identity, bias=col("bred", h)), ("KT1", h))
                act.wait_ge(rms_sum, 1)
                o = got(act, ("xT1", 0))
                A(xlT[:, 0, :], o, ACT.Copy, scale=col("lgam", 0))
                taken(A(xhT[:, 0, :], o, ACT.Copy, scale=col("hgam", 0)), ("xT1", 0))

                def gelu(key, dst, bias):
                    o = got(act, key)
                    taken(A(dst, o, ACT.Gelu, bias=bias), key)

                act.wait_ge(lse_max, 1)
                link(A(hH[:, 7, :], krow, ACT.Exp, bias=nmax, accum_out=lsum))
                A(lnv, lsum, ACT.Ln, scale=1.0 / K_EFF).then_inc(ln_ready, 1)
                for r in range(ROUNDS):
                    act.wait_ge(ce_ready, r + 1)
                    A(ev, ce, ACT.Exp).then_inc(ev_ready, 1)
                    if r == 0:
                        gelu(("h", "light"), hL, col("lb1"))
                        focus_abs("k4")
                    for m in ((0, 1, 2), (3,), (), ())[r]:
                        gelu(("h", m), hH[:, m, :], col("hb1", m))
                    if r == 1:
                        focus_rest("k4", 0)
                        for m in range(4, 8):
                            gelu(("h", m), hH[:, m, :], col("hb1", m))
                    A(lspare, eps6, ACT.Ln)
                    n = ITERS * (r + 1) - 1
                    if r == ROUNDS - 1:
                        got(act, "chain")
                        taken(A(lnv, psb("chain")[:, n:n + 1], ACT.Ln, scale=22026.465794806718), "chain")
                    else:
                        act.wait_ge(total_ready, n + 1)
                        A(lnv, psb("chain")[:, n:n + 1], ACT.Ln, scale=22026.465794806718).then_inc(ln_ready, 1)
                act.wait_ge(kcol_ready, 1)
                A(score, kcol, ACT.Exp).then_inc(score_ready, 1)

                copy(("xT2", 0), xnT[:, 0, :])
                for t in range(NT):
                    act.wait_ge(max1_ready, t + 1)
                    taken(A(P1[:, t, :], psb(("S1", t))[:, 0:KEYW], ACT.Exp, bias=nm4[:, t:t + 1],
                            accum_out=den4[:, t:t + 1]), ("S1", t))

                copy(("xT3", 0), xnT[:, 0, :])
                o = got(act, "RT3")
                taken(A(sc.rearrange("p t e -> p (t e)"), o[:, 0:32], ACT.Sigmoid), "RT3")
                act.wait_ge(cw_ready, 1)
                for t in range(NT):
                    A(extra[:, t, :], xn[:, t, :], ACT.Relu, scale=cw[:, t, 7:8]).then_inc(extra_ready, 1)
                for e in range(4):
                    o = got(act, ("G3", e))
                    if e >= 2:
                        in_sbuf(act, ("U3", e - 2))
                    taken(A(sg3[:, e % 2, :], o, ACT.Silu), ("G3", e))

                copy(("xT4", 0), xnT[:, 0, :])
                act.wait_ge(sparse_ready, 1)
                focus_abs("q4")
                focus_rest("q4", 1)
                for h in range(2):
                    copy(("K6", 1, h), K6[1][:, h, :])
                for i in range(2):
                    copy(("V6", 1, i), V6[1][:, 2 * i:2 * i + 2, :].rearrange("p t d -> p (t d)"))
                copy(("QT4", 0), qsT[:, 0, :])
                copy(("QT4", 1), qsT[:, 1, :])
                copy(("yT4", 0), yT4[:, 0, :])
                copy(("yT4", 1), yT4[:, 1, :])

                copy(("xT5", 0), xnT[:, 0, :])
                in_sbuf(act, "RT5")
                A(sc.rearrange("p t e -> p (t e)"), sc.rearrange("p t e -> p (t e)"), ACT.Exp).then_inc(router_exp, 1)
                for e in range(10):
                    for f in range(2):
                        o = got(act, ("G5", e, f))
                        if e:
                            in_sbuf(act, ("U5", e - 1, f))
                        taken(A(sg5[:, f, :], o, ACT.Silu), ("G5", e, f))

                copy(("xT6", 0), xnT[:, 0, :])
                scale = float(S) ** -0.5

                def q_scaled(a, h):
                    o = got(act, ("Q6", a, h))
                    taken(A(Q6[:, h, :], o, ACT.Copy, scale=scale), ("Q6", a, h))

                for h in range(2):
                    copy(("K6", 0, h), K6[0][:, h, :])
                    q_scaled(0, h)
                for i in range(2):
                    copy(("V6", 0, i), V6[0][:, 2 * i:2 * i + 2, :].rearrange("p t d -> p (t d)"))
                for a in range(2):
                    for t in range(NT):
                        n = (t + 1) * P if a == 0 else S
                        act.wait_ge(max6_ready, NT * a + t + 1)
                        taken(A(P6[:, t, 0:n], psb(("S6", a, t))[:, 0:n], ACT.Exp, bias=nm4[:, t:t + 1],
                                accum_out=den4[:, t:t + 1]), ("S6", a, t))
                    if a == 0:
                        copy(("aT6", 0), attT[:, 0, :])
                        copy(("aT6", 1), attT[:, 1, :])
                        for h in range(2):
                            q_scaled(1, h)
                copy(("nT6", 0), attT[:, 0, :])
                copy(("nT6", 1), attT[:, 1, :])
                for m in range(2):
                    o = got(act, ("h6", m))
                    taken(A(v6[:, m, :], o, ACT.Identity, bias=col("b1", m)), ("h6", m))

                copy(("xT7", 0), xnT[:, 0, :])
                for m in range(6):
                    o = got(act, ("G7", m))
                    if m >= 2:
                        in_sbuf(act, ("U7", m - 2))
                    taken(A(sg7[:, m % 2, :], o, ACT.Silu), ("G7", m))
                meet(act, b)

        @block.vector
        def _(dve):
            V = nc.vector
            dve.wait_ge(const_loaded, 48)

            def taken(ins, key):
                ins.then_inc(psum_taken[bank(key)], 1)

            with dve.Fori(0, NB) as b:
                n_step = [0]

                def link(ins):
                    n_step[0] += 1
                    ins.then_inc(dve_step, 1)
                    dve.wait_ge(dve_step, n_step[0])

                def flat(ap):
                    return ap.rearrange("p t d -> p (t d)")

                def two(o):
                    return o.rearrange("p (t d) -> p t d", t=2)

                def copy(key, dst):
                    taken(V.tensor_copy(dst, got(dve, key)), key)

                def norm_stats(src):
                    for t in range(NT):
                        n_step[0] += 1
                        V.bn_stats(stats[:, t, :], src[:, t, :]).then_inc(dve_step, 1)
                    for t in range(NT):
                        dve.wait_ge(dve_step, n_step[0] - NT + 1 + t)
                        ins = V.bn_aggr(mv[:, t, :], stats[:, t, :])
                    ins.then_inc(ln_stats, 1)

                def norm(s, src, dst, affine=False):
                    norm_stats(src)
                    normalised(s, src, dst, affine)

                def normalised(s, src, dst, affine=False):
                    idx = LN_INDEX[s]
                    if affine:
                        dve.wait_ge(ln_stats, idx + 1)
                        for t in range(NT):
                            n_step[0] += 1
                            V.scalar_tensor_tensor(dst[:, t, :], src[:, t, :], mv[:, t, 0:1], row("gamma"),
                                                   ALU.subtract, ALU.mult).then_inc(dve_step, 1)
                    dve.wait_ge(ln_rstd, idx + 1)
                    for t in range(NT if affine else 0):
                        dve.wait_ge(dve_step, n_step[0] - NT + 1 + t)
                        V.scalar_tensor_tensor(dst[:, t, :], dst[:, t, :], rstd[:, t:t + 1], row("beta"),
                                               ALU.mult, ALU.add).then_inc(xn_ready, 1)
                    if affine:
                        dve.wait_ge(xn_ready, NT * (idx + 1))
                        return
                    for t in range(NT):
                        V.tensor_scalar(dst[:, t, :], src[:, t, :], mv[:, t, 0:1], rstd[:, t:t + 1],
                                        ALU.subtract, ALU.mult).then_inc(xn_ready, 1)

                dve.wait_ge(xn_loaded, (b + 1) * 16)
                norm_stats(xn)
                for g in range(NG):
                    if g == 1:
                        dve.wait_ge(ln_stats, 1)
                        normalised(0, xn, xn)
                    o = got(dve, ("K", g))
                    taken(V.scalar_tensor_tensor(Kr[:, g, :], o, col("bk", g), K("rope"), ALU.add, ALU.mult), ("K", g))
                copy(("xT0", 1), xnT[:, 1, :])
                for g in range(NG):
                    o = got(dve, ("Q", g))
                    taken(V.scalar_tensor_tensor(Qr[:, g, :], o, col("bq", g), K("rope"), ALU.add, ALU.mult), ("Q", g))

                def row_max(u):
                    for j in range(2):
                        got(dve, ("S", u, j))
                    V.reduce_max(nm[:, u % 2, :], ps[:, 2 * (u % 2):2 * (u % 2) + 2, 0:WIN[u // (NH // 2)]], AX_X,
                                 negate=True).then_inc(max_ready, 1)

                for g in range(NG):
                    in_sbuf(dve, ("Q", g))
                dve.wait_ge(zeros_ready, 3)
                for j in range(HG // 2):
                    r = slice(32 * j, 32 * j + 32)
                    V.tensor_copy(Qz[0][r, :, j, :], Qr[r, :, 0:P]).then_inc(queries_spread, 1)
                for i in range(2):
                    o = got(dve, ("V", i))
                    for t in (2 * i, 2 * i + 1):
                        ins = V.tensor_tensor(V0[:, t, :, 0:DK], two(o)[:, t % 2, :].rearrange("p (h n) -> p h n", h=NH),
                                              row("bv").rearrange("p (h n) -> p h n", h=NH), ALU.add)
                    taken(ins, ("V", i))

                def out_tile(qt):
                    in_sbuf(dve, ("D", qt))
                    taken(V.tensor_tensor(OT[:, :, qt * P:(qt + 1) * P],
                                          got(dve, ("O", qt)).rearrange("p (g n) -> p g n", g=NG),
                                          rsum.rearrange("p (g n) -> p g n", g=NG), ALU.mult), ("O", qt))

                for u in range(NU + 2):
                    if u >= 9 and (u - 9) % (NH // 2) == 0:
                        qt = (u - 9) // (NH // 2)
                        for j in range(2):
                            in_sbuf(dve, ("S", u - 2, j))
                        V.reciprocal(rden[:, qt, :], den[:, qt, :]).then_inc(sums_ready, 1)
                    if u >= 2:
                        for n in UNIT_TILES[u - 2]:
                            if PT_TILES[n][1] is not None:
                                o = got(dve, ("PT", n))
                                w = S if u - 2 >= NH // 2 else 2 * FIRST
                                taken(V.tensor_copy(PTs[:, n % 3, 0:w], o[:, 0:w]), ("PT", n))
                    if u >= 10 and (u - 10) % (NH // 2) == 0:
                        out_tile((u - 10) // (NH // 2))
                    if u < NU:
                        row_max(u)
                out_tile(NT - 1)
                dve.wait_ge(x_biased, 1)

                def x_plus(name, i):
                    o = got(dve, (name, i))
                    xs = flat(x[:, 2 * i:2 * i + 2, :])
                    taken(V.tensor_tensor(xs, xs, o, ALU.add), (name, i))

                def add_to_x(name):
                    for i in range(2):
                        x_plus(name, i)
                    in_sbuf(dve, (name, 0))
                    in_sbuf(dve, (name, 1))

                add_to_x("Y0")

                norm(1, x, xn)
                for t in range(NT):
                    dve.wait_ge(xn_ready, NT + t + 1)
                    ins = V.tensor_tensor_reduce(out=hH[:, 0, 0:D], in0=xn[:, t, :], in1=row("rt"), scale=1.0,
                                                 scalar=0.0, op0=ALU.mult, op1=ALU.add, accum_out=scol[:, t:t + 1])
                    if t < NT - 1:
                        link(ins)
                ins.then_inc(scol_ready, 1)
                copy("R", srow)
                dve.wait_ge(rms_ready, 1)
                for t in range(NT):
                    V.tensor_scalar(xn[:, t, :], xn[:, t, :], rmsr[:, t:t + 1], None, ALU.mult).then_inc(xr_ready, 1)
                in_sbuf(dve, "R")
                link(V.tensor_scalar(krow, srow, LOG_N_K, None, ALU.min))
                V.reduce_max(nmax, krow, AX_X, negate=True).then_inc(lse_max, 1)
                o = got(dve, ("xT1", 1))
                V.tensor_scalar(xlT[:, 1, :], o, col("lgam", 1), None, ALU.mult)
                taken(V.tensor_scalar(xhT[:, 1, :], o, col("hgam", 1), None, ALU.mult), ("xT1", 1))

                def focus(w, i):
                    for j in range(2):
                        o = two(got(dve, (w, j)))
                        dve.wait_ge(abs_ready, 2 * i + j + 1)
                        for t in (2 * j, 2 * j + 1):
                            ins = V.scalar_tensor_tensor(fb[:, t, :], o[:, t % 2, :], 1.0, fa[:, t, :], ALU.mult, ALU.max,
                                                         accum_out=fsum[:, t:t + 1])
                            if t % 2:
                                taken(ins, (w, j))
                            yield
                        in_sbuf(dve, (w, j))
                    link(V.tensor_scalar(fsum, fsum, -1.0 / D, -1e-6, ALU.mult, ALU.add))
                    yield
                    yield
                    dve.wait_ge(log_ready, i + 1)
                    link(V.tensor_scalar(fa, fa, col("focus"), None, ALU.mult))
                    yield
                    V.reduce_max(fmax, fa, AX_X, negate=True).then_inc(focus_in, 1)
                    yield
                    yield
                    yield
                    dve.wait_ge(focus_exp, NT * (i + 1))
                    link(V.reciprocal(fco, psumm))
                    link(V.tensor_tensor(fco, fco, fsum, ALU.mult))
                    yield
                    for t in range(NT):
                        ins = V.tensor_scalar(yin[:, t, :, 0:DK], fb[:, t, :].rearrange("p (h n) -> p h n", h=NH),
                                              fco[:, t:t + 1], None, ALU.mult)
                        yield
                    link(ins)
                    for t in range(NT):
                        for h in range(NH):
                            ins = V.max(top8[:, t, h, :], yin[:, t, h, 0:DK])
                            if h % 4 == 3 and (t, h) != (NT - 1, NH - 1):
                                yield
                    link(ins)
                    link(V.memset(top8[:, :, :, 5:8], 1.0))
                    yield
                    for t in range(NT):
                        for h in range(NH):
                            ins = V.match_replace(yout[:, t, h, :], top8[:, t, h, :], yin[:, t, h, :], 0.0)
                            if h % 4 == 3 and (t, h) != (NT - 1, NH - 1):
                                yield
                    link(ins)
                    V.tensor_copy(ym[i].rearrange("p t (h n) -> p t h n", h=NH),
                                  yout[:, :, :, 0:DK]).then_inc(sparse_ready, 1)

                dve.wait_ge(lse_max, 1)
                dve.wait_ge(ln_ready, 1)
                link(V.scalar_tensor_tensor(lsh[:, 0:1], lnv, -SHIFT, nmax, ALU.add, ALU.subtract))
                dve.wait_ge(ones_ready, 2)
                keys = focus("k4", 0)
                for r in range(ROUNDS):
                    V.tensor_scalar(ce, scol, lsh[:, r % 2:r % 2 + 1], 60.0, ALU.subtract, ALU.min).then_inc(ce_ready, 1)
                    dve.wait_ge(ev_ready, r + 1)
                    for i in range(ITERS):
                        n = r * ITERS + i
                        if i == 0:
                            level = EXP_SHIFT
                        else:
                            dve.wait_ge(total_ready, n)
                            level = psb("chain")[:, n - 1:n]
                        V.tensor_scalar(jc, ev, level, 0.0, ALU.min, ALU.add,
                                        accum_out=rs[:, n % 2:n % 2 + 1]).then_inc(rowsum_ready, 1)
                        for _ in range((i >= 8, 1, 1, 2)[r]):
                            next(keys, None)
                        if r == ROUNDS - 1 and i == 0:
                            dve.wait_ge(x_biased, 2)
                        if r == ROUNDS - 1 and i < 2:
                            x_plus("yl", i)
                        dve.wait_ge(rowsum_ready, n + 1)
                    if r == ROUNDS - 1:
                        in_sbuf(dve, "chain")
                    else:
                        dve.wait_ge(ln_ready, r + 2)
                    link(V.scalar_tensor_tensor(lsh[:, (r + 1) % 2:(r + 1) % 2 + 1], lnv, -(SHIFT + 10.0),
                                                lsh[:, r % 2:r % 2 + 1], ALU.add, ALU.add))
                link(V.tensor_scalar(lfin, lsh[:, 0:1], SHIFT, None, ALU.add))
                link(V.tensor_scalar(krow, srow, lfin, 0.0, ALU.subtract, ALU.min))
                link(V.tensor_scalar(krow, krow, -103.97, None, ALU.max))
                link(V.tensor_scalar(kcol, scol, lfin, 0.0, ALU.subtract, ALU.min))
                V.tensor_scalar(kcol, kcol, -103.97, None, ALU.max).then_inc(kcol_ready, 1)
                dve.wait_ge(kcol_ready, 1)
                dve.wait_ge(setup_done, 2)
                for i in range(2):
                    got(dve, ("yh", i))
                for t in range(NT):
                    w = (NT - 1 - t) * P
                    V.scalar_tensor_tensor(hH[:, 2 * t, :], krow, kcol[:, t:t + 1], KB("lt")[:, w:w + S], ALU.is_ge,
                                           ALU.mult, accum_out=rk1[:, t:t + 1]).then_inc(rank_ready, 1)
                    V.scalar_tensor_tensor(hH[:, 2 * t + 1, :], krow, kcol[:, t:t + 1], KB("ge")[:, w:w + S], ALU.is_gt,
                                           ALU.mult, accum_out=rk2[:, t:t + 1]).then_inc(rank_ready, 1)
                dve.wait_ge(rank_ready, 2 * NT)
                link(V.tensor_tensor(rk1, rk1, rk2, ALU.add))
                link(V.tensor_scalar(rk1, rk1, float(TOP_HEAVY), None, ALU.is_lt))
                dve.wait_ge(score_ready, 1)
                link(V.tensor_scalar(wgt, score, -1.0, 1.0, ALU.mult, ALU.add))
                link(V.tensor_tensor(wgt, wgt, score, ALU.add))
                link(V.tensor_tensor(wgt, wgt, rk1, ALU.mult))
                in_sbuf(dve, ("yl", 0))
                in_sbuf(dve, ("yl", 1))
                for i in range(2):
                    o = two(got(dve, ("yh", i)))
                    for t in (2 * i, 2 * i + 1):
                        ins = V.scalar_tensor_tensor(x[:, t, :], o[:, t % 2, :], wgt[:, t:t + 1], x[:, t, :],
                                                     ALU.mult, ALU.add)
                    taken(ins, ("yh", i))
                in_sbuf(dve, ("yh", 0))
                in_sbuf(dve, ("yh", 1))

                norm(2, x, xn)
                copy(("xT2", 1), xnT[:, 1, :])
                for t in range(NT):
                    o = got(dve, ("S1", t))
                    V.reduce_max(nm4[:, t:t + 1], o[:, 0:KEYW], AX_X, negate=True).then_inc(max1_ready, 1)
                for t in range(NT):
                    o = got(dve, ("PT1", t))
                    V.tensor_copy(PT1[:, t, 0:P], o[:, 0:P])
                    taken(V.tensor_copy(PT1[0:64, t, P:2 * P], o[0:64, P:2 * P]), ("PT1", t))

                def weighted(key_of, scalar, dst=x):
                    for i in range(2):
                        o = two(got(dve, key_of(i)))
                        for t in (2 * i, 2 * i + 1):
                            ins = V.scalar_tensor_tensor(dst[:, t, :], o[:, t % 2, :], scalar(t), dst[:, t, :],
                                                         ALU.mult, ALU.add)
                        taken(ins, key_of(i))
                    in_sbuf(dve, key_of(1))

                link(V.reciprocal(rden4, den4))
                weighted(lambda i: ("O1", i), lambda t: rden4[:, t:t + 1])
                in_sbuf(dve, ("O1", 0))

                norm(3, x, xn)
                copy(("xT3", 1), xnT[:, 1, :])
                in_sbuf(dve, ("xT3", 1))
                link(V.tensor_scalar(conv, xnT[:, 1, :], col("convw", 7), None, ALU.mult))
                for k in range(1, 4):
                    ins = V.scalar_tensor_tensor(conv, xnT_[:, 1, 4 - k:4 - k + S], col("convw", 7 - k), conv,
                                                 ALU.mult, ALU.add)
                    if k < 3:
                        link(ins)
                ins.then_inc(conv_ready, 1)
                in_sbuf(dve, "RT3")

                def top2():
                    for t in range(NT):
                        ins = V.max(t8[:, t, :], tb[:, t, 0:8])
                    link(ins)
                    link(V.memset(t8[:, :, 2:8], BIG))
                    for t in range(NT):
                        ins = V.match_replace(tr[:, t, 0:14], t8[:, t, :], tb[:, t, 0:14], -BIG)
                    link(ins)
                    link(V.tensor_scalar(tr[:, :, 0:8], tr[:, :, 0:8], -2.9e38, None, ALU.is_le))
                    link(V.tensor_tensor(cw[:, :, 0:8], tr[:, :, 0:8], sc, ALU.mult))

                link(V.tensor_tensor(tb[:, :, 0:8], sc, row("rbias", NT), ALU.add))
                top2()
                link(V.reduce_sum(c46, cw[:, :, 0:8], AX_X))
                link(V.tensor_scalar(c46, c46, 1e-9, None, ALU.add))
                link(V.reciprocal(c46, c46))
                V.tensor_tensor(cw[:, :, 0:8], cw[:, :, 0:8], c46.unsqueeze(2).broadcast_to([P, NT, 8]), ALU.mult).then_inc(cw_ready, 1)
                dve.wait_ge(cw_ready, 1)
                def gated(gkey, ukey, sg, dst):
                    in_sbuf(dve, gkey)
                    o = got(dve, ukey)
                    next(keys, None)
                    taken(V.tensor_tensor(dst, sg, o, ALU.mult), ukey)

                dve.wait_ge(x_biased, 3)
                link(V.tensor_tensor(c46, cw[:, :, 4], cw[:, :, 6], ALU.add))
                for t in range(NT):
                    n_step[0] += 1
                    V.scalar_tensor_tensor(x[:, t, :], xn[:, t, :], c46[:, t:t + 1], x[:, t, :],
                                           ALU.mult, ALU.add).then_inc(dve_step, 1)
                dve.wait_ge(dve_step, n_step[0])
                dve.wait_ge(extra_ready, NT)
                link(V.tensor_tensor(x[:, :, :], x[:, :, :], extra, ALU.add))
                for e in range(4):
                    gated(("G3", e), ("U3", e), sg3[:, e % 2, :], hid3[:, e % 2, :])
                    if e == 0:
                        for i in range(2):
                            o = got(dve, ("CT3", i))
                            taken(V.tensor_tensor(flat(x[:, 2 * i:2 * i + 2, :]), flat(x[:, 2 * i:2 * i + 2, :]), o,
                                                  ALU.add), ("CT3", i))
                            in_sbuf(dve, ("CT3", i))
                    else:
                        weighted(lambda i: ("Y3", e - 1, i), lambda t: cw[:, t, e - 1:e])
                    for _ in range(5):
                        next(keys, None)
                for _ in keys:
                    pass
                weighted(lambda i: ("Y3", 3, i), lambda t: cw[:, t, 3:4])
                in_sbuf(dve, ("Y3", 3, 0))

                norm(4, x, xn)
                copy(("xT4", 1), xnT[:, 1, :])
                for _ in focus("q4", 1):
                    pass
                dve.wait_ge(sparse_ready, 2)
                for c in range(2):
                    o = got(dve, ("KV4", c))
                    bm = K("bmask")
                    V.scalar_tensor_tensor(kvm[:, c, 0:P], o[:, 0:P], 1.0 / S, bm[:, 0:P], ALU.mult, ALU.mult)
                    taken(V.tensor_scalar(kvm[:, c, P:136], bm[:, P:136], o[:, P:P + 1], 1.0 / S, ALU.mult, ALU.mult),
                          ("KV4", c))
                for t in range(NT):
                    o = got(dve, ("y4", t))[:, 0:272].rearrange("p (c n) -> p c n", c=2)
                    link(V.tensor_scalar(zr, o[:, :, P:136], 1e-6, None, ALU.add))
                    link(V.reciprocal(zr, zr))
                    taken(V.tensor_tensor(y4[:, t, :].rearrange("p (c h n) -> p c h n", c=2, h=8),
                                          o[:, :, 0:P].rearrange("p c (h n) -> p c h n", h=8),
                                          zr.unsqueeze(3).broadcast_to([P, 2, 8, DK]), ALU.mult), ("y4", t))
                    in_sbuf(dve, ("y4", t))
                add_to_x("O4")

                norm(5, x, xn)
                copy(("xT5", 1), xnT[:, 1, :])
                o = got(dve, "RT5")[:, 0:32].rearrange("p (t e) -> p t e", t=NT)
                link(V.reduce_max(c46, o, AX_X, negate=True))
                taken(V.tensor_tensor(sc, o, c46.unsqueeze(2).broadcast_to([P, NT, 8]), ALU.add), "RT5")
                in_sbuf(dve, "RT5")
                dve.wait_ge(router_exp, 1)
                link(V.reduce_sum(c46, sc, AX_X))
                link(V.reciprocal(c46, c46))
                link(V.tensor_tensor(sc, sc, c46.unsqueeze(2).broadcast_to([P, NT, 8]), ALU.mult))
                link(V.tensor_copy(tb[:, :, 0:8], sc))
                top2()
                for e in range(10):
                    for f in range(2):
                        gated(("G5", e, f), ("U5", e, f), sg5[:, f, :], hid5[:, e % 2, f, :])
                    if e:
                        weighted(lambda i: ("Y5", e - 1, i), lambda t: cw[:, t, e - 1:e])
                weighted(lambda i: ("Y5", 9, i), lambda t: cw[:, t, 9:10])
                in_sbuf(dve, ("Y5", 9, 0))

                norm(6, x, xn)
                copy(("xT6", 1), xnT[:, 1, :])

                def normalise_pair(a, i):
                    link(V.reciprocal(rden4[:, 2 * i:2 * i + 2], den4[:, 2 * i:2 * i + 2]))
                    o = two(got(dve, ("O6", a, i)))
                    for tt in (2 * i, 2 * i + 1):
                        if a == 0:
                            ins = V.tensor_scalar(att[:, tt, :], o[:, tt % 2, :], rden4[:, tt:tt + 1], None, ALU.mult)
                        else:
                            ins = V.scalar_tensor_tensor(n2[:, tt, :], o[:, tt % 2, :], rden4[:, tt:tt + 1],
                                                         n1[:, tt, :], ALU.mult, ALU.add)
                    taken(ins, ("O6", a, i))
                    in_sbuf(dve, ("O6", a, i))

                for a in range(2):
                    for t in range(NT):
                        n = (t + 1) * P if a == 0 else S
                        o = got(dve, ("S6", a, t))
                        V.reduce_max(nm4[:, t:t + 1], o[:, 0:n], AX_X, negate=True).then_inc(max6_ready, 1)
                    for t in range(NT):
                        nb = t + 1 if a == 0 else NT
                        o = got(dve, ("P6", a, t))
                        if t == 2:
                            got(dve, ("O6", a, 0))
                        if t == 3:
                            normalise_pair(a, 0)
                        taken(V.tensor_copy(PT6[:, t % 2, 0:nb * P], o[:, 0:nb * P]), ("P6", a, t))
                    normalise_pair(a, 1)
                    if a == 0:
                        link(V.tensor_tensor(n1, att, xn[:, :, :], ALU.add))
                        norm("6a", n1, n1, affine=True)
                    else:
                        norm("6b", n2, n2, affine=True)
                for m in range(2):
                    in_sbuf(dve, ("h6", m))
                    V.scalar_tensor_tensor(h6[:, m, :], v6[:, m, :], 0.2, v6[:, m, :], ALU.mult, ALU.max).then_inc(h6_ready, 1)
                for i in range(2):
                    o = two(got(dve, ("f6", i)))
                    taken(V.tensor_tensor(n1[:, 2 * i:2 * i + 2, :], o, n2[:, 2 * i:2 * i + 2, :], ALU.add), ("f6", i))
                in_sbuf(dve, ("f6", 0))
                in_sbuf(dve, ("f6", 1))
                norm("6c", n1, n1, affine=True)
                link(V.scalar_tensor_tensor(x[:, :, :], n1, 0.0, x[:, :, :], ALU.max, ALU.add))

                norm(7, x, xn)
                copy(("xT7", 1), xnT[:, 1, :])
                for m in range(6):
                    gated(("G7", m), ("U7", m), sg7[:, m % 2, :], hid7[:, m, :])
                add_to_x("Y7")
                meet(dve, b)


LOG_N_K = 0.5753641449035618
SHIFT = 20.0
EXP_SHIFT = 485165195.4097903


def _constants(np):
    c = {}
    inv = (1.0 / 10000.0 ** (np.arange(0, DK, 2, dtype=np.float32) / np.float32(DK))).astype(np.float32)
    f = np.arange(S, dtype=np.float32)[:, None] * inv[None, :]
    emb = np.concatenate([f, f], 1)
    cos, sin = np.cos(emb).astype(np.float32), np.sin(emb).astype(np.float32)
    rope = np.zeros((P, S), np.float32)
    for j in range(HG):
        rope[32 * j:32 * j + 16] = cos.T
        rope[32 * j + 16:32 * j + 24] = -sin.T[0:8]
        rope[32 * j + 24:32 * j + 32] = sin.T[8:16]
    c["rope"] = rope * np.float32(0.5)
    r = np.arange(P)
    c["fold"] = ((r[:, None] // 32 == r[None] // 32) & (r[:, None] % 16 == r[None] % 16)).astype(np.float32)
    c["ident"] = np.eye(P, dtype=np.float32)
    bm = np.zeros((P, 136), np.float32)
    bm[:, :P] = r[:, None] // DK == r[None] // DK
    bm[:, P:] = r[:, None] // DK == np.arange(8)[None]
    c["bmask"] = bm
    i = np.arange(S)[:, None]
    j = np.arange(S)[None]
    blocked = (np.abs(i - j) > 128) | (j > i)
    blocked &= ~((i < 16) | (j < 16))
    m = np.where(blocked, -1e30, 0.0)
    none = np.full((P, 32), -1e30)
    g = [np.concatenate([m[qt * P:(qt + 1) * P, 0:16], none[:, 0:16]], 1) for qt in range(NT)]
    parts = [m[0:128], m[128:256, 0:128], none, m[128:256, 128:256],
             g[2], m[256:384, 128:384], m[384:512, 256:512], g[3]]
    c["mask0"] = np.concatenate(parts, 1)
    band = []
    for t in range(NT):
        q = t * P + r[:, None]
        k = t * P - 32 + np.arange(KEYW)[None]
        band.append(np.where((np.abs(q - k) <= 20) & (k >= 0) & (k < S), 0.0, -1e8))
    c["band"] = np.concatenate(band, 1)
    c["causal"] = np.where(r[None] > r[:, None], -1e30, 0.0)
    c["identb"] = np.eye(P)
    lt = (np.arange(896)[None] - 384 < r[:, None])
    c["lt"], c["ge"] = lt * 1.0, 1.0 - lt
    a = np.concatenate([c[n] for n, _ in CONST], 1).astype(np.float32)
    z = np.concatenate([c[n] for n, _ in CONSTB], 1).astype(np.float32)
    return a, z


def _layout(np, i):
    def rows_of(w):
        return w.reshape(-1, P, w.shape[1]).transpose(1, 0, 2).reshape(P, -1)

    def padded_heads(w):
        h = w.reshape((NH, DK) + w.shape[1:])
        partner = np.concatenate([h[:, 1::2], h[:, ::2]], 1)
        return np.concatenate([h, partner], 1).reshape((NH * 32,) + w.shape[1:])

    def zero_rows(w):
        h = w.reshape(NH, DK, D)
        return np.concatenate([h, np.zeros_like(h)], 1).reshape(NH * 32, D)

    def reversed_heads(w):
        return w.reshape(NH, DK, D)[:, ::-1].reshape(D, D)

    w = {"wq": rows_of(padded_heads(i["L0_xattn_wq"]).T), "wk": rows_of(padded_heads(i["L0_xattn_wk"]).T),
         "wv": rows_of(i["L0_xattn_wv"].T), "wo": rows_of(zero_rows(i["L0_xattn_wo"].T)),
         "lw1": rows_of(i["L0_ffn_light_w1"]), "lw2": rows_of(i["L0_ffn_light_w2"]),
         "wred": rows_of(i["L1_xattn_W_reduce"].T), "l1r": rows_of(i["L1_ffn_Wr"]),
         "l1g": np.concatenate([rows_of(e) for e in i["L1_ffn_Wg"]], 1),
         "l1u": np.concatenate([rows_of(e) for e in i["L1_ffn_Wu"]], 1),
         "l1d": np.concatenate([rows_of(e) for e in i["L1_ffn_Wd"]], 1),
         "w2q": rows_of(reversed_heads(i["L2_xattn_Wq"]).T), "w2k": rows_of(reversed_heads(i["L2_xattn_Wk"]).T),
         "w2v": rows_of(i["L2_xattn_Wv"].T), "w2p": rows_of(i["L2_xattn_Wp"].T), "l2r": rows_of(i["L2_ffn_router_w"]),
         "k1": rows_of(i["L3_xattn_Wk1"]), "q1": rows_of(i["L3_xattn_Wq1"]), "v1": rows_of(i["L3_xattn_Wv1"]),
         "k2": rows_of(i["L3_xattn_Wk2"]), "q2": rows_of(i["L3_xattn_Wq2"]), "v2": rows_of(i["L3_xattn_Wv2"]),
         "f1": rows_of(i["L3_xattn_W1"]), "f2": rows_of(i["L3_xattn_W2"])}
    heavy1, heavy2 = i["L0_ffn_heavy_w1"], i["L0_ffn_heavy_w2"]
    chunks = [np.concatenate([rows_of(heavy1[:, c * 512:(c + 1) * 512]), rows_of(heavy2[c * 512:(c + 1) * 512])], 1)
              for c in range(2)]

    def expert(g, u, d):
        z = np.zeros((P, CHUNK - 1536), g.dtype)
        return np.concatenate([rows_of(g), rows_of(u), rows_of(d), z], 1)

    chunks += [expert(i["L2_ffn_gate_w"][e], i["L2_ffn_up_w"][e], i["L2_ffn_down_w"][e]) for e in range(8)]
    chunks += [expert(i["L2_ffn_shared_gate_w"][:, f], i["L2_ffn_shared_up_w"][:, f], i["L2_ffn_shared_down_w"][f])
               for f in (slice(0, 256), slice(256, 512))]
    c = {"bq": padded_heads(i["L0_xattn_bq"]).reshape(4, P).T, "bk": padded_heads(i["L0_xattn_bk"]).reshape(4, P).T,
         "lgam": i["L0_ffn_light_gamma"].reshape(2, P).T, "hgam": i["L0_ffn_heavy_gamma"].reshape(2, P).T,
         "lb1": i["L0_ffn_light_b1"].reshape(1, P).T, "hb1": i["L0_ffn_heavy_b1"].reshape(8, P).T,
         "bred": i["L1_xattn_b_reduce"].reshape(2, P).T,
         "convw": i["L1_ffn_conv_w"].reshape(4, 2, P).transpose(2, 1, 0).reshape(P, 8),
         "b1": i["L3_xattn_b1"].reshape(2, P).T,
         "focus": np.broadcast_to(np.reshape(i["L2_xattn_focusing_factor"], (1, 1)), (P, 1))}
    r = {"bv": i["L0_xattn_bv"], "bo": i["L0_xattn_bo"], "lb2": i["L0_ffn_light_b2"], "hb2": i["L0_ffn_heavy_b2"],
         "convb": i["L1_ffn_conv_b"], "b2": i["L3_xattn_b2"], "gamma": i["L3_xattn_gamma"],
         "beta": i["L3_xattn_beta"], "rt": i["L0_ffn_routing_token"], "rbias": i["L1_ffn_router_bias"]}
    const, constb = _constants(np)
    def again(a):
        return np.concatenate([a, a[:1]])

    ctx = again(i["ctx_1024"])
    shifted = np.zeros((NB + 1, 5 * P, D), ctx.dtype)
    shifted[:, 32:32 + S] = ctx
    return {
        "x": again(i["x"]).reshape(-1, NT, P, D).transpose(0, 2, 1, 3).reshape(-1, NT * D),
        "ctxT": ctx.reshape(-1, S, 2, P).transpose(0, 3, 2, 1).reshape(-1, 2 * S),
        "ctxs": shifted.reshape(-1, 5, P, D).transpose(0, 2, 1, 3).reshape(-1, 5 * D),
        "weights": np.concatenate([w[n] for n, _ in WEIGHTS], 1),
        "stream": np.concatenate(chunks, 0),
        "wint": np.concatenate([rows_of(i["L3_ffn_w_gate"].T), rows_of(i["L3_ffn_w_up"].T),
                                rows_of(i["L3_ffn_w_down"].T)], 1),
        "cols": np.concatenate([c[n] for n, _ in COLS], 1),
        "rows": np.broadcast_to(np.concatenate([r[n] for n, _ in ROWS])[None], (P, sum(n for _, n in ROWS))),
        "const": const, "constb": constb}


def kernel(**inputs):
    import numpy as _np
    import concourse.bacc as _bacc
    from concourse import mybir as _mybir
    from concourse.bass_utils import run_bass_kernel_spmd as _run

    nc = _bacc.Bacc("TRN2", target_bir_lowering=False, num_devices=1)
    arrays, args = {}, []
    for name, a in _layout(_np, {k: _np.asarray(v) for k, v in inputs.items()}).items():
        a = _np.ascontiguousarray(a)
        arrays[f"in_{name}"] = a
        args.append(nc.dram_tensor(f"in_{name}", a.shape, _mybir.dt.from_np(a.dtype), kind="ExternalInput").ap())
    args.append(nc.dram_tensor("out_x", (NB * P, NT * D), _mybir.dt.float32, kind="ExternalOutput").ap())
    network(nc, *args)
    r = _run(nc, [arrays], core_ids=[0]).results[0]["out_x"]
    return r.reshape(NB, P, NT, D).transpose(0, 2, 1, 3).reshape(NB, S, D)
```
